# Optimizing a Trainium2 kernel written in Bass

```python
import numpy as np
import jax
import jax.numpy as jnp

def _softmax(x, axis=-1):
    return jax.nn.softmax(x, axis=axis)

def _gelu(x):
    return jax.nn.gelu(x, approximate=True)

def _silu(x):
    return jax.nn.silu(x)

def _sigmoid(x):
    return jax.nn.sigmoid(x)

def _layernorm(x, axis=-1, eps=1e-05):
    m = jnp.mean(x, axis=axis, keepdims=True)
    v = jnp.var(x, axis=axis, keepdims=True)
    return (x - m) / jnp.sqrt(v + eps)

def _scatter_add(tgt, idx, src, axis=0):
    return tgt.at[idx].add(src)

def _segment_sum(src, seg, n):
    return jax.ops.segment_sum(src, seg, n)
kernel_name = 'mk_gps_d2_gnn_r32_7036a3'

def setup_inputs(seed: int=0):
    np.random.seed(seed)
    _w = jnp.asarray

    def _rec_inputs():
        import jax
        import jax.numpy as jnp
        _gk = jax.random.key(seed)
        x = -0.0003713 + 1 * jax.random.normal(jax.random.fold_in(_gk, 1), (3125, 256), jnp.float32)
        _s = jax.random.randint(jax.random.fold_in(_gk, 2), (25000,), 0, 3125, jnp.int32)
        _d = jax.random.randint(jax.random.fold_in(_gk, 3), (25000,), 0, 3125, jnp.int32)
        _loop = jnp.arange(3125, dtype=jnp.int32)
        src = jnp.concatenate([_s, _d, _loop])
        dst = jnp.concatenate([_d, _s, _loop])
        _o = jnp.argsort(dst, stable=True)
        src = src[_o]
        dst = dst[_o]
        edge_type_6 = jax.random.randint(jax.random.fold_in(_gk, 13), (53125,), 0, 6, jnp.int32)
        edge_weight = jax.random.uniform(jax.random.fold_in(_gk, 14), (53125,), jnp.float32, 0.0, 0.999998)
        return (x, src, dst, edge_type_6, edge_weight)
    x, src, dst, edge_type_6, edge_weight = _rec_inputs()

    def _L0_gnn_setup():
        import jax, jax.numpy as jnp
        import numpy as np
        N_NODES = 50000
        N_EDGES = 25000
        F_IN = 256
        F_OUT = 256
        key = jax.random.key(seed)
        k_x, k_w, k_r, k_c, k_v = jax.random.split(key, 5)
        limit = np.sqrt(6.0 / (F_IN + F_OUT)).astype(np.float32)
        x = jax.random.normal(k_x, (N_NODES, F_IN), dtype=jnp.float32)
        weight = jax.random.uniform(k_w, (F_IN, F_OUT), dtype=jnp.float32, minval=-limit, maxval=limit)
        bias = jnp.zeros((F_OUT,), dtype=jnp.float32)
        rows = jax.random.randint(k_r, (N_EDGES,), 0, N_NODES, dtype=jnp.int64 if jax.config.jax_enable_x64 else jnp.int32)
        cols = jax.random.randint(k_c, (N_EDGES,), 0, N_NODES, dtype=jnp.int64 if jax.config.jax_enable_x64 else jnp.int32)
        vals = jax.random.uniform(k_v, (N_EDGES,), dtype=jnp.float32)
        return {'x': x, 'weight': weight, 'bias': bias, 'rows': rows, 'cols': cols, 'vals': vals}
    _L0_gnn_all = _L0_gnn_setup()
    _L0_gnn_in = {k: v for k, v in _L0_gnn_all.items() if k in ('weight', 'bias')}
    del _L0_gnn_all

    def _L0_mix_setup():
        import jax, jax.numpy as jnp
        import numpy as np
        NUM_HEADS = 8
        key = jax.random.key(seed)
        ks = jax.random.split(key, 5)
        B, N, C = (8, 512, 256)
        x = jax.random.normal(ks[0], (B, N, C), dtype=jnp.float32)
        Wq = jax.random.normal(ks[1], (C, C), dtype=jnp.float32) * 0.02
        Wkv = jax.random.normal(ks[2], (2 * C, C), dtype=jnp.float32) * 0.02
        Wproj = jax.random.normal(ks[3], (C, C), dtype=jnp.float32) * 0.02
        bproj = jnp.zeros((C,), dtype=jnp.float32)
        return {'x': x, 'Wq': Wq, 'Wkv': Wkv, 'Wproj': Wproj, 'bproj': bproj}
    _L0_mix_all = _L0_mix_setup()
    _L0_mix_in = {k: v for k, v in _L0_mix_all.items() if k in ('Wq', 'Wkv', 'Wproj', 'bproj')}
    del _L0_mix_all

    def _L0_ffn_setup():
        import jax, jax.numpy as jnp
        import numpy as np
        B, N, D = (16, 128, 256)
        NUM_EXPERTS, TOP_K, HEADS = (4, 2, 4)
        N_EDGES = 32768
        LN_EPS = 1e-05

        def _layernorm(x, g, b):
            mu = x.mean(-1, keepdims=True)
            var = ((x - mu) ** 2).mean(-1, keepdims=True)
            return (x - mu) * jax.lax.rsqrt(var + LN_EPS) * g + b

        def _forward(x, edge_index, W_gat, att_src, att_dst, b_gat, ln_gamma, ln_beta, W1, b1, W2, b2):
            Bc, Nc, Dc = x.shape
            M = Bc * Nc
            x_flat = x.reshape(M, Dc)
            h = (x_flat @ W_gat).reshape(M, HEADS, NUM_EXPERTS)
            loops = jnp.arange(M, dtype=edge_index.dtype)
            src = jnp.concatenate([edge_index[0], loops])
            dst = jnp.concatenate([edge_index[1], loops])
            a_src = (h * att_src).sum(-1)
            a_dst = (h * att_dst).sum(-1)
            e = jax.nn.leaky_relu(a_src[src] + a_dst[dst], negative_slope=0.2)
            e_max = jax.ops.segment_max(e, dst, num_segments=M)
            ee = jnp.exp(e - e_max[dst])
            denom = jax.ops.segment_sum(ee, dst, num_segments=M)
            alpha = ee / (denom[dst] + 1e-16)
            msg = h[src] * alpha[:, :, None]
            agg = jax.ops.segment_sum(msg, dst, num_segments=M).reshape(M, HEADS * NUM_EXPERTS) + b_gat
            scores = _layernorm(agg, ln_gamma, ln_beta).reshape(M, HEADS, NUM_EXPERTS).mean(1)
            scores = scores.reshape(Bc, Nc, NUM_EXPERTS)
            topk_s, topk_i = jax.lax.top_k(scores, TOP_K)
            w = jax.nn.softmax(topk_s, axis=-1)
            out = jnp.zeros_like(x)
            for ei in range(NUM_EXPERTS):
                g = jnp.where(topk_i == ei, w, 0.0).sum(-1)
                hh = jax.nn.gelu(x @ W1[ei] + b1[ei], approximate=False)
                out = out + g[..., None] * (hh @ W2[ei] + b2[ei])
            return out
        key = jax.random.key(seed)
        ks = jax.random.split(key, 8)
        s = 0.05
        return {'x': jax.random.normal(ks[0], (B, N, D), jnp.float32), 'W_gat': jax.random.normal(ks[1], (D, HEADS * NUM_EXPERTS), jnp.float32) * s, 'att_src': jax.random.normal(ks[2], (HEADS, NUM_EXPERTS), jnp.float32) * s, 'att_dst': jax.random.normal(ks[3], (HEADS, NUM_EXPERTS), jnp.float32) * s, 'b_gat': jnp.zeros((HEADS * NUM_EXPERTS,), jnp.float32), 'ln_gamma': jnp.ones((HEADS * NUM_EXPERTS,), jnp.float32), 'ln_beta': jnp.zeros((HEADS * NUM_EXPERTS,), jnp.float32), 'W1': jax.random.normal(ks[4], (NUM_EXPERTS, D, 2 * D), jnp.float32) * s, 'b1': jnp.zeros((NUM_EXPERTS, 2 * D), jnp.float32), 'W2': jax.random.normal(ks[5], (NUM_EXPERTS, 2 * D, D), jnp.float32) * s, 'b2': jnp.zeros((NUM_EXPERTS, D), jnp.float32), 'edge_index': jax.random.randint(ks[6], (2, N_EDGES), 0, B * N, jnp.int32)}
    _L0_ffn_all = _L0_ffn_setup()
    _L0_ffn_in = {k: v for k, v in _L0_ffn_all.items() if k in ('W_gat', 'att_src', 'att_dst', 'b_gat', 'ln_gamma', 'ln_beta', 'W1', 'b1', 'W2', 'b2', 'edge_index')}
    del _L0_ffn_all

    def _L1_gnn_setup():
        import jax, jax.numpy as jnp
        import numpy as np
        N_NODES = 50000
        N_EDGES = 12500
        D_IN = 256
        D_OUT = 256
        N_REL = 6
        N_HEADS = 4
        key = jax.random.key(seed)
        ks = jax.random.split(key, 12)
        s_in = 1.0 / np.sqrt(D_IN)
        s_out = 1.0 / np.sqrt(D_OUT)
        return {'x': jax.random.normal(ks[0], (N_NODES, D_IN), dtype=jnp.float32), 'edge_index': jax.random.randint(ks[1], (2, N_EDGES), 0, N_NODES, dtype=jnp.int64), 'edge_types': jax.random.randint(ks[2], (N_EDGES,), 0, N_REL, dtype=jnp.int64), 'W': jax.random.uniform(ks[3], (N_REL, D_IN, D_OUT), jnp.float32, -s_in, s_in), 'b': jax.random.uniform(ks[4], (N_REL, D_OUT), jnp.float32, -s_in, s_in), 'in_proj_w': jax.random.uniform(ks[5], (3 * D_OUT, D_OUT), jnp.float32, -s_out, s_out), 'in_proj_b': jnp.zeros((3 * D_OUT,), jnp.float32), 'attn_out_w': jax.random.uniform(ks[6], (D_OUT, D_OUT), jnp.float32, -s_out, s_out), 'attn_out_b': jnp.zeros((D_OUT,), jnp.float32), 'proj_w': jax.random.uniform(ks[7], (D_OUT, D_OUT), jnp.float32, -s_out, s_out), 'proj_b': jax.random.uniform(ks[8], (D_OUT,), jnp.float32, -s_out, s_out)}
    _L1_gnn_all = _L1_gnn_setup()
    _L1_gnn_in = {k: v for k, v in _L1_gnn_all.items() if k in ('W', 'b', 'in_proj_w', 'in_proj_b', 'attn_out_w', 'attn_out_b', 'proj_w', 'proj_b')}
    del _L1_gnn_all

    def _L1_mix_setup():
        import jax, jax.numpy as jnp
        import numpy as np
        NHEAD = 8
        ATT_EPS = 1e-06
        LN_EPS = 1e-05

        def _layernorm(x, g, b):
            mu = jnp.mean(x, axis=-1, keepdims=True)
            var = jnp.mean(jnp.square(x - mu), axis=-1, keepdims=True)
            return (x - mu) * jax.lax.rsqrt(var + LN_EPS) * g + b
        key = jax.random.key(seed)
        ks = jax.random.split(key, 7)
        N, L, C = (4, 512, 256)
        s = 1.0 / np.sqrt(C)
        return {'x': jax.random.normal(ks[0], (N, L, C), jnp.float32), 'Wq': jax.random.normal(ks[1], (C, C), jnp.float32) * s, 'Wk': jax.random.normal(ks[2], (C, C), jnp.float32) * s, 'Wv': jax.random.normal(ks[3], (C, C), jnp.float32) * s, 'Wm': jax.random.normal(ks[4], (C, C), jnp.float32) * s, 'W1': jax.random.normal(ks[5], (2 * C, 2 * C), jnp.float32) * (1.0 / np.sqrt(2 * C)), 'W2': jax.random.normal(ks[6], (2 * C, C), jnp.float32) * (1.0 / np.sqrt(2 * C)), 'g1': jnp.ones((C,), jnp.float32), 'b1': jnp.zeros((C,), jnp.float32), 'g2': jnp.ones((C,), jnp.float32), 'b2': jnp.zeros((C,), jnp.float32)}
    _L1_mix_all = _L1_mix_setup()
    _L1_mix_in = {k: v for k, v in _L1_mix_all.items() if k in ('Wq', 'Wk', 'Wv', 'Wm', 'W1', 'W2', 'g1', 'b1', 'g2', 'b2')}
    del _L1_mix_all

    def _L1_ffn_setup():
        import jax, jax.numpy as jnp
        import numpy as np
        C = 256
        HID = 1024
        E = 8
        TEMP = 1.0
        key = jax.random.key(seed)
        ks = jax.random.split(key, 7)
        x = jax.random.normal(ks[0], (8, 512, C), dtype=jnp.float32)
        W1 = jax.random.normal(ks[1], (C, HID), dtype=jnp.float32) * 0.02
        b1 = jnp.zeros((HID,), dtype=jnp.float32)
        Wg = jax.random.normal(ks[2], (HID, E), dtype=jnp.float32) * 0.02
        bg = jnp.zeros((E,), dtype=jnp.float32)
        Wd = jax.random.normal(ks[3], (E, HID, C), dtype=jnp.float32) * 0.02
        bd = jnp.zeros((E, C), dtype=jnp.float32)
        return {'x': x, 'W1': W1, 'b1': b1, 'Wg': Wg, 'bg': bg, 'Wd': Wd, 'bd': bd}
    _L1_ffn_all = _L1_ffn_setup()
    _L1_ffn_in = {k: v for k, v in _L1_ffn_all.items() if k in ('W1', 'b1', 'Wg', 'bg', 'Wd', 'bd')}
    del _L1_ffn_all
    return {'x': x, 'src': src, 'dst': dst, 'edge_type_6': edge_type_6, 'edge_weight': edge_weight, 'L0_gnn_weight': _L0_gnn_in['weight'], 'L0_gnn_bias': _L0_gnn_in['bias'], 'L0_mix_Wq': _L0_mix_in['Wq'], 'L0_mix_Wkv': _L0_mix_in['Wkv'], 'L0_mix_Wproj': _L0_mix_in['Wproj'], 'L0_mix_bproj': _L0_mix_in['bproj'], 'L0_ffn_W_gat': _L0_ffn_in['W_gat'], 'L0_ffn_att_src': _L0_ffn_in['att_src'], 'L0_ffn_att_dst': _L0_ffn_in['att_dst'], 'L0_ffn_b_gat': _L0_ffn_in['b_gat'], 'L0_ffn_ln_gamma': _L0_ffn_in['ln_gamma'], 'L0_ffn_ln_beta': _L0_ffn_in['ln_beta'], 'L0_ffn_W1': _L0_ffn_in['W1'], 'L0_ffn_b1': _L0_ffn_in['b1'], 'L0_ffn_W2': _L0_ffn_in['W2'], 'L0_ffn_b2': _L0_ffn_in['b2'], 'L0_ffn_edge_index': _L0_ffn_in['edge_index'], 'L1_gnn_W': _L1_gnn_in['W'], 'L1_gnn_b': _L1_gnn_in['b'], 'L1_gnn_in_proj_w': _L1_gnn_in['in_proj_w'], 'L1_gnn_in_proj_b': _L1_gnn_in['in_proj_b'], 'L1_gnn_attn_out_w': _L1_gnn_in['attn_out_w'], 'L1_gnn_attn_out_b': _L1_gnn_in['attn_out_b'], 'L1_gnn_proj_w': _L1_gnn_in['proj_w'], 'L1_gnn_proj_b': _L1_gnn_in['proj_b'], 'L1_mix_Wq': _L1_mix_in['Wq'], 'L1_mix_Wk': _L1_mix_in['Wk'], 'L1_mix_Wv': _L1_mix_in['Wv'], 'L1_mix_Wm': _L1_mix_in['Wm'], 'L1_mix_W1': _L1_mix_in['W1'], 'L1_mix_W2': _L1_mix_in['W2'], 'L1_mix_g1': _L1_mix_in['g1'], 'L1_mix_b1': _L1_mix_in['b1'], 'L1_mix_g2': _L1_mix_in['g2'], 'L1_mix_b2': _L1_mix_in['b2'], 'L1_ffn_W1': _L1_ffn_in['W1'], 'L1_ffn_b1': _L1_ffn_in['b1'], 'L1_ffn_Wg': _L1_ffn_in['Wg'], 'L1_ffn_bg': _L1_ffn_in['bg'], 'L1_ffn_Wd': _L1_ffn_in['Wd'], 'L1_ffn_bd': _L1_ffn_in['bd']}

def reference(x, src, dst, edge_type_6, edge_weight, L0_gnn_weight, L0_gnn_bias, L0_mix_Wq, L0_mix_Wkv, L0_mix_Wproj, L0_mix_bproj, L0_ffn_W_gat, L0_ffn_att_src, L0_ffn_att_dst, L0_ffn_b_gat, L0_ffn_ln_gamma, L0_ffn_ln_beta, L0_ffn_W1, L0_ffn_b1, L0_ffn_W2, L0_ffn_b2, L0_ffn_edge_index, L1_gnn_W, L1_gnn_b, L1_gnn_in_proj_w, L1_gnn_in_proj_b, L1_gnn_attn_out_w, L1_gnn_attn_out_b, L1_gnn_proj_w, L1_gnn_proj_b, L1_mix_Wq, L1_mix_Wk, L1_mix_Wv, L1_mix_Wm, L1_mix_W1, L1_mix_W2, L1_mix_g1, L1_mix_b1, L1_mix_g2, L1_mix_b2, L1_ffn_W1, L1_ffn_b1, L1_ffn_Wg, L1_ffn_bg, L1_ffn_Wd, L1_ffn_bd):
    import jax
    import jax.numpy as jnp

    def _L0_gnn_ref(x, weight, bias, rows, cols, vals):
        import jax, jax.numpy as jnp
        import numpy as np
        N_NODES = 50000
        N_EDGES = 25000
        F_IN = 256
        F_OUT = 256
        support = jnp.matmul(x, weight)
        msgs = vals[:, None] * support[cols]
        out = jax.ops.segment_sum(msgs, rows, num_segments=x.shape[0])
        return out + bias

    def _L0_mix_ref(x, Wq, Wkv, Wproj, bproj):
        import jax, jax.numpy as jnp
        import numpy as np
        NUM_HEADS = 8
        B, N, C = x.shape
        h = NUM_HEADS
        d = C // h
        q = jnp.einsum('bnc,oc->bno', x, Wq).reshape(B, N, h, d).transpose(0, 2, 1, 3)
        kv = jnp.einsum('bnc,oc->bno', x, Wkv).reshape(B, N, 2, h, d)
        k = kv[:, :, 0].transpose(0, 2, 1, 3)
        v = kv[:, :, 1].transpose(0, 2, 1, 3)
        q = jax.nn.elu(q) + 1.0
        k = jax.nn.elu(k) + 1.0
        k_sum = k.sum(axis=2)
        D_inv = 1.0 / jnp.maximum(jnp.einsum('bhnd,bhd->bhn', q, k_sum), 1e-06)
        context = jnp.einsum('bhnd,bhne->bhde', k, v)
        attn = jnp.einsum('bhnd,bhde->bhne', q, context) * D_inv[..., None]
        out = attn.transpose(0, 2, 1, 3).reshape(B, N, C)
        out = jnp.einsum('bnc,oc->bno', out, Wproj) + bproj
        return out

    def _L0_ffn_ref(x, W_gat, att_src, att_dst, b_gat, ln_gamma, ln_beta, W1, b1, W2, b2, edge_index):
        import jax, jax.numpy as jnp
        import numpy as np
        B, N, D = (16, 128, 256)
        NUM_EXPERTS, TOP_K, HEADS = (4, 2, 4)
        N_EDGES = 32768
        LN_EPS = 1e-05

        def _layernorm(x, g, b):
            mu = x.mean(-1, keepdims=True)
            var = ((x - mu) ** 2).mean(-1, keepdims=True)
            return (x - mu) * jax.lax.rsqrt(var + LN_EPS) * g + b

        def _forward(x, edge_index, W_gat, att_src, att_dst, b_gat, ln_gamma, ln_beta, W1, b1, W2, b2):
            Bc, Nc, Dc = x.shape
            M = Bc * Nc
            x_flat = x.reshape(M, Dc)
            h = (x_flat @ W_gat).reshape(M, HEADS, NUM_EXPERTS)
            loops = jnp.arange(M, dtype=edge_index.dtype)
            src = jnp.concatenate([edge_index[0], loops])
            dst = jnp.concatenate([edge_index[1], loops])
            a_src = (h * att_src).sum(-1)
            a_dst = (h * att_dst).sum(-1)
            e = jax.nn.leaky_relu(a_src[src] + a_dst[dst], negative_slope=0.2)
            e_max = jax.ops.segment_max(e, dst, num_segments=M)
            ee = jnp.exp(e - e_max[dst])
            denom = jax.ops.segment_sum(ee, dst, num_segments=M)
            alpha = ee / (denom[dst] + 1e-16)
            msg = h[src] * alpha[:, :, None]
            agg = jax.ops.segment_sum(msg, dst, num_segments=M).reshape(M, HEADS * NUM_EXPERTS) + b_gat
            scores = _layernorm(agg, ln_gamma, ln_beta).reshape(M, HEADS, NUM_EXPERTS).mean(1)
            scores = scores.reshape(Bc, Nc, NUM_EXPERTS)
            topk_s, topk_i = jax.lax.top_k(scores, TOP_K)
            w = jax.nn.softmax(topk_s, axis=-1)
            out = jnp.zeros_like(x)
            for ei in range(NUM_EXPERTS):
                g = jnp.where(topk_i == ei, w, 0.0).sum(-1)
                hh = jax.nn.gelu(x @ W1[ei] + b1[ei], approximate=False)
                out = out + g[..., None] * (hh @ W2[ei] + b2[ei])
            return out
        return _forward(x, edge_index, W_gat, att_src, att_dst, b_gat, ln_gamma, ln_beta, W1, b1, W2, b2)

    def _L1_gnn_ref(x, edge_index, edge_types, W, b, in_proj_w, in_proj_b, attn_out_w, attn_out_b, proj_w, proj_b):
        import jax, jax.numpy as jnp
        import numpy as np
        N_NODES = 50000
        N_EDGES = 12500
        D_IN = 256
        D_OUT = 256
        N_REL = 6
        N_HEADS = 4
        num_nodes = x.shape[0]
        hd = D_OUT // N_HEADS
        transformed = jnp.einsum('ni,rio->rno', x, W) + b[:, None, :]
        src, dst = (edge_index[0], edge_index[1])
        msgs = transformed[edge_types, src]
        agg = jnp.zeros((N_REL, num_nodes, D_OUT), x.dtype).at[edge_types, dst].add(msgs)
        s = jnp.transpose(agg, (1, 0, 2))
        qkv = s @ in_proj_w.T + in_proj_b
        q, k, v = jnp.split(qkv, 3, axis=-1)
        q = q.reshape(num_nodes, N_REL, N_HEADS, hd)
        k = k.reshape(num_nodes, N_REL, N_HEADS, hd)
        v = v.reshape(num_nodes, N_REL, N_HEADS, hd)
        scores = jnp.einsum('nrhd,nshd->nhrs', q, k) / np.sqrt(hd)
        probs = jax.nn.softmax(scores, axis=-1)
        attn = jnp.einsum('nhrs,nshd->nrhd', probs, v).reshape(num_nodes, N_REL, D_OUT)
        attended = attn @ attn_out_w.T + attn_out_b
        aggregated_output = attended.mean(axis=1)
        out = (aggregated_output + x[:, :D_OUT]) @ proj_w.T + proj_b
        return out

    def _L1_mix_ref(x, Wq, Wk, Wv, Wm, W1, W2, g1, b1, g2, b2):
        import jax, jax.numpy as jnp
        import numpy as np
        NHEAD = 8
        ATT_EPS = 1e-06
        LN_EPS = 1e-05

        def _layernorm(x, g, b):
            mu = jnp.mean(x, axis=-1, keepdims=True)
            var = jnp.mean(jnp.square(x - mu), axis=-1, keepdims=True)
            return (x - mu) * jax.lax.rsqrt(var + LN_EPS) * g + b
        N, L, C = x.shape
        H = NHEAD
        D = C // H
        q = (x @ Wq).reshape(N, L, H, D)
        k = (x @ Wk).reshape(N, L, H, D)
        v = (x @ Wv).reshape(N, L, H, D)
        Q = jax.nn.elu(q) + 1.0
        K = jax.nn.elu(k) + 1.0
        v = v / L
        KV = jnp.einsum('nshd,nshv->nhdv', K, v)
        Z = 1.0 / (jnp.einsum('nlhd,nhd->nlh', Q, K.sum(axis=1)) + ATT_EPS)
        msg = jnp.einsum('nlhd,nhdv,nlh->nlhv', Q, KV, Z) * L
        msg = msg.reshape(N, L, C) @ Wm
        msg = _layernorm(msg, g1, b1)
        h = jnp.concatenate([x, msg], axis=-1) @ W1
        h = jax.nn.relu(h) @ W2
        msg = _layernorm(h, g2, b2)
        return x + msg

    def _L1_ffn_ref(x, W1, b1, Wg, bg, Wd, bd):
        import jax, jax.numpy as jnp
        import numpy as np
        C = 256
        HID = 1024
        E = 8
        TEMP = 1.0
        orig_shape = x.shape
        xf = x.reshape(-1, orig_shape[-1])
        H = jax.nn.gelu(xf @ W1 + b1, approximate=False)
        probs = jax.nn.softmax((H @ Wg + bg) / TEMP, axis=-1)
        assign = jnp.argmax(probs, axis=-1)
        out = jnp.zeros_like(xf)
        for e in range(Wd.shape[0]):
            y = H @ Wd[e] + bd[e]
            sel = (assign == e)[:, None]
            out = out + jnp.where(sel, probs[:, e:e + 1] * y, 0.0)
        return out.reshape(orig_shape)
    edge_index = jnp.stack([src, dst])
    xn = _layernorm(x, axis=-1)
    x = x + _L0_gnn_ref(xn, L0_gnn_weight, L0_gnn_bias, src, dst, edge_weight) + _L0_mix_ref(xn[None], L0_mix_Wq, L0_mix_Wkv, L0_mix_Wproj, L0_mix_bproj)[0]
    x = x + _L0_ffn_ref(_layernorm(x, axis=-1)[None], L0_ffn_W_gat, L0_ffn_att_src, L0_ffn_att_dst, L0_ffn_b_gat, L0_ffn_ln_gamma, L0_ffn_ln_beta, L0_ffn_W1, L0_ffn_b1, L0_ffn_W2, L0_ffn_b2, L0_ffn_edge_index)[0]
    xn = _layernorm(x, axis=-1)
    x = x + _L1_gnn_ref(xn, edge_index, edge_type_6, L1_gnn_W, L1_gnn_b, L1_gnn_in_proj_w, L1_gnn_in_proj_b, L1_gnn_attn_out_w, L1_gnn_attn_out_b, L1_gnn_proj_w, L1_gnn_proj_b) + _L1_mix_ref(xn[None], L1_mix_Wq, L1_mix_Wk, L1_mix_Wv, L1_mix_Wm, L1_mix_W1, L1_mix_W2, L1_mix_g1, L1_mix_b1, L1_mix_g2, L1_mix_b2)[0]
    x = x + _L1_ffn_ref(_layernorm(x, axis=-1)[None], L1_ffn_W1, L1_ffn_b1, L1_ffn_Wg, L1_ffn_bg, L1_ffn_Wd, L1_ffn_bd)[0]
    return x

_drawn_inputs = setup_inputs


def setup_inputs(seed=0):
    import zlib

    import numpy as np

    out = dict(_drawn_inputs(seed))
    spreads = {'L0_gnn_bias': (0.0, 0.1),
     'L0_mix_bproj': (0.0, 0.1),
     'L0_ffn_b_gat': (0.0, 0.1),
     'L0_ffn_ln_gamma': (1.0, 0.2),
     'L0_ffn_ln_beta': (0.0, 0.1),
     'L0_ffn_b1': (0.0, 0.1),
     'L0_ffn_b2': (0.0, 0.1),
     'L1_gnn_in_proj_b': (0.0, 0.8),
     'L1_gnn_attn_out_b': (0.0, 0.527),
     'L1_mix_g1': (1.0, 0.2),
     'L1_mix_b1': (0.0, 0.365),
     'L1_mix_g2': (1.0, 0.2),
     'L1_mix_b2': (0.0, 0.305),
     'L1_ffn_b1': (0.0, 0.8),
     'L1_ffn_bg': (0.0, 0.8),
     'L1_ffn_bd': (0.0, 0.8)}
    factors = {'L0_mix_Wq': 8.0,
     'L0_mix_Wkv': 8.0,
     'L0_mix_Wproj': 8.0,
     'L0_ffn_att_src': 3.365,
     'L0_ffn_att_dst': 4.71,
     'L1_gnn_b': 8.0,
     'L1_gnn_proj_b': 6.115,
     'L1_mix_Wq': 3.972,
     'L1_ffn_W1': 8.0,
     'L1_ffn_Wg': 8.0,
     'L1_ffn_Wd': 8.0}
    for name, (base, spread) in spreads.items():
        noise = np.random.default_rng([zlib.crc32(name.encode()), seed]).standard_normal(out[name].shape)
        drawn = base * np.exp(spread * noise) if base else spread * noise
        out[name] = jnp.asarray(drawn.astype(out[name].dtype))
    for name, factor in factors.items():
        out[name] = (out[name] * factor).astype(out[name].dtype)
    return out
```

```python
import concourse.bass as bass
from concourse import mybir
from contextlib import ExitStack

F32 = mybir.dt.float32
I32 = mybir.dt.int32
ALU = mybir.AluOpType
ACT = mybir.ActivationFunctionType
AX = mybir.AxisListType

N = 3125
D = 256
P = 125
NT = N // P
KC = D // 128
E_GRAPH = 53125
E_GAT = 32768
N_REL = 6
N_EXP0 = 4
HID0 = 512
N_EXP1 = 8
HID1 = 1024
ROUND = 12582912.0
FAR = -3.0e38
EPS = 1e-5


class Chain:

    def __init__(self, eng, sem, base=0):
        self.eng, self.sem, self.base, self.n = eng, sem, base, 0

    def __call__(self, ins):
        self.n += 1
        ins.then_inc(self.sem, 1)
        self.eng.wait_ge(self.sem, self.base + self.n)


class Phase:

    def __init__(self, nc, ctx, name):
        self.nc, self.ctx, self.name, self.sems = nc, ctx, name, []
        ctx.callback(self.give_back)

    def sb(self, name, shape, dt=F32):
        return self.ctx.enter_context(self.nc.sbuf_tensor(f"{self.name}_{name}", shape, dt))

    def ps(self, name, shape, dt=F32):
        return self.ctx.enter_context(self.nc.psum_tensor(f"{self.name}_{name}", shape, dt))

    def sem(self, name):
        self.sems.append(self.nc.alloc_semaphore(f"{self.name}_{name}"))
        return self.sems[-1]

    def give_back(self):
        if self.sems:
            self.nc.clear_and_free_semaphores(self.sems)
            self.nc.all_engine_barrier()


def rows(ap):
    return ap.rearrange("(t p) f -> p t f", p=P)


def make_constants(nc, cn):
    with ExitStack() as ctx:
        ph = Phase(nc, ctx, "cst")
        ramp_i = ph.sb("ramp_i", [128, 640], I32)
        part_i = ph.sb("part_i", [128, 1], I32)
        filled, made = ph.sem("filled"), ph.sem("made")
        with nc.Block() as block:
            @block.gpsimd
            def _(pool):
                nc.gpsimd.memset(cn["ident"][:, :], 0.0).then_inc(filled, 1)
                nc.gpsimd.memset(cn["ones"][:, :], 1.0).then_inc(filled, 1)
                nc.gpsimd.memset(cn["tri"][:, :], 1.0).then_inc(filled, 1)
                nc.gpsimd.memset(cn["blocks"][:, :], 0.0).then_inc(filled, 1)
                nc.gpsimd.memset(cn["zeros"][:, :], 0.0).then_inc(filled, 1)
                nc.gpsimd.memset(cn["one_row"][:, :], 1.0).then_inc(filled, 1)
                nc.gpsimd.iota(ramp_i[:, :], [[1, 640]], base=0, channel_multiplier=0).then_inc(made, 1)
                nc.gpsimd.iota(part_i[:, :], [[1, 1]], base=0, channel_multiplier=1).then_inc(made, 1)
                pool.wait_ge(filled, 6)
                nc.gpsimd.affine_select(out=cn["ident"][:, :], in_=cn["ident"][:, :], compare_op=ALU.not_equal,
                                        fill=1.0, base=0, pattern=[[-1, 128]], channel_multiplier=1).then_inc(made, 1)
                nc.gpsimd.affine_select(out=cn["tri"][:, :], in_=cn["tri"][:, :], compare_op=ALU.is_gt,
                                        fill=0.0, base=0, pattern=[[1, 128]], channel_multiplier=-1).then_inc(made, 1)

            @block.vector
            def _(dve):
                dve.wait_ge(made, 4)
                nc.vector.tensor_copy(cn["ramp"][:, :], ramp_i[:, :])
                nc.vector.tensor_copy(cn["part"][:, :], part_i[:, :])
                for h in range(4):
                    nc.vector.memset(cn["blocks"][32 * h:32 * h + 32, 32 * h:32 * h + 32], 1.0)


def layer_norm_stats(nc, ph, rstd, mean, x, tiles=NT):
    st = ph.sb("st", [P, tiles, 6])
    mv = ph.sb("mv", [P, tiles, 2])
    ve = ph.sb("ve", [P, tiles])
    sd = ph.sb("sd", [P, tiles])
    steps, var_ready, root_ready = ph.sem("ln_steps"), ph.sem("var_ready"), ph.sem("root_ready")
    with nc.Block() as block:
        @block.vector
        def _(dve):
            chain = Chain(dve, steps)
            with dve.Fori(0, tiles) as t:
                nc.vector.bn_stats(st[:, bass.ds(t, 1), :].rearrange("p a f -> p (a f)"),
                                   x[:, bass.ds(t, 1), :].rearrange("p a f -> p (a f)")).then_inc(steps, 1)
            chain.n = tiles
            dve.wait_ge(steps, tiles)
            for t in range(tiles):
                last = nc.vector.bn_aggr(mv[:, t, :], st[:, t, :])
                if t < tiles - 1:
                    last.then_inc(steps, 1)
                    chain.n += 1
            chain(last)
            chain(nc.vector.tensor_copy(mean[:, :], mv[:, :, 0]))
            nc.vector.tensor_scalar(ve[:, :], mv[:, :, 1], EPS, None, ALU.add).then_inc(var_ready, 1)
            dve.wait_ge(root_ready, 1)
            nc.vector.reciprocal(rstd[:, :], sd[:, :])

        @block.scalar
        def _(act):
            act.wait_ge(var_ready, 1)
            nc.scalar.activation(sd[:, :], ve[:, :], ACT.Sqrt).then_inc(root_ready, 1)


def sort_edges(nc, ph, cn, parts, cols, step, nb, tiles, table, tab, tb, key_d, other_d, type_d=None, weight_d=None):
    shape = [parts, cols]
    key_i, other_i, addr_i = ph.sb("key_i", shape, I32), ph.sb("other_i", shape, I32), ph.sb("addr_i", shape, I32)
    key, bk, loc, pos = ph.sb("key", shape), ph.sb("bk", shape), ph.sb("loc", shape), ph.sb("pos", shape)
    hit, run, one = ph.sb("hit", shape), ph.sb("run", shape), ph.sb("one", shape)
    rec = ph.sb("rec", [parts, cols, 4], I32)
    cnt, pre, tot = ph.sb("cnt", [parts, nb]), ph.sb("pre", [parts, nb]), ph.sb("tot", [128, nb])
    lots, upto, start = ph.sb("lots", [128, nb]), ph.sb("upto", [128, nb]), ph.sb("start", [128, nb])
    tbf = ph.sb("tbf", [1, tiles])
    empty = tab
    ridx, rrec = ph.sb("ridx", [parts, step], I32), ph.sb("rrec", [parts, step, 4], I32)
    ps_tot, ps_pre = ph.ps("ps_tot", [128, nb]), ph.ps("ps_pre", [128, nb])
    loaded, steps, counted, summed = ph.sem("loaded"), ph.sem("steps"), ph.sem("counted"), ph.sem("summed")
    empty_ready, cleared, recs_ready = ph.sem("empty_ready"), ph.sem("cleared"), ph.sem("recs_ready")
    copied, scattered, gate, reloaded = ph.sem("copied"), ph.sem("scattered"), ph.sem("gate"), ph.sem("reloaded")
    n_loads = 2 + (type_d is not None) + (weight_d is not None)
    type_i = ph.sb("type_i", shape, I32) if type_d is not None else None
    recf = rec[:, :, :].bitcast(F32)

    def cut(d):
        return d.rearrange("(p c) -> p c", p=parts)

    with nc.Block() as block:
        @block.sync
        def _(sp):
            sp.dma_start(key_i[:, :], cut(key_d)).then_inc(loaded, 16)
            sp.dma_start(other_i[:, :], cut(other_d)).then_inc(loaded, 16)
            if type_d is not None:
                sp.dma_start(type_i[:, :], cut(type_d)).then_inc(loaded, 16)
            if weight_d is not None:
                sp.dma_start(one[:, :], cut(weight_d)).then_inc(loaded, 16)
            sp.wait_ge(empty_ready, 1)
            sp.dma_start(table.rearrange("(p t) f -> p t f", p=128), empty[:, :, :]).then_inc(cleared, 16)

        @block.vector
        def _(dve):
            chain = Chain(dve, steps)
            chain(nc.vector.memset(empty[:, :, :], 0))
            nc.vector.memset(empty[:, :, 1].bitcast(F32), -1.0).then_inc(empty_ready, 1)
            chain(nc.vector.memset(rec[:, :, :], 0))
            chain(nc.vector.memset(pos[:, :], 0.0))
            chain(nc.vector.memset(tbf[:, :], 0.0))
            dve.wait_ge(loaded, 16 * n_loads)
            chain(nc.vector.tensor_copy(rec[:, :, 0], other_i[:, :]))
            if weight_d is not None:
                chain(nc.vector.tensor_copy(recf[:, :, 2], one[:, :]))
            chain(nc.vector.memset(one[:, :], 1.0))
            chain(nc.vector.tensor_copy(key[:, :], key_i[:, :]))
            chain(nc.vector.tensor_scalar(bk[:, :], key[:, :], -float(P // 2), 1.0 / P, ALU.add, ALU.mult))
            chain(nc.vector.tensor_scalar(bk[:, :], bk[:, :], ROUND, None, ALU.add))
            chain(nc.vector.tensor_scalar(bk[:, :], bk[:, :], -ROUND, None, ALU.add))
            chain(nc.vector.scalar_tensor_tensor(loc[:, :], bk[:, :], -float(P), key[:, :], ALU.mult, ALU.add))
            chain(nc.vector.tensor_copy(recf[:, :, 1], loc[:, :]))
            if type_d is not None:
                chain(nc.vector.tensor_copy(hit[:, :], type_i[:, :]))
                chain(nc.vector.scalar_tensor_tensor(key[:, :], bk[:, :], float(N_REL), hit[:, :], ALU.mult, ALU.add))
                chain(nc.vector.tensor_copy(run[:, :], other_i[:, :]))
                chain(nc.vector.scalar_tensor_tensor(run[:, :], hit[:, :], float(N), run[:, :], ALU.mult, ALU.add))
                chain(nc.vector.tensor_copy(rec[:, :, 0], run[:, :]))
            else:
                chain(nc.vector.tensor_copy(key[:, :], bk[:, :]))
            k0 = chain.n
            with dve.Fori(0, nb) as b:
                nc.vector.tensor_scalar(hit[:, :], key[:, :], cn["ramp"][0:parts, bass.ds(b, 1)], 0.0, ALU.is_equal,
                                        ALU.add, accum_out=cnt[:, bass.ds(b, 1)]).then_inc(steps, 1)
                dve.wait_ge(steps, b + (k0 + 1))
            chain.n = k0 + nb
            nc.vector.tensor_copy(pre[:, 0:1], cnt[:, 0:1]).then_inc(counted, 1)
            dve.wait_ge(summed, 1)
            chain(nc.vector.tensor_scalar(lots[:, :], ps_tot[:, :], 1.0 / 128, -127.0 / 256, ALU.mult, ALU.add))
            chain(nc.vector.tensor_scalar(lots[:, :], lots[:, :], ROUND, None, ALU.add))
            chain(nc.vector.tensor_scalar(lots[:, :], lots[:, :], -ROUND, 1.0, ALU.add, ALU.add))
            chain(nc.vector.tensor_tensor_scan(upto[:, :], cn["one_row"][:, 0:nb], lots[:, :], 0.0, ALU.mult, ALU.add))
            chain(nc.vector.tensor_tensor(start[:, :], upto[:, :], lots[:, :], ALU.subtract))
            chain(nc.vector.scalar_tensor_tensor(pre[:, :], start[0:parts, :], 128.0, ps_pre[0:parts, :],
                                                 ALU.mult, ALU.add))
            k0, per = chain.n, 5
            with dve.Fori(0, nb) as b:
                inner = Chain(dve, steps, b * per + k0)
                bs = bass.ds(b, 1)
                ramp_b = cn["ramp"][0:parts, bs]
                inner(nc.vector.tensor_scalar(hit[:, :], key[:, :], ramp_b, None, ALU.is_equal))
                inner(nc.vector.tensor_tensor_scan(run[:, :], one[:, :], hit[:, :], pre[:, bs], ALU.mult, ALU.add))
                inner(nc.vector.tensor_tensor(hit[:, :], hit[:, :], run[:, :], ALU.mult))
                inner(nc.vector.tensor_tensor(pos[:, :], pos[:, :], hit[:, :], ALU.add))
                inner(nc.vector.scalar_tensor_tensor(tbf[:, :], cn["ramp"][0:1, 0:tiles], start[0:1, bs], tbf[:, :],
                                                     ALU.is_ge, ALU.add))
            chain.n = k0 + per * nb
            chain(nc.vector.tensor_scalar(tb[:, :], tbf[:, :], -1.0, None, ALU.add))
            chain(nc.vector.tensor_scalar(pos[:, :], pos[:, :], -1.0, None, ALU.add))
            chain(nc.vector.tensor_scalar(bk[:, :], pos[:, :], 1.0 / 128, -127.0 / 256, ALU.mult, ALU.add))
            chain(nc.vector.tensor_scalar(bk[:, :], bk[:, :], ROUND, None, ALU.add))
            chain(nc.vector.tensor_scalar(bk[:, :], bk[:, :], -ROUND, None, ALU.add))
            chain(nc.vector.scalar_tensor_tensor(run[:, :], bk[:, :], -128.0, pos[:, :], ALU.mult, ALU.add))
            chain(nc.vector.scalar_tensor_tensor(run[:, :], run[:, :], float(tiles), bk[:, :], ALU.mult, ALU.add))
            nc.vector.tensor_copy(addr_i[:, :], run[:, :]).then_inc(recs_ready, 1)

        @block.tensor
        def _(pe):
            pe.wait_ge(counted, 1)
            nc.tensor.matmul(ps_tot[:, :], cn["ones"][0:parts, :], cnt[:, :], start=True, stop=True)
            nc.tensor.matmul(ps_pre[:, :], cn["tri"][0:parts, :], cnt[:, :], start=True, stop=True).then_inc(summed, 1)

        @block.gpsimd
        def _(pool):
            pool.wait_ge(recs_ready, 1)
            pool.wait_ge(cleared, 16)
            with pool.Fori(0, cols // step) as c:
                nc.gpsimd.tensor_copy(ridx[:, :], addr_i[:, bass.ds(c * step, step)]).then_inc(copied, 1)
                nc.gpsimd.tensor_copy(rrec[:, :, :], rec[:, bass.ds(c * step, step), :]).then_inc(copied, 1)
                pool.wait_ge(copied, c * 2 + 2)
                pool.sem_inc(gate, 1)
                for u in range(step):
                    nc.gpsimd.indirect_dma_start(table, bass.IndirectOffsetOnAxis(ap=ridx[:, u:u + 1], axis=0),
                                                 rrec[:, u, :], None).then_inc(scattered, 16)
                pool.wait_ge(scattered, c * (16 * step) + 16 * step)
                pool.sem_inc(gate, 1)
            pool.dma_start(tab[:, :, :], table.rearrange("(p t) f -> p t f", p=128)).then_inc(reloaded, 16)
            pool.wait_ge(reloaded, 16)


def aggregate(nc, ph, cn, tiles, tab, tb, source, acc, weighted, transposed):
    G = 4
    gath, hot = ph.sb("gath", [128, 2, G, D]), ph.sb("hot", [128, 2, G, P])
    idx = ph.sb("idx", [128, 2, G], I32)
    out_p = 128 if transposed else P
    prod = [[ph.ps(f"prod{g}{j}", [128, 512]) for j in range(G)] for g in range(2)]
    w = 2 * P if transposed else D
    gathered = [ph.sem(f"gathered{g}") for g in range(2)]
    hot_ready = [ph.sem(f"hot_ready{g}") for g in range(2)]
    used = [ph.sem(f"used{g}") for g in range(2)]
    added = [ph.sem(f"added{g}") for g in range(2)]
    idx_ready, gate, gate_v, steps = ph.sem("idx_ready"), ph.sem("agate"), ph.sem("gate_v"), ph.sem("asteps")
    tabf = tab[:, :, :].bitcast(F32)
    assert tiles % (2 * G) == 0
    rounds = tiles // (2 * G)

    with nc.Block() as block:
        @block.gpsimd
        def _(pool):
            with pool.Fori(0, rounds) as r:
                for g in range(2):
                    pool.wait_ge(used[g], r + 1)
                    pool.sem_inc(gate, 1)
                    nc.gpsimd.tensor_copy(idx[:, g, :], tab[:, bass.ds(r * (2 * G) + g * G, G), 0]).then_inc(idx_ready, 1)
                    pool.wait_ge(idx_ready, r * 2 + (g + 1))
                    pool.sem_inc(gate, 1)
                    for j in range(G):
                        nc.gpsimd.indirect_dma_start(gath[:, g, j, :], None, source,
                                                     bass.IndirectOffsetOnAxis(ap=idx[:, g, j:j + 1], axis=0)
                                                     ).then_inc(gathered[g], 16)

        @block.vector
        def _(dve):
            for g in range(2):
                dve.sem_inc(added[g], 1)
            with dve.Fori(0, rounds) as r:
                for g in range(2):
                    dve.wait_ge(used[g], r + 1)
                    for j in range(G):
                        t = bass.ds(r * (2 * G) + g * G + j, 1)
                        ins = nc.vector.tensor_scalar(
                            hot[:, g, j, :], cn["ramp"][:, 0:P], tabf[:, t, 1], tabf[:, t, 2] if weighted else 1.0,
                            ALU.is_equal, ALU.mult)
                    ins.then_inc(hot_ready[g], 1)
                for g in range(2):
                    chain = Chain(dve, steps, r * (2 * G) + g * G)
                    dve.wait_ge(used[g], r + 2)
                    for j in range(G):
                        b = dve.value_load(tb[0:1, bass.ds(r * (2 * G) + g * G + j, 1)], min_val=0,
                                           max_val=acc.shape[1] - 1)
                        a = acc[:, bass.ds(b, 1), :].rearrange("p a f -> p (a f)")
                        chain(nc.vector.tensor_tensor(a, a, prod[g][j][0:out_p, 0:w], ALU.add))
                    dve.sem_inc(added[g], 1)

        @block.tensor
        def _(pe):
            for g in range(2):
                pe.sem_inc(used[g], 1)
            with pe.Fori(0, rounds) as r:
                for g in range(2):
                    pe.wait_ge(gathered[g], r * (16 * G) + 16 * G)
                    pe.wait_ge(hot_ready[g], r + 1)
                    pe.wait_ge(added[g], r + 1)
                    for j in range(G):
                        if transposed:
                            for h in range(2):
                                ins = nc.tensor.matmul(prod[g][j][:, h * P:(h + 1) * P], gath[:, g, j, h * 128:(h + 1) * 128],
                                                       hot[:, g, j, :], start=True, stop=True)
                        else:
                            ins = nc.tensor.matmul(prod[g][j][0:P, 0:D], hot[:, g, j, :], gath[:, g, j, :], start=True, stop=True)
                    ins.then_inc(used[g], 1)


def project(nc, ph, cn, x, mean, rstd, xT, w_sb, width, evac, stores, kv=None, xn_d=None):
    xc, xTc = ph.sb("xc", [P, D]), ph.sb("xTc", [128, KC, P])
    nb = (width + 511) // 512
    pt, po = ph.ps("pt", [128, KC, P]), [ph.ps(f"po{i}", [P, 512]) for i in range(nb)]
    low, low_e = ph.sb("low", [P, D]), ph.sb("low_e", [P, D])
    normed, turned, xT_ready, xT_kept = ph.sem("normed"), ph.sem("turned"), ph.sem("xT_ready"), ph.sem("xT_kept")
    made, evacuated, stored = ph.sem("made"), ph.sem("evacuated"), ph.sem("stored")
    gate_p, gate_a, steps = ph.sem("gate_p"), ph.sem("gate_a"), ph.sem("psteps")
    lowered, exped, kv_used = ph.sem("lowered"), ph.sem("exped"), ph.sem("kv_used")
    n_st = len(stores) + (xn_d is not None)

    with nc.Block() as block:
        @block.vector
        def _(dve):
            with dve.Fori(0, NT) as t:
                dve.wait_ge(turned, t + 1)
                if n_st:
                    dve.wait_ge(stored, t * (16 * n_st) + 16)
                nc.vector.tensor_scalar(xc[:, :], x[:, bass.ds(t, 1), :].rearrange("p a f -> p (a f)"), mean[:, bass.ds(t, 1)],
                                        rstd[:, bass.ds(t, 1)], ALU.subtract, ALU.mult).then_inc(normed, 1)
                dve.wait_ge(made, t + 2)
                if kv is not None:
                    dve.wait_ge(kv_used, t + 1)
                for c, n, kind, to, bias in evac:
                    src = po[c // 512][:, c % 512:c % 512 + n]
                    if kind == "bias":
                        ins = nc.vector.tensor_tensor(to(t), src, bias, ALU.add)
                    elif kind == "copy":
                        ins = nc.vector.tensor_scalar(to(t), src, 1.0, None, ALU.mult)
                    else:
                        nc.vector.tensor_scalar(low[:, :], src, 0.0, None, ALU.min).then_inc(lowered, 1)
                        dve.wait_ge(exped, t + 1)
                        ins = nc.vector.scalar_tensor_tensor(to(t), src, 0.0, low_e[:, :], ALU.max, ALU.add)
                ins.then_inc(steps, 1)
                dve.wait_ge(steps, t + 1)
                dve.sem_inc(evacuated, 1)

        @block.scalar
        def _(act):
            act.sem_inc(xT_ready, 1)
            with act.Fori(0, NT) as t:
                act.wait_ge(turned, t + 2)
                act.wait_ge(xT_kept, t + 1)
                act.wait_ge(made, t + 1)
                nc.scalar.activation(xTc[:, :, :], pt[:, :, :], ACT.Copy).then_inc(xT_ready, 1)
                if kv is not None:
                    act.wait_ge(lowered, t + 1)
                    nc.scalar.activation(low_e[:, :], low[:, :], ACT.Exp).then_inc(exped, 1)

        @block.gpsimd
        def _(pool):
            pool.sem_inc(xT_kept, 1)
            with pool.Fori(0, NT) as t:
                pool.wait_ge(xT_ready, t + 2)
                pool.sem_inc(gate_p, 1)
                nc.gpsimd.tensor_copy(xT[:, :, bass.ds(t, 1), :].rearrange("p k a f -> p k (a f)"), xTc[:, :, :]).then_inc(xT_kept, 1)

        @block.sync
        def _(sp):
            if not n_st:
                return
            sp.sem_inc(stored, 16)
            with sp.Fori(0, NT) as t:
                if xn_d is not None:
                    sp.wait_ge(normed, t + 1)
                    sp.dma_start(xn_d[:, bass.ds(t, 1), :].rearrange("p a f -> p (a f)"), xc[:, :]).then_inc(stored, 16)
                if stores:
                    sp.wait_ge(evacuated, t + 2)
                    for to, buf in stores:
                        sp.dma_start(to[:, bass.ds(t, 1), :].rearrange("p a f -> p (a f)"), buf).then_inc(stored, 16)
            sp.wait_ge(stored, NT * 16 * n_st + 16)

        @block.tensor
        def _(pe):
            pe.sem_inc(turned, 1)
            pe.sem_inc(kv_used, 1)
            pe.sem_inc(made, 1)
            pe.sem_inc(evacuated, 1)
            if kv is not None:
                kvp, ksp, k_sb, v_sb = kv
                nc.tensor.matmul(kvp[:, :], cn["zeros"][:, 0:128], cn["zeros"][:, 0:258], start=True, stop=False)
            with pe.Fori(0, NT) as t:
                pe.wait_ge(normed, t + 1)
                pe.wait_ge(xT_ready, t + 1)
                for k in range(KC):
                    ins = nc.tensor.matmul(pt[:, k, :], xc[:, k * 128:(k + 1) * 128], cn["ident"][0:P, 0:P], start=True, stop=True)
                ins.then_inc(turned, 1)
                pe.wait_ge(xT_ready, t + 2)
                pe.wait_ge(evacuated, t + 1)
                for i in range(nb):
                    n = min(512, width - 512 * i)
                    for k in range(KC):
                        ins = nc.tensor.matmul(po[i][:, 0:n], xTc[:, k, :], w_sb[:, k, 512 * i:512 * i + n],
                                               start=(k == 0), stop=(k == KC - 1))
                ins.then_inc(made, 1)
                if kv is not None:
                    pe.wait_ge(evacuated, t + 2)
                    for h in range(2):
                        hs = slice(h * 128, (h + 1) * 128)
                        nc.tensor.matmul(kvp[:, hs], v_sb[:, hs], k_sb[:, hs], start=False, stop=False, skip_group_check=True)
                        ins = nc.tensor.matmul(kvp[:, 256 + h:257 + h], k_sb[:, hs], cn["ones"][0:P, 0:1],
                                               start=False, stop=False, skip_group_check=True)
                    ins.then_inc(kv_used, 1)
            if kv is not None:
                nc.tensor.matmul(kvp[:, :], cn["zeros"][:, 0:128], cn["zeros"][:, 0:258], start=False, stop=True)


def fold_context(nc, ph, cn, kvp, cb, kb, ks, wT, fold):
    pf = [ph.ps(f"pf{h}", [128, D]) for h in range(2)]
    ready, made, steps = ph.sem("fc_ready"), ph.sem("fc_made"), ph.sem("fc_steps")
    with nc.Block() as block:
        @block.vector
        def _(dve):
            chain = Chain(dve, steps)
            chain(nc.vector.tensor_copy(ks[:, :], kvp[:, 256:258]))
            for h in range(2):
                nc.vector.tensor_scalar(kb[:, h, :], cn["blocks"][:, :], ks[:, h:h + 1], None, ALU.mult)
                chain(nc.vector.tensor_tensor(cb[:, h, :], kvp[:, h * 128:(h + 1) * 128], cn["blocks"][:, :], ALU.mult))
            dve.sem_inc(ready, 1)
            dve.wait_ge(made, 1)
            for h in range(2):
                nc.vector.tensor_copy(fold[:, h, :], pf[h][:, :])

        @block.tensor
        def _(pe):
            pe.wait_ge(ready, 1)
            for h in range(2):
                ins = nc.tensor.matmul(pf[h][:, :], cb[:, h, :], wT[:, h, :], start=True, stop=True)
            ins.then_inc(made, 1)


def linear_attention(nc, ph, cn, xT, wq, kb, fold, guard, finish):
    pq, pd, po = ph.ps("pq", [128, 2, P]), ph.ps("pd", [128, 2, P]), ph.ps("po", [P, D])
    low, low_e, q1 = ph.sb("low", [128, 2, P]), ph.sb("low_e", [128, 2, P]), ph.sb("q1", [128, 2, P])
    r0, r1, qn = ph.sb("r0", [128, 2, P]), ph.sb("r1", [128, 2, P]), ph.sb("qn", [128, 2, P])
    q_made, lowered, exped, q_ready = ph.sem("q_made"), ph.sem("lowered"), ph.sem("exped"), ph.sem("q_ready")
    d_made, qn_ready, o_made, finished, steps = (ph.sem("d_made"), ph.sem("qn_ready"), ph.sem("o_made"), ph.sem("finished"),
                                                 ph.sem("la_steps"))
    with nc.Block() as block:
        @block.tensor
        def _(pe):
            pe.sem_inc(q_ready, 1)
            pe.sem_inc(finished, 1)
            with pe.Fori(0, NT) as t:
                pe.wait_ge(q_ready, t + 1)
                for h in range(2):
                    for k in range(KC):
                        ins = nc.tensor.matmul(pq[:, h, :], wq[:, k, h * 128:(h + 1) * 128],
                                               xT[:, k, bass.ds(t, 1), :].rearrange("p a f -> p (a f)"), start=(k == 0), stop=(k == KC - 1))
                ins.then_inc(q_made, 1)
                pe.wait_ge(q_ready, t + 2)
                for h in range(2):
                    ins = nc.tensor.matmul(pd[:, h, :], kb[:, h, :], q1[:, h, :], start=True, stop=True)
                ins.then_inc(d_made, 1)
                pe.wait_ge(qn_ready, t + 1)
                pe.wait_ge(finished, t + 1)
                for h in range(2):
                    ins = nc.tensor.matmul(po[:, :], qn[:, h, :], fold[:, h, :], start=(h == 0), stop=(h == 1))
                ins.then_inc(o_made, 1)

        @block.scalar
        def _(act):
            with act.Fori(0, NT) as t:
                act.wait_ge(lowered, t + 1)
                nc.scalar.activation(low_e[:, :, :], low[:, :, :], ACT.Exp).then_inc(exped, 1)

        @block.vector
        def _(dve):
            with dve.Fori(0, NT) as t:
                chain = Chain(dve, steps, t * 3)
                dve.wait_ge(q_made, t + 1)
                nc.vector.tensor_scalar(low[:, :, :], pq[:, :, :], 0.0, None, ALU.min).then_inc(lowered, 1)
                dve.wait_ge(exped, t + 1)
                chain(nc.vector.scalar_tensor_tensor(q1[:, :, :], pq[:, :, :], 0.0, low_e[:, :, :], ALU.max, ALU.add))
                dve.sem_inc(q_ready, 1)
                dve.wait_ge(d_made, t + 1)
                chain(nc.vector.tensor_scalar(r0[:, :, :], pd[:, :, :], guard[1], None, guard[0]))
                chain(nc.vector.reciprocal(r1[:, :, :], r0[:, :, :]))
                nc.vector.tensor_tensor(qn[:, :, :], q1[:, :, :], r1[:, :, :], ALU.mult).then_inc(qn_ready, 1)
                dve.wait_ge(o_made, t + 1)
                finish(t, po[:, :]).then_inc(finished, 1)


def load(nc, ph, pairs):
    loaded = ph.sem("weights_loaded")
    with nc.Block() as block:
        @block.sync
        def _(sp):
            for to, src in pairs:
                sp.dma_start(to, src).then_inc(loaded, 16)
            sp.wait_ge(loaded, 16 * len(pairs))


def chunks(w):
    return w.rearrange("(k p) m -> p k m", p=128)


def row(v, parts=P):
    return v.rearrange("(a f) -> a f", a=1).to_broadcast([parts, v.shape[0]])


def layer0(nc, cn, A, x, xT, support_d):
    with ExitStack() as ctx:
        ph = Phase(nc, ctx, "a1")
        w = ph.sb("w", [128, KC, 3 * D])
        wq, wp = ph.sb("wq", [128, KC, D]), ph.sb("wp", [128, KC, D])
        mean, rstd = ph.sb("mean", [P, NT]), ph.sb("rstd", [P, NT])
        sup, k_sb, v_sb = ph.sb("sup", [P, D]), ph.sb("k", [P, D]), ph.sb("v", [P, D])
        cb, kb, ks, fold = ph.sb("cb", [128, 2, 128]), ph.sb("kb", [128, 2, 128]), ph.sb("ks", [128, 2]), ph.sb("fold", [128, 2, D])
        b0, b1, bias = ph.sb("b0", [P, D]), ph.sb("b1", [P, D]), ph.sb("bias", [P, D])
        kvp = ph.ps("kvp", [128, 258])
        load(nc, ph, [(w[:, :, 0:2 * D], chunks(A["L0_mix_WkvT"])), (w[:, :, 2 * D:3 * D], chunks(A["L0_gnn_weight"])),
                      (wq[:, :, :], chunks(A["L0_mix_WqT"])), (wp[:, :, :], chunks(A["L0_mix_WprojT"])),
                      (b0[:, :], row(A["L0_gnn_bias"])), (b1[:, :], row(A["L0_mix_bproj"])),
                      (x[:, :, :], rows(A["x"]))])
        layer_norm_stats(nc, ph, rstd, mean, x)
        with ExitStack() as inner:
            p2 = Phase(nc, inner, "a2")
            project(nc, p2, cn, x, mean, rstd, xT, w, 3 * D,
                    [(0, D, "elu", lambda t: k_sb[:, :], None), (D, D, "copy", lambda t: v_sb[:, :], None),
                     (2 * D, D, "copy", lambda t: sup[:, :], None)],
                    [(rows(support_d), sup[:, :])], kv=(kvp, None, k_sb, v_sb))
        with ExitStack() as inner:
            p3 = Phase(nc, inner, "a3")
            fold_context(nc, p3, cn, kvp, cb, kb, ks, wp, fold)
        with ExitStack() as inner:
            p4 = Phase(nc, inner, "a4")
            gate = p4.sem("bias_ready")
            with nc.Block() as block:
                @block.vector
                def _(dve):
                    nc.vector.tensor_tensor(bias[:, :], b0[:, :], b1[:, :], ALU.add).then_inc(gate, 1)
                    dve.wait_ge(gate, 1)
                    for t in range(NT):
                        nc.vector.tensor_tensor(x[:, t, :], x[:, t, :], bias[:, :], ALU.add)

            def finish(t, psum):
                a = x[:, bass.ds(t, 1), :].rearrange("p a f -> p (a f)")
                return nc.vector.tensor_tensor(a, a, psum, ALU.add)
            linear_attention(nc, p4, cn, xT, wq, kb, fold, (ALU.max, 1e-6), finish)
    with ExitStack() as ctx:
        ph = Phase(nc, ctx, "as")
        tiles = 440
        tab, tb = ph.sb("tab", [128, tiles, 4], I32), ph.sb("tb", [1, tiles], I32)
        table = nc.dram_tensor("table_a", [128 * tiles, 4], I32, kind="Internal").ap()
        with ExitStack() as inner:
            p2 = Phase(nc, inner, "at")
            sort_edges(nc, p2, cn, P, E_GRAPH // P, 25, NT, tiles, table, tab, tb, A["src"], A["dst"],
                       weight_d=A["edge_weight"])
        with ExitStack() as inner:
            p3 = Phase(nc, inner, "ag")
            aggregate(nc, p3, cn, tiles, tab, tb, support_d, x, True, False)


def spread(ap, axis, shape):
    return ap.unsqueeze(axis).to_broadcast(shape)


def gat_max(nc, ph, cn, tiles, tab, tb, source, ge, top):
    G = 2
    gath, idx = ph.sb("gath", [128, 2, G, 20]), ph.sb("idx", [128, 2, G], I32)
    diag, cand, best = ph.sb("diag", [128, 2, G, 5, 128]), ph.sb("cand", [P, 4, 128]), ph.sb("best", [P, 4])
    pen = ph.sb("pen", [P, 128])
    wide = [[ph.ps(f"wide{g}{j}", [P, 1024]) for j in range(G)] for g in range(2)]
    gathered = [ph.sem(f"gathered{g}") for g in range(2)]
    read, made, added = ([ph.sem(f"read{g}") for g in range(2)], [ph.sem(f"made{g}") for g in range(2)],
                         [ph.sem(f"added{g}") for g in range(2)])
    idx_ready, gate, steps, diag_ready = ph.sem("idx_ready"), ph.sem("gate"), ph.sem("steps"), ph.sem("diag_ready")
    tabf = tab[:, :, :].bitcast(F32)
    assert tiles % (2 * G) == 0
    rounds = tiles // (2 * G)
    with nc.Block() as block:
        @block.gpsimd
        def _(pool):
            with pool.Fori(0, rounds) as r:
                for g in range(2):
                    pool.wait_ge(read[g], r + 1)
                    pool.sem_inc(gate, 1)
                    nc.gpsimd.tensor_copy(idx[:, g, :], tab[:, bass.ds(r * (2 * G) + g * G, G), 0]).then_inc(idx_ready, 1)
                    pool.wait_ge(idx_ready, r * 2 + (g + 1))
                    pool.sem_inc(gate, 1)
                    for j in range(G):
                        nc.gpsimd.indirect_dma_start(gath[:, g, j, :], None, source,
                                                     bass.IndirectOffsetOnAxis(ap=idx[:, g, j:j + 1], axis=0)
                                                     ).then_inc(gathered[g], 16)

        @block.vector
        def _(dve):
            for g in range(2):
                dve.sem_inc(read[g], 1)
                dve.sem_inc(added[g], 1)
            per = 2 * (2 + 4 * G)
            with dve.Fori(0, rounds) as r:
                chain = Chain(dve, steps, r * per)
                for g in range(2):
                    dve.wait_ge(gathered[g], r * (16 * G) + 16 * G)
                    t = bass.ds(r * (2 * G) + g * G, G)
                    chain(nc.vector.tensor_scalar(ge[:, t, 0:20], gath[:, g, :, :], 1.0, None, ALU.mult))
                    chain(nc.vector.tensor_scalar(ge[:, t, 20], tabf[:, t, 1], 1.0, None, ALU.mult))
                    for j in range(G):
                        tj = bass.ds(r * (2 * G) + g * G + j, 1)
                        vals = ge[:, tj, 16:21].rearrange("p a f -> p (a f)")
                        ins = nc.vector.tensor_tensor(diag[:, g, j, :, :], spread(cn["ident"][:, :], 1, [128, 5, 128]),
                                                      spread(vals, 2, [128, 5, 128]), ALU.mult)
                    ins.then_inc(diag_ready, 1)
                    dve.sem_inc(read[g], 1)
                for g in range(2):
                    dve.wait_ge(made[g], r + 2)
                    for j in range(G):
                        w = wide[g][j]
                        chain(nc.vector.tensor_scalar(pen[:, :], w[:, 512:640], cn["part"][0:P, 0:1], FAR,
                                                      ALU.not_equal, ALU.mult))
                        chain(nc.vector.tensor_tensor(cand[:, :, :], w[:, 0:512].rearrange("p (h e) -> p h e", h=4),
                                                      spread(pen[:, :], 1, [P, 4, 128]), ALU.add))
                        chain(nc.vector.tensor_reduce(best[:, :], cand[:, :, :], AX.X, ALU.max))
                        b = dve.value_load(tb[0:1, bass.ds(r * (2 * G) + g * G + j, 1)], min_val=0, max_val=NT - 1)
                        a = top[:, bass.ds(b, 1), :].rearrange("p a f -> p (a f)")
                        chain(nc.vector.tensor_tensor(a, a, best[:, :], ALU.max))
                    dve.sem_inc(added[g], 1)
                assert chain.n == per

        @block.tensor
        def _(pe):
            for g in range(2):
                pe.sem_inc(made[g], 1)
            with pe.Fori(0, rounds) as r:
                for g in range(2):
                    pe.wait_ge(diag_ready, r * 2 + (g + 1))
                    pe.wait_ge(added[g], r + 1)
                    for j in range(G):
                        flat = diag[:, g, j, :, :].rearrange("p c e -> p (c e)")
                        nc.tensor.matmul(wide[g][j][:, 0:512], cn["ones"][:, 0:P], flat[:, 0:512], start=True, stop=True)
                        ins = nc.tensor.matmul(wide[g][j][:, 512:640], cn["ones"][:, 0:P], flat[:, 512:640], start=True, stop=True)
                    ins.then_inc(made[g], 1)


def gat_sum(nc, ph, cn, tiles, tab, tb, ge, adm, num):
    G = 4
    hot, hotT = ph.sb("hot", [128, 2, G, P]), ph.sb("hotT", [P, 2, G, 128])
    z0, z1, z2, z3 = (ph.sb(f"z{i}", [128, G, 4]) for i in range(4))
    zz = ph.sb("zz", [128, 2, G, 4])
    recs = ph.sb("recs", [128, 2, G, 20])
    pt = [ph.ps(f"pt{g}", [P, G, 128]) for g in range(2)]
    px = [ph.ps(f"px{g}", [128, G, 8]) for g in range(2)]
    pa = [ph.ps(f"pa{g}", [P, G, 20]) for g in range(2)]

    def pair(name):
        return [ph.sem(f"{name}{g}") for g in range(2)]
    hot_ready, turned, hotT_ready, spread_out, z_ready, e_ready, rec_ready, summed, added = (
        pair(n) for n in ("hot_ready", "turned", "hotT_ready", "spread_out", "z_ready", "e_ready", "rec_ready", "summed", "added"))
    steps = ph.sem("steps")
    tabf = tab[:, :, :].bitcast(F32)
    assert tiles % (2 * G) == 0
    rounds = tiles // (2 * G)
    with nc.Block() as block:
        @block.vector
        def _(dve):
            for g in range(2):
                dve.sem_inc(added[g], 1)
            per = 2 * (4 + G)
            with dve.Fori(0, rounds) as r:
                chain = Chain(dve, steps, r * per)
                for g in range(2):
                    dve.wait_ge(summed[g], r + 1)
                    for j in range(G):
                        t = bass.ds(r * (2 * G) + g * G + j, 1)
                        ins = nc.vector.tensor_scalar(hot[:, g, j, :], cn["ramp"][:, 0:P], tabf[:, t, 1], None, ALU.is_equal)
                    ins.then_inc(hot_ready[g], 1)
                for g in range(2):
                    t = bass.ds(r * (2 * G) + g * G, G)
                    dve.wait_ge(spread_out[g], r + 1)
                    chain(nc.vector.tensor_tensor(z0[:, :, :], px[g][:, :, 0:4], ge[:, t, 16:20], ALU.add))
                    chain(nc.vector.scalar_tensor_tensor(z1[:, :, :], z0[:, :, :], 0.2, z0[:, :, :], ALU.mult, ALU.max))
                    chain(nc.vector.tensor_tensor(z2[:, :, :], z1[:, :, :], px[g][:, :, 4:8], ALU.subtract))
                    nc.vector.tensor_scalar(zz[:, g, :, :], z2[:, :, :], 0.0, None, ALU.min).then_inc(z_ready[g], 1)
                    dve.wait_ge(e_ready[g], r + 1)
                    chain(nc.vector.tensor_tensor(
                        recs[:, g, :, 0:16].rearrange("p t (h e) -> p t h e", h=4),
                        ge[:, t, 0:16].rearrange("p t (h e) -> p t h e", h=4),
                        spread(recs[:, g, :, 16:20], 3, [128, G, 4, 4]), ALU.mult))
                    dve.sem_inc(rec_ready[g], 1)
                for g in range(2):
                    dve.wait_ge(summed[g], r + 2)
                    for j in range(G):
                        b = dve.value_load(tb[0:1, bass.ds(r * (2 * G) + g * G + j, 1)], min_val=0, max_val=NT - 1)
                        a = num[:, bass.ds(b, 1), :].rearrange("p a f -> p (a f)")
                        chain(nc.vector.tensor_tensor(a, a, pa[g][:, j, :], ALU.add))
                    dve.sem_inc(added[g], 1)
                assert chain.n == per

        @block.scalar
        def _(act):
            with act.Fori(0, rounds) as r:
                for g in range(2):
                    act.wait_ge(turned[g], r + 1)
                    nc.scalar.activation(hotT[:, g, :, :], pt[g][:, :, :], ACT.Copy).then_inc(hotT_ready[g], 1)
                for g in range(2):
                    act.wait_ge(z_ready[g], r + 1)
                    nc.scalar.activation(recs[:, g, :, 16:20], zz[:, g, :, :], ACT.Exp).then_inc(e_ready[g], 1)

        @block.tensor
        def _(pe):
            for g in range(2):
                pe.sem_inc(summed[g], 1)
            with pe.Fori(0, rounds) as r:
                for g in range(2):
                    pe.wait_ge(hot_ready[g], r + 1)
                    for j in range(G):
                        ins = nc.tensor.matmul(pt[g][:, j, :], hot[:, g, j, :], cn["ident"][:, :], start=True, stop=True)
                    ins.then_inc(turned[g], 1)
                for g in range(2):
                    pe.wait_ge(hotT_ready[g], r + 1)
                    for j in range(G):
                        b = pe.value_load(tb[0:1, bass.ds(r * (2 * G) + g * G + j, 1)], min_val=0, max_val=NT - 1)
                        ins = nc.tensor.matmul(px[g][:, j, :], hotT[:, g, j, :],
                                               adm[:, bass.ds(b, 1), :].rearrange("p a f -> p (a f)"), start=True, stop=True)
                    ins.then_inc(spread_out[g], 1)
                for g in range(2):
                    pe.wait_ge(rec_ready[g], r + 1)
                    pe.wait_ge(added[g], r + 1)
                    for j in range(G):
                        ins = nc.tensor.matmul(pa[g][:, j, :], hot[:, g, j, :], recs[:, g, j, :], start=True, stop=True)
                    ins.then_inc(summed[g], 1)


def gating(nc, cn, A, x, xT, gates, hs_d):
    with ExitStack() as ctx:
        ph = Phase(nc, ctx, "b1")
        w = ph.sb("w", [128, KC, 16])
        mean, rstd = ph.sb("mean", [P, NT]), ph.sb("rstd", [P, NT])
        h = ph.sb("h", [P, NT, 24])
        att_s, att_d, t16 = ph.sb("att_s", [P, 16]), ph.sb("att_d", [P, 16]), ph.sb("t16", [P, NT, 16])
        u16 = ph.sb("u16", [P, NT, 16])
        top, adm, num = ph.sb("top", [P, NT, 4]), ph.sb("adm", [P, NT, 8]), ph.sb("num", [P, NT, 20])
        tiles = 288
        tab, tb = ph.sb("tab", [128, tiles, 4], I32), ph.sb("tb", [1, tiles], I32)
        ge = ph.sb("ge", [128, tiles, 24])
        bg, lg, lb = ph.sb("bg", [P, 16]), ph.sb("lg", [P, 16]), ph.sb("lb", [P, 16])
        table = nc.dram_tensor("table_b", [128 * tiles, 4], I32, kind="Internal").ap()
        load(nc, ph, [(w[:, :, :], chunks(A["L0_ffn_W_gat"])), (att_s[:, :], row(A["L0_ffn_att_src"])),
                      (att_d[:, :], row(A["L0_ffn_att_dst"])), (bg[:, :], row(A["L0_ffn_b_gat"])),
                      (lg[:, :], row(A["L0_ffn_ln_gamma"])), (lb[:, :], row(A["L0_ffn_ln_beta"]))])
        layer_norm_stats(nc, ph, rstd, mean, x)
        with ExitStack() as inner:
            p2 = Phase(nc, inner, "b2")
            project(nc, p2, cn, x, mean, rstd, xT, w, 16,
                    [(0, 16, "copy", lambda t: h[:, bass.ds(t, 1), 0:16].rearrange("p a f -> p (a f)"), None)], [])
        with ExitStack() as inner:
            p3 = Phase(nc, inner, "b3")
            steps, ready, stored = p3.sem("steps"), p3.sem("ready"), p3.sem("stored")
            with nc.Block() as block:
                @block.vector
                def _(dve):
                    chain = Chain(dve, steps)
                    for att, c in ((att_s, 16), (att_d, 20)):
                        chain(nc.vector.tensor_tensor(t16[:, :, :], h[:, :, 0:16], spread(att[:, :], 1, [P, NT, 16]), ALU.mult))
                        chain(nc.vector.tensor_reduce(h[:, :, c:c + 4], t16[:, :, :].rearrange("p t (h e) -> p t h e", h=4),
                                                      AX.X, ALU.add))
                    dve.sem_inc(ready, 1)
                    nc.vector.tensor_copy(top[:, :, :], h[:, :, 16:20])

                @block.sync
                def _(sp):
                    sp.wait_ge(ready, 1)
                    sp.dma_start(rows(hs_d), h[:, :, 0:20]).then_inc(stored, 16)
                    sp.wait_ge(stored, 16)
        with ExitStack() as inner:
            p4 = Phase(nc, inner, "bt")
            sort_edges(nc, p4, cn, 128, E_GAT // 128, 32, NT, tiles, table, tab, tb, A["L0_ffn_edge_index"][1, :],
                       A["L0_ffn_edge_index"][0, :])
        with ExitStack() as inner:
            p5 = Phase(nc, inner, "bm")
            gat_max(nc, p5, cn, tiles, tab, tb, hs_d, ge, top)
        with ExitStack() as inner:
            p6 = Phase(nc, inner, "b6")
            steps, ready, exped = p6.sem("steps"), p6.sem("ready"), p6.sem("exped")
            e0, e1 = p6.sb("e0", [P, NT, 4]), p6.sb("e1", [P, NT, 4])
            with nc.Block() as block:
                @block.vector
                def _(dve):
                    chain = Chain(dve, steps)
                    chain(nc.vector.tensor_copy(adm[:, :, 0:4], h[:, :, 20:24]))
                    chain(nc.vector.tensor_tensor(e0[:, :, :], top[:, :, :], h[:, :, 20:24], ALU.add))
                    chain(nc.vector.scalar_tensor_tensor(adm[:, :, 4:8], e0[:, :, :], 0.2, e0[:, :, :], ALU.mult, ALU.max))
                    chain(nc.vector.tensor_tensor(e0[:, :, :], h[:, :, 16:20], h[:, :, 20:24], ALU.add))
                    chain(nc.vector.scalar_tensor_tensor(e1[:, :, :], e0[:, :, :], 0.2, e0[:, :, :], ALU.mult, ALU.max))
                    nc.vector.tensor_tensor(e0[:, :, :], e1[:, :, :], adm[:, :, 4:8], ALU.subtract).then_inc(ready, 1)
                    dve.wait_ge(exped, 1)
                    for hd in range(4):
                        nc.vector.tensor_tensor(num[:, :, 4 * hd:4 * hd + 4], h[:, :, 4 * hd:4 * hd + 4],
                                                num[:, :, 16 + hd:17 + hd].to_broadcast([P, NT, 4]), ALU.mult)

                @block.scalar
                def _(act):
                    act.wait_ge(ready, 1)
                    nc.scalar.activation(num[:, :, 16:20], e0[:, :, :], ACT.Exp).then_inc(exped, 1)
        with ExitStack() as inner:
            p7 = Phase(nc, inner, "bs")
            gat_sum(nc, p7, cn, tiles, tab, tb, ge, adm, num)
        with ExitStack() as inner:
            p8 = Phase(nc, inner, "b8")
            steps, ready, rooted, gap, exped = p8.sem("steps"), p8.sem("ready"), p8.sem("rooted"), p8.sem("gap"), p8.sem("exped")
            den, rden, m, v, sd, rs = (p8.sb(n, [P, NT, 4]) for n in ("den", "rden", "m", "v", "sd", "rs"))
            s, s2, eq, far, sel1, sel2 = (p8.sb(n, [P, NT, 4]) for n in ("s", "s2", "eq", "far", "sel1", "sel2"))
            m1, m2, first, dq, q, w1, w2 = (p8.sb(n, [P, NT]) for n in ("m1", "m2", "first", "dq", "q", "w1", "w2"))

            def all4(a):
                return spread(a[:, :], 2, [P, NT, 4])

            def all16(a):
                return spread(a, 2, [P, NT, 16])
            expert = spread(cn["ramp"][0:P, 0:4], 1, [P, NT, 4])
            with nc.Block() as block:
                @block.vector
                def _(dve):
                    chain = Chain(dve, steps)
                    chain(nc.vector.tensor_scalar(den[:, :, :], num[:, :, 16:20], 1e-16, None, ALU.add))
                    chain(nc.vector.reciprocal(rden[:, :, :], den[:, :, :]))
                    for hd in range(4):
                        chain(nc.vector.tensor_tensor(t16[:, :, 4 * hd:4 * hd + 4], num[:, :, 4 * hd:4 * hd + 4],
                                                      rden[:, :, hd:hd + 1].to_broadcast([P, NT, 4]), ALU.mult))
                    chain(nc.vector.tensor_tensor(t16[:, :, :], t16[:, :, :], spread(bg[:, :], 1, [P, NT, 16]), ALU.add))
                    chain(nc.vector.tensor_reduce(m[:, :, 0], t16[:, :, :], AX.X, ALU.add))
                    chain(nc.vector.tensor_scalar(m[:, :, 1], m[:, :, 0], 1.0 / 16, None, ALU.mult))
                    chain(nc.vector.tensor_tensor(t16[:, :, :], t16[:, :, :], all16(m[:, :, 1]), ALU.subtract))
                    chain(nc.vector.tensor_tensor(u16[:, :, :], t16[:, :, :], t16[:, :, :], ALU.mult))
                    chain(nc.vector.tensor_reduce(v[:, :, 0], u16[:, :, :], AX.X, ALU.add))
                    nc.vector.tensor_scalar(v[:, :, 1], v[:, :, 0], 1.0 / 16, EPS, ALU.mult, ALU.add).then_inc(ready, 1)
                    dve.wait_ge(rooted, 1)
                    chain(nc.vector.reciprocal(rs[:, :, 0], sd[:, :, 0]))
                    chain(nc.vector.tensor_tensor(t16[:, :, :], t16[:, :, :], all16(rs[:, :, 0]), ALU.mult))
                    chain(nc.vector.tensor_tensor(t16[:, :, :], t16[:, :, :], spread(lg[:, :], 1, [P, NT, 16]), ALU.mult))
                    chain(nc.vector.tensor_tensor(t16[:, :, :], t16[:, :, :], spread(lb[:, :], 1, [P, NT, 16]), ALU.add))
                    chain(nc.vector.tensor_reduce(s[:, :, :], t16[:, :, :].rearrange("p t (h e) -> p t e h", h=4), AX.X, ALU.add))
                    chain(nc.vector.tensor_scalar(s[:, :, :], s[:, :, :], 0.25, None, ALU.mult))

                    def choose(score, best, sel):
                        chain(nc.vector.tensor_reduce(best[:, :], score[:, :, :], AX.X, ALU.max))
                        chain(nc.vector.tensor_tensor(eq[:, :, :], score[:, :, :], all4(best), ALU.not_equal))
                        chain(nc.vector.scalar_tensor_tensor(far[:, :, :], eq[:, :, :], 100.0, expert, ALU.mult, ALU.add))
                        chain(nc.vector.tensor_reduce(first[:, :], far[:, :, :], AX.X, ALU.min))
                        chain(nc.vector.tensor_tensor(sel[:, :, :], expert, all4(first), ALU.is_equal))
                    choose(s, m1, sel1)
                    chain(nc.vector.scalar_tensor_tensor(s2[:, :, :], sel1[:, :, :], FAR, s[:, :, :], ALU.mult, ALU.add))
                    choose(s2, m2, sel2)
                    nc.vector.tensor_tensor(dq[:, :], m2[:, :], m1[:, :], ALU.subtract).then_inc(gap, 1)
                    dve.wait_ge(exped, 1)
                    chain(nc.vector.tensor_scalar(w2[:, :], q[:, :], 1.0, None, ALU.add))
                    chain(nc.vector.reciprocal(w1[:, :], w2[:, :]))
                    chain(nc.vector.tensor_tensor(w2[:, :], q[:, :], w1[:, :], ALU.mult))
                    chain(nc.vector.tensor_tensor(sel1[:, :, :], sel1[:, :, :], all4(w1), ALU.mult))
                    chain(nc.vector.tensor_tensor(sel2[:, :, :], sel2[:, :, :], all4(w2), ALU.mult))
                    chain(nc.vector.tensor_tensor(gates[:, :, :], sel1[:, :, :], sel2[:, :, :], ALU.add))

                @block.scalar
                def _(act):
                    act.wait_ge(ready, 1)
                    nc.scalar.activation(sd[:, :, 0], v[:, :, 1], ACT.Sqrt).then_inc(rooted, 1)
                    act.wait_ge(gap, 1)
                    nc.scalar.activation(q[:, :], dq[:, :], ACT.Exp).then_inc(exped, 1)


def experts0(nc, cn, A, x, xT, gates):
    M = HID0 // 128
    with ExitStack() as ctx:
        ph = Phase(nc, ctx, "e0")
        w1, w2 = ph.sb("w1", [128, N_EXP0, KC, HID0]), ph.sb("w2", [128, N_EXP0, M, D])
        b1, b2 = ph.sb("b1", [128, N_EXP0, M]), ph.sb("b2", [P, N_EXP0, D])
        hT, tmp = ph.sb("hT", [128, 2, M, P]), ph.sb("tmp", [P, D])
        load(nc, ph, [(w1[:, e, :, :], chunks(A["L0_ffn_W1"][e, :, :])) for e in range(N_EXP0)]
             + [(w2[:, e, :, :], chunks(A["L0_ffn_W2"][e, :, :])) for e in range(N_EXP0)]
             + [(b1[:, :, :], A["L0_ffn_b1"].rearrange("p (e m) -> p e m", e=N_EXP0)),
                (b2[:, :, :].rearrange("p e f -> p (e f)"), row(A["L0_ffn_b2"]))])
        hid = [ph.ps(f"hid{i}", [128, M, P]) for i in range(2)]
        y = [ph.ps(f"y{i}", [P, 512]) for i in range(2)]
        h_made, gelued, y_made, added, steps = (ph.sem(n) for n in ("h_made", "gelued", "y_made", "added", "steps"))
        with nc.Block() as block:
            @block.tensor
            def _(pe):
                pe.sem_inc(y_made, 2)
                with pe.Fori(0, NT) as t:
                    def hidden(e):
                        s = t * N_EXP0 + e
                        pe.wait_ge(gelued, s + 1)
                        for m in range(M):
                            for k in range(KC):
                                ins = nc.tensor.matmul(hid[e % 2][:, m, :], w1[:, e, k, m * 128:(m + 1) * 128],
                                                       xT[:, k, bass.ds(t, 1), :].rearrange("p a f -> p (a f)"),
                                                       start=(k == 0), stop=(k == KC - 1))
                        ins.then_inc(h_made, 1)
                    hidden(0)
                    for e in range(N_EXP0):
                        if e + 1 < N_EXP0:
                            hidden(e + 1)
                        s = t * N_EXP0 + e
                        pe.wait_ge(gelued, s + 3)
                        pe.wait_ge(added, s + 1)
                        for m in range(M):
                            ins = nc.tensor.matmul(y[e % 2][:, 0:D], hT[:, e % 2, m, :], w2[:, e, m, :], start=(m == 0), stop=(m == M - 1))
                        ins.then_inc(y_made, 1)

            @block.scalar
            def _(act):
                act.sem_inc(gelued, 2)
                with act.Fori(0, NT) as t:
                    for e in range(N_EXP0):
                        s = t * N_EXP0 + e
                        act.wait_ge(h_made, s + 1)
                        act.wait_ge(y_made, s + 1)
                        for m in range(M):
                            ins = nc.scalar.activation(hT[:, e % 2, m, :], hid[e % 2][:, m, :], ACT.Gelu, bias=b1[:, e, m:m + 1])
                        ins.then_inc(gelued, 1)

            @block.vector
            def _(dve):
                dve.sem_inc(added, 2)
                with dve.Fori(0, NT) as t:
                    a = x[:, bass.ds(t, 1), :].rearrange("p a f -> p (a f)")
                    chain = Chain(dve, steps, t * (2 * N_EXP0))
                    for e in range(N_EXP0):
                        dve.wait_ge(y_made, t * N_EXP0 + e + 3)
                        chain(nc.vector.tensor_tensor(tmp[:, :], y[e % 2][:, 0:D], b2[:, e, :], ALU.add))
                        dve.sem_inc(added, 1)
                        chain(nc.vector.scalar_tensor_tensor(a, tmp[:, :], gates[:, bass.ds(t, 1), e], a, ALU.mult, ALU.add))


def mix1(nc, cn, A, x, xT, kvp, mean, rstd):
    H1 = 2 * D
    with ExitStack() as ctx:
        ph = Phase(nc, ctx, "m1")
        wq, wm = ph.sb("wq", [128, KC, D]), ph.sb("wm", [128, KC, D])
        w1, w2 = ph.sb("w1", [128, 2 * KC, H1]), ph.sb("w2", [128, 2 * KC, D])
        g1, b1, g2, b2 = (ph.sb(n, [P, D]) for n in ("g1", "b1", "g2", "b2"))
        cb, kb, ks, fold = ph.sb("cb", [128, 2, 128]), ph.sb("kb", [128, 2, 128]), ph.sb("ks", [128, 2]), ph.sb("fold", [128, 2, D])
        msg = ph.sb("msg", [P, NT, D])
        load(nc, ph, [(wq[:, :, :], chunks(A["L1_mix_Wq"])), (wm[:, :, :], chunks(A["L1_mix_Wm"])),
                      (w1[:, :, :], chunks(A["L1_mix_W1"])), (w2[:, :, :], chunks(A["L1_mix_W2"])),
                      (g1[:, :], row(A["L1_mix_g1"])), (b1[:, :], row(A["L1_mix_b1"])),
                      (g2[:, :], row(A["L1_mix_g2"])), (b2[:, :], row(A["L1_mix_b2"]))])

        def tile_of(a, t):
            return a[:, bass.ds(t, 1), :].rearrange("p a f -> p (a f)")
        with ExitStack() as inner:
            p2 = Phase(nc, inner, "m2")
            fold_context(nc, p2, cn, kvp, cb, kb, ks, wm, fold)
        with ExitStack() as inner:
            p3 = Phase(nc, inner, "m3")
            linear_attention(nc, p3, cn, xT, wq, kb, fold, (ALU.add, 1e-6),
                             lambda t, psum: nc.vector.tensor_scalar(tile_of(msg, t), psum, 1.0, None, ALU.mult))
        with ExitStack() as inner:
            p4 = Phase(nc, inner, "m4")
            mm, mr = p4.sb("mm", [P, NT]), p4.sb("mr", [P, NT])
            layer_norm_stats(nc, p4, mr, mm, msg)
            ma, mc, mn = p4.sb("ma", [P, D]), p4.sb("mc", [P, D]), p4.sb("mn", [P, D])
            mT, hr = p4.sb("mT", [128, KC, P]), p4.sb("hr", [128, 4, P])
            pt, hid, po = p4.ps("pt", [128, KC, P]), p4.ps("hid", [128, 4, P]), p4.ps("po", [P, 512])
            mn_ready, turned, mT_ready, h_made, relued, o_made, kept, steps = (
                p4.sem(n) for n in ("mn_ready", "turned", "mT_ready", "h_made", "relued", "o_made", "kept", "steps"))
            with nc.Block() as block:
                @block.vector
                def _(dve):
                    dve.sem_inc(kept, 1)
                    with dve.Fori(0, NT) as t:
                        chain = Chain(dve, steps, t * 3)
                        dve.wait_ge(turned, t + 1)
                        chain(nc.vector.tensor_scalar(ma[:, :], tile_of(msg, t), mm[:, bass.ds(t, 1)], mr[:, bass.ds(t, 1)],
                                                      ALU.subtract, ALU.mult))
                        chain(nc.vector.tensor_tensor(mc[:, :], ma[:, :], g1[:, :], ALU.mult))
                        nc.vector.tensor_tensor(mn[:, :], mc[:, :], b1[:, :], ALU.add).then_inc(mn_ready, 1)
                        dve.wait_ge(o_made, t + 1)
                        chain(nc.vector.tensor_scalar(tile_of(msg, t), po[:, 0:D], 1.0, None, ALU.mult))
                        dve.sem_inc(kept, 1)

                @block.scalar
                def _(act):
                    act.sem_inc(mT_ready, 1)
                    act.sem_inc(relued, 1)
                    with act.Fori(0, NT) as t:
                        act.wait_ge(turned, t + 2)
                        act.wait_ge(h_made, t + 1)
                        nc.scalar.activation(mT[:, :, :], pt[:, :, :], ACT.Copy).then_inc(mT_ready, 1)
                        act.wait_ge(h_made, t + 2)
                        nc.scalar.activation(hr[:, :, :], hid[:, :, :], ACT.Relu).then_inc(relued, 1)

                @block.tensor
                def _(pe):
                    pe.sem_inc(turned, 1)
                    pe.sem_inc(h_made, 1)
                    with pe.Fori(0, NT) as t:
                        pe.wait_ge(mn_ready, t + 1)
                        pe.wait_ge(mT_ready, t + 1)
                        for k in range(KC):
                            ins = nc.tensor.matmul(pt[:, k, :], mn[:, k * 128:(k + 1) * 128], cn["ident"][0:P, 0:P], start=True, stop=True)
                        ins.then_inc(turned, 1)
                        pe.wait_ge(mT_ready, t + 2)
                        pe.wait_ge(relued, t + 1)
                        for m in range(4):
                            for k in range(2 * KC):
                                src = (xT[:, k, bass.ds(t, 1), :].rearrange("p a f -> p (a f)") if k < KC else mT[:, k - KC, :])
                                ins = nc.tensor.matmul(hid[:, m, :], w1[:, k, m * 128:(m + 1) * 128], src,
                                                       start=(k == 0), stop=(k == 2 * KC - 1))
                        ins.then_inc(h_made, 1)
                        pe.wait_ge(relued, t + 2)
                        pe.wait_ge(kept, t + 1)
                        for m in range(4):
                            ins = nc.tensor.matmul(po[:, 0:D], hr[:, m, :], w2[:, m, :], start=(m == 0), stop=(m == 3))
                        ins.then_inc(o_made, 1)
        with ExitStack() as inner:
            p5 = Phase(nc, inner, "m5")
            mm, mr = p5.sb("mm", [P, NT]), p5.sb("mr", [P, NT])
            layer_norm_stats(nc, p5, mr, mm, msg)
            ma, mc, xn = p5.sb("ma", [P, D]), p5.sb("mc", [P, D]), p5.sb("xn", [P, D])
            steps = p5.sem("steps")
            with nc.Block() as block:
                @block.vector
                def _(dve):
                    per = 7
                    with dve.Fori(0, NT) as t:
                        chain = Chain(dve, steps, t * per)
                        a = tile_of(x, t)
                        chain(nc.vector.tensor_scalar(ma[:, :], tile_of(msg, t), mm[:, bass.ds(t, 1)], mr[:, bass.ds(t, 1)],
                                                      ALU.subtract, ALU.mult))
                        chain(nc.vector.tensor_tensor(mc[:, :], ma[:, :], g2[:, :], ALU.mult))
                        chain(nc.vector.tensor_tensor(ma[:, :], mc[:, :], b2[:, :], ALU.add))
                        chain(nc.vector.tensor_scalar(xn[:, :], a, mean[:, bass.ds(t, 1)], rstd[:, bass.ds(t, 1)],
                                                      ALU.subtract, ALU.mult))
                        chain(nc.vector.tensor_tensor(a, a, xn[:, :], ALU.add))
                        chain(nc.vector.tensor_tensor(a, a, ma[:, :], ALU.add))
                        chain.n += 1
                        dve.sem_inc(steps, 1)


def relation_attention(nc, ph, A, sT, o_d):
    R, H, W3 = N_REL, 4, 3 * D
    w, bias = ph.sb("w", [128, KC, W3]), ph.sb("bias", [P, W3])
    load(nc, ph, [(w[:, :, :], chunks(A["L1_gnn_in_proj_wT"])), (bias[:, :], row(A["L1_gnn_in_proj_b"]))])
    sc_T = ph.sb("sc_T", [128, R, 2, P])
    qkv, prod = ph.sb("qkv", [P, R, W3]), ph.sb("prod", [P, R, D])
    sc, ex = ph.sb("sc", [P, H, R, R]), ph.sb("ex", [P, H, R, R])
    mx, sm, rs = ph.sb("mx", [P, H * R]), ph.sb("sm", [P, H * R]), ph.sb("rs", [P, H * R])
    pm, o = ph.sb("pm", [P, H, R]), ph.sb("o", [P, D])
    pq = [[ph.ps(f"pq{i}{c}", [P, 512]) for c in range(2)] for i in range(2)]
    fetched, q_made, q_kept, shifted, exped, o_ready, stored, steps, gate = (
        ph.sem(n) for n in ("fetched", "q_made", "q_kept", "shifted", "exped", "o_ready", "stored", "steps", "gate"))
    with nc.Block() as block:
        @block.gpsimd
        def _(pool):
            with pool.Fori(0, NT) as t:
                pool.wait_ge(q_made, t * R + 1)
                pool.sem_inc(gate, 1)
                nc.gpsimd.tensor_copy(sc_T[:, :, :, :].rearrange("p r h f -> p r (h f)"), sT[:, bass.ds(t * R, R), :]).then_inc(fetched, 1)

        @block.tensor
        def _(pe):
            pe.sem_inc(q_made, 1)
            with pe.Fori(0, NT) as t:
                pe.wait_ge(fetched, t + 1)
                for r in range(R):
                    pe.wait_ge(q_kept, t * R + r + 1)
                    for c, n in ((0, 512), (1, 256)):
                        for k in range(KC):
                            ins = nc.tensor.matmul(pq[r % 2][c][:, 0:n], sc_T[:, r, k, :], w[:, k, 512 * c:512 * c + n],
                                                   start=(k == 0), stop=(k == KC - 1))
                    ins.then_inc(q_made, 1)

        @block.vector
        def _(dve):
            dve.sem_inc(q_kept, 2)
            per = 2 * R + 2 * R + 9
            with dve.Fori(0, NT) as t:
                chain = Chain(dve, steps, t * per)
                for r in range(R):
                    dve.wait_ge(q_made, t * R + r + 2)
                    chain(nc.vector.tensor_tensor(qkv[:, r, 0:512], pq[r % 2][0][:, :], bias[:, 0:512], ALU.add))
                    chain(nc.vector.tensor_tensor(qkv[:, r, 512:W3], pq[r % 2][1][:, 0:256], bias[:, 512:W3], ALU.add))
                    dve.sem_inc(q_kept, 1)
                for r in range(R):
                    chain(nc.vector.tensor_tensor(prod[:, :, :], qkv[:, :, D:2 * D], spread(qkv[:, r, 0:D], 1, [P, R, D]), ALU.mult))
                    chain(nc.vector.tensor_reduce(sc[:, :, r, :].rearrange("p h s -> p s h"),
                                                  prod[:, :, :].rearrange("p s (h d) -> p s h d", h=H), AX.X, ALU.add))
                flat = sc[:, :, :, :].rearrange("p h r s -> p (h r) s")
                eflat = ex[:, :, :, :].rearrange("p h r s -> p (h r) s")
                chain(nc.vector.tensor_reduce(mx[:, :], flat, AX.X, ALU.max))
                nc.vector.tensor_tensor(flat, flat, spread(mx[:, :], 2, [P, H * R, R]), ALU.subtract).then_inc(shifted, 1)
                dve.wait_ge(exped, t + 1)
                chain(nc.vector.tensor_reduce(sm[:, :], eflat, AX.X, ALU.add))
                chain(nc.vector.reciprocal(rs[:, :], sm[:, :]))
                chain(nc.vector.tensor_tensor(eflat, eflat, spread(rs[:, :], 2, [P, H * R, R]), ALU.mult))
                chain(nc.vector.tensor_reduce(pm[:, :, :], ex[:, :, :, :].rearrange("p h r s -> p h s r"), AX.X, ALU.add))
                chain(nc.vector.tensor_scalar(pm[:, :, :], pm[:, :, :], 1.0 / R, None, ALU.mult))
                chain(nc.vector.tensor_tensor(prod[:, :, :].rearrange("p s (h d) -> p s h d", h=H),
                                              qkv[:, :, 2 * D:W3].rearrange("p s (h d) -> p s h d", h=H),
                                              spread(pm[:, :, :].rearrange("p h s -> p s h"), 3, [P, R, H, D // H]), ALU.mult))
                dve.wait_ge(stored, t * 16 + 16)
                chain(nc.vector.tensor_reduce(o[:, :], prod[:, :, :].rearrange("p s f -> p f s"), AX.X, ALU.add))
                chain.n += 1
                dve.sem_inc(steps, 1)
                dve.sem_inc(o_ready, 1)
                assert chain.n == per

        @block.scalar
        def _(act):
            with act.Fori(0, NT) as t:
                act.wait_ge(shifted, t + 1)
                nc.scalar.activation(ex[:, :, :, :], sc[:, :, :, :], ACT.Exp, scale=float(D // H) ** -0.5).then_inc(exped, 1)

        @block.sync
        def _(sp):
            sp.sem_inc(stored, 16)
            with sp.Fori(0, NT) as t:
                sp.wait_ge(o_ready, t + 1)
                sp.dma_start(rows(o_d)[:, bass.ds(t, 1), :].rearrange("p a f -> p (a f)"), o[:, :]).then_inc(stored, 16)
            sp.wait_ge(stored, 16 * NT + 16)


def relation_output(nc, ph, cn, A, x, xT, o_d):
    wo, wp = ph.sb("wo", [128, KC, D]), ph.sb("wp", [128, KC, D])
    ab, pb = ph.sb("ab", [128, KC]), ph.sb("pb", [P, D])
    load(nc, ph, [(wo[:, :, :], chunks(A["L1_gnn_attn_out_wT"])), (wp[:, :, :], chunks(A["L1_gnn_proj_wT"])),
                  (ab[:, :], A["L1_gnn_attn_out_b"]), (pb[:, :], row(A["L1_gnn_proj_b"]))])
    oc, oT, sT = ph.sb("oc", [P, 2, D]), ph.sb("oT", [128, KC, P]), ph.sb("sT", [128, KC, P])
    pt, pa, po = ph.ps("pt", [128, KC, P]), ph.ps("pa", [128, KC, P]), ph.ps("po", [P, 512])
    turned, oT_ready, a_made, sT_ready, o_made, added, steps = (
        ph.sem(n) for n in ("turned", "oT_ready", "a_made", "sT_ready", "o_made", "added", "steps"))
    loaded = ph.sem("loaded")
    with nc.Block() as block:
        @block.sync
        def _(sp):
            with sp.Fori(0, NT) as t:
                sp.wait_ge(turned, t + 1)
                sp.dma_start(oc[:, 0, :], rows(o_d)[:, bass.ds(t, 1), :].rearrange("p a f -> p (a f)")).then_inc(loaded, 16)

        @block.tensor
        def _(pe):
            pe.sem_inc(turned, 1)
            pe.sem_inc(oT_ready, 1)
            pe.sem_inc(a_made, 1)
            pe.sem_inc(o_made, 1)
            pe.sem_inc(added, 1)
            with pe.Fori(0, NT) as t:
                pe.wait_ge(loaded, t * 16 + 16)
                pe.wait_ge(oT_ready, t + 1)
                for k in range(KC):
                    ins = nc.tensor.matmul(pt[:, k, :], oc[:, 0, k * 128:(k + 1) * 128], cn["ident"][0:P, 0:P], start=True, stop=True)
                ins.then_inc(turned, 1)
                pe.wait_ge(oT_ready, t + 2)
                pe.wait_ge(sT_ready, t + 1)
                for h in range(2):
                    for k in range(KC):
                        ins = nc.tensor.matmul(pa[:, h, :], wo[:, k, h * 128:(h + 1) * 128], oT[:, k, :], start=(k == 0), stop=(k == KC - 1))
                ins.then_inc(a_made, 1)
                pe.wait_ge(sT_ready, t + 2)
                pe.wait_ge(added, t + 1)
                for k in range(KC):
                    ins = nc.tensor.matmul(po[:, 0:D], sT[:, k, :], wp[:, k, :], start=(k == 0), stop=(k == KC - 1))
                ins.then_inc(o_made, 1)

        @block.scalar
        def _(act):
            with act.Fori(0, NT) as t:
                act.wait_ge(turned, t + 2)
                act.wait_ge(a_made, t + 1)
                nc.scalar.activation(oT[:, :, :], pt[:, :, :], ACT.Copy).then_inc(oT_ready, 1)

        @block.vector
        def _(dve):
            dve.sem_inc(sT_ready, 1)
            with dve.Fori(0, NT) as t:
                chain = Chain(dve, steps, t * 3)
                a = x[:, bass.ds(t, 1), :].rearrange("p a f -> p (a f)")
                chain(nc.vector.tensor_tensor(a, a, pb[:, :], ALU.add))
                dve.wait_ge(a_made, t + 2)
                dve.wait_ge(o_made, t + 1)
                for h in range(KC):
                    ins = nc.vector.scalar_tensor_tensor(sT[:, h, :], pa[:, h, :], ab[:, h:h + 1],
                                                         xT[:, h, bass.ds(t, 1), :].rearrange("p a f -> p (a f)"), ALU.add, ALU.add)
                chain(ins)
                dve.sem_inc(sT_ready, 1)
                dve.wait_ge(o_made, t + 2)
                chain(nc.vector.tensor_tensor(a, a, po[:, 0:D], ALU.add))
                dve.sem_inc(added, 1)


def turn(nc, ph, cn, x, mean, rstd, xT):
    xc, pt = ph.sb("xc", [P, 2, D]), [ph.ps(f"pt{i}", [128, KC, P]) for i in range(2)]
    normed, turned, kept, gate = ph.sem("normed"), ph.sem("turned"), ph.sem("kept"), ph.sem("gate")
    with nc.Block() as block:
        @block.vector
        def _(dve):
            with dve.Fori(0, NT) as t:
                dve.wait_ge(turned, t + 1)
                nc.vector.tensor_scalar(xc[:, 0, :], x[:, bass.ds(t, 1), :].rearrange("p a f -> p (a f)"), mean[:, bass.ds(t, 1)],
                                        rstd[:, bass.ds(t, 1)], ALU.subtract, ALU.mult).then_inc(normed, 1)

        @block.tensor
        def _(pe):
            pe.sem_inc(turned, 1)
            with pe.Fori(0, NT) as t:
                pe.wait_ge(normed, t + 1)
                pe.wait_ge(kept, t + 1)
                for k in range(KC):
                    ins = nc.tensor.matmul(pt[0][:, k, :], xc[:, 0, k * 128:(k + 1) * 128], cn["ident"][0:P, 0:P], start=True, stop=True)
                ins.then_inc(turned, 1)

        @block.scalar
        def _(act):
            act.sem_inc(kept, 1)
            with act.Fori(0, NT) as t:
                act.wait_ge(turned, t + 2)
                act.sem_inc(gate, 1)
                nc.scalar.activation(xT[:, :, bass.ds(t, 1), :].rearrange("p k a f -> p k (a f)"), pt[0][:, :, :], ACT.Copy).then_inc(kept, 1)


def experts1(nc, cn, A, x, xT):
    M, E = HID1 // 128, N_EXP1
    with ExitStack() as ctx:
        ph = Phase(nc, ctx, "f1")
        mean, rstd = ph.sb("mean", [P, NT]), ph.sb("rstd", [P, NT])
        w1, wg, wd = ph.sb("w1", [128, KC, HID1]), ph.sb("wg", [128, M, E]), ph.sb("wd", [128, M, E, D])
        b1, bg, bd = ph.sb("b1", [128, M]), ph.sb("bg", [P, E]), ph.sb("bd", [P, E, D])
        load(nc, ph, [(w1[:, :, :], chunks(A["L1_ffn_W1"])), (wg[:, :, :], chunks(A["L1_ffn_Wg"])),
                      (b1[:, :], A["L1_ffn_b1"]), (bg[:, :], row(A["L1_ffn_bg"])),
                      (bd[:, :, :].rearrange("p e f -> p (e f)"), row(A["L1_ffn_bd"]))]
             + [(wd[:, :, e, :], chunks(A["L1_ffn_Wd"][e, :, :])) for e in range(E)])
        layer_norm_stats(nc, ph, rstd, mean, x)
        with ExitStack() as inner:
            turn(nc, Phase(nc, inner, "f2"), cn, x, mean, rstd, xT)
        hT = ph.sb("hT", [128, M, P])
        lg, dl, ex, pr, far, sel = (ph.sb(n, [P, E]) for n in ("lg", "dl", "ex", "pr", "far", "sel"))
        mx, sm, rs, pm, first = (ph.sb(n, [P, 1]) for n in ("mx", "sm", "rs", "pm", "first"))
        gate, tmp = ph.sb("gate", [P, E]), ph.sb("tmp", [P, E, D])
        hid = [ph.ps(f"hid{i}", [128, M // 2, P]) for i in range(2)]
        plg, y = ph.ps("plg", [P, E]), [ph.ps(f"y{c}", [P, 512]) for c in range(E // 2)]
        h_made, gelued, g_made, g_read, shifted, exped, y_made, y_read, steps = (
            ph.sem(n) for n in ("h_made", "gelued", "g_made", "g_read", "shifted", "exped", "y_made", "y_read", "steps"))
        with nc.Block() as block:
            @block.tensor
            def _(pe):
                pe.sem_inc(gelued, 1)
                pe.sem_inc(y_made, 1)
                with pe.Fori(0, NT) as t:
                    pe.wait_ge(gelued, t + 1)
                    for m in range(M):
                        for k in range(KC):
                            ins = nc.tensor.matmul(hid[m // 4][:, m % 4, :], w1[:, k, m * 128:(m + 1) * 128],
                                                   xT[:, k, bass.ds(t, 1), :].rearrange("p a f -> p (a f)"),
                                                   start=(k == 0), stop=(k == KC - 1))
                    ins.then_inc(h_made, 1)
                    pe.wait_ge(gelued, t + 2)
                    pe.wait_ge(g_read, t + 1)
                    for m in range(M):
                        ins = nc.tensor.matmul(plg[:, :], hT[:, m, :], wg[:, m, :], start=(m == 0), stop=(m == M - 1))
                    ins.then_inc(g_made, 1)
                    pe.wait_ge(y_read, t + 1)
                    for c in range(E // 2):
                        for m in range(M):
                            ins = nc.tensor.matmul(y[c][:, :], hT[:, m, :], wd[:, m, 2 * c:2 * c + 2, :].rearrange("p e f -> p (e f)"),
                                                   start=(m == 0), stop=(m == M - 1))
                    ins.then_inc(y_made, 1)

            @block.scalar
            def _(act):
                with act.Fori(0, NT) as t:
                    act.wait_ge(h_made, t + 1)
                    act.wait_ge(y_made, t + 1)
                    for m in range(M):
                        ins = nc.scalar.activation(hT[:, m, :], hid[m // 4][:, m % 4, :], ACT.Gelu, bias=b1[:, m:m + 1])
                    ins.then_inc(gelued, 1)
                    act.wait_ge(shifted, t + 1)
                    nc.scalar.activation(ex[:, :], dl[:, :], ACT.Exp).then_inc(exped, 1)

            @block.vector
            def _(dve):
                dve.sem_inc(g_read, 1)
                dve.sem_inc(y_read, 1)
                per = 10 + 1 + E
                expert = cn["ramp"][0:P, 0:E]
                with dve.Fori(0, NT) as t:
                    chain = Chain(dve, steps, t * per)
                    a = x[:, bass.ds(t, 1), :].rearrange("p a f -> p (a f)")
                    dve.wait_ge(g_made, t + 1)
                    chain(nc.vector.tensor_tensor(lg[:, :], plg[:, :], bg[:, :], ALU.add))
                    dve.sem_inc(g_read, 1)
                    chain(nc.vector.tensor_reduce(mx[:, :], lg[:, :], AX.X, ALU.max))
                    nc.vector.tensor_scalar(dl[:, :], lg[:, :], mx[:, :], None, ALU.subtract).then_inc(shifted, 1)
                    dve.wait_ge(exped, t + 1)
                    chain(nc.vector.tensor_reduce(sm[:, :], ex[:, :], AX.X, ALU.add))
                    chain(nc.vector.reciprocal(rs[:, :], sm[:, :]))
                    chain(nc.vector.tensor_scalar(pr[:, :], ex[:, :], rs[:, :], None, ALU.mult))
                    chain(nc.vector.tensor_reduce(pm[:, :], pr[:, :], AX.X, ALU.max))
                    chain(nc.vector.tensor_scalar(far[:, :], pr[:, :], pm[:, :], 100.0, ALU.not_equal, ALU.mult))
                    chain(nc.vector.tensor_tensor(sel[:, :], far[:, :], expert, ALU.add))
                    chain(nc.vector.tensor_reduce(first[:, :], sel[:, :], AX.X, ALU.min))
                    chain(nc.vector.scalar_tensor_tensor(gate[:, :], expert, first[:, :], pr[:, :], ALU.is_equal, ALU.mult))
                    dve.wait_ge(y_made, t + 2)
                    for c in range(E // 2):
                        ins = nc.vector.tensor_tensor(tmp[:, 2 * c:2 * c + 2, :].rearrange("p e f -> p (e f)"), y[c][:, :],
                                                      bd[:, 2 * c:2 * c + 2, :].rearrange("p e f -> p (e f)"), ALU.add)
                    chain(ins)
                    dve.sem_inc(y_read, 1)
                    for e in range(E):
                        chain(nc.vector.scalar_tensor_tensor(a, tmp[:, e, :], gate[:, e:e + 1], a, ALU.mult, ALU.add))
                    assert chain.n == per


def move(nc, ctx, name, pairs):
    ph = Phase(nc, ctx, name)
    moved = ph.sem("moved")
    with nc.Block() as block:
        @block.sync
        def _(sp):
            for to, src in pairs:
                sp.dma_start(to, src).then_inc(moved, 16)
            sp.wait_ge(moved, 16 * len(pairs))


def gps_kernel(nc, A, out):
    with ExitStack() as ctx:
        def sb(name, shape, dt=F32):
            return ctx.enter_context(nc.sbuf_tensor(name, shape, dt))

        def dram(name, shape):
            return nc.dram_tensor(name, shape, F32, kind="Internal").ap()
        cn = {"ident": sb("ident", [128, 128]), "ones": sb("ones", [128, 128]), "tri": sb("tri", [128, 128]),
              "blocks": sb("blocks", [128, 128]), "ramp": sb("ramp", [128, 640]), "part": sb("part", [128, 1]),
              "zeros": sb("zeros", [128, 258]), "one_row": sb("one_row", [128, 150])}
        make_constants(nc, cn)
        x_d, xT_d, o_d = dram("x_kept", [N, D]), dram("xT_kept", [128, KC * N]), dram("attended", [N, D])
        support_d, hs_d, trans_d = dram("support", [N, D]), dram("gat_rows", [N, 20]), dram("transformed", [N_REL * N, D])
        with ExitStack() as mid:
            x = mid.enter_context(nc.sbuf_tensor("x", [P, NT, D], F32))
            xT = mid.enter_context(nc.sbuf_tensor("xT", [128, KC, NT, P], F32))
            gates = mid.enter_context(nc.sbuf_tensor("gates", [P, NT, 4], F32))
            layer0(nc, cn, A, x, xT, support_d)
            gating(nc, cn, A, x, xT, gates, hs_d)
            experts0(nc, cn, A, x, xT, gates)
            with ExitStack() as inner:
                ph = Phase(nc, inner, "c1")
                mean, rstd = ph.sb("mean", [P, NT]), ph.sb("rstd", [P, NT])
                kvp = ph.ps("kvp", [128, 258])
                with ExitStack() as deep:
                    p2 = Phase(nc, deep, "c2")
                    w = p2.sb("w", [128, KC, 2 * D + N_REL * D])
                    bias, tr = p2.sb("bias", [P, N_REL * D]), p2.sb("tr", [P, N_REL * D])
                    k_sb, v_sb = p2.sb("k", [P, D]), p2.sb("v", [P, D])
                    load(nc, p2, [(w[:, :, 0:D], chunks(A["L1_mix_Wk"])), (w[:, :, D:2 * D], chunks(A["L1_mix_Wv"])),
                                  (w[:, :, 2 * D:], chunks(A["L1_gnn_W"])), (bias[:, :], row(A["L1_gnn_b"]))])
                    layer_norm_stats(nc, p2, rstd, mean, x)

                    def part(i):
                        return lambda t: tr[:, 512 * i:512 * i + 512]
                    project(nc, p2, cn, x, mean, rstd, xT, w, 2 * D + N_REL * D,
                            [(0, D, "elu", lambda t: k_sb[:, :], None), (D, D, "copy", lambda t: v_sb[:, :], None)]
                            + [(2 * D + 512 * i, 512, "bias", part(i), bias[:, 512 * i:512 * i + 512]) for i in range(3)],
                            [(rows(trans_d[r * N:(r + 1) * N, :]), tr[:, r * D:(r + 1) * D]) for r in range(N_REL)],
                            kv=(kvp, None, k_sb, v_sb))
                mix1(nc, cn, A, x, xT, kvp, mean, rstd)
                move(nc, inner, "keep", [(rows(x_d), x[:, :, :]), (xT_d, xT[:, :, :, :].rearrange("p k t f -> p (k t f)"))])
        with ExitStack() as mid:
            ph = Phase(nc, mid, "r1")
            nb, tiles = NT * N_REL, 568
            sT = ph.sb("sT", [128, nb, 2 * P])
            table = nc.dram_tensor("table_c", [128 * tiles, 4], I32, kind="Internal").ap()
            with ExitStack() as inner:
                p2 = Phase(nc, inner, "r2")
                tab, tb = p2.sb("tab", [128, tiles, 4], I32), p2.sb("tb", [1, tiles], I32)
                with ExitStack() as deep:
                    sort_edges(nc, Phase(nc, deep, "r3"), cn, P, E_GRAPH // P, 25, nb, tiles, table, tab, tb, A["dst"], A["src"],
                               type_d=A["edge_type_6"])
                with ExitStack() as deep:
                    with nc.Block() as block:
                        @block.vector
                        def _(dve):
                            nc.vector.memset(sT[:, :, :], 0.0)
                    aggregate(nc, Phase(nc, deep, "r4"), cn, tiles, tab, tb, trans_d, sT, False, True)
            with ExitStack() as inner:
                relation_attention(nc, Phase(nc, inner, "r5"), A, sT, o_d)
        with ExitStack() as mid:
            x = mid.enter_context(nc.sbuf_tensor("x_again", [P, NT, D], F32))
            xT = mid.enter_context(nc.sbuf_tensor("xT_again", [128, KC, NT, P], F32))
            move(nc, mid, "fetch", [(x[:, :, :], rows(x_d)), (xT[:, :, :, :].rearrange("p k t f -> p (k t f)"), xT_d)])
            with ExitStack() as inner:
                relation_output(nc, Phase(nc, inner, "r6"), cn, A, x, xT, o_d)
            experts1(nc, cn, A, x, xT)
            move(nc, mid, "out", [(rows(out), x[:, :, :])])


_OUTS = [((N, D), "float32")]


def kernel(**inputs):
    import numpy as _np
    import concourse.bacc as _bacc
    from concourse import mybir as _mybir
    from concourse.bass_utils import run_bass_kernel_spmd as _run

    turned = {"L0_mix_Wq": "L0_mix_WqT", "L0_mix_Wkv": "L0_mix_WkvT", "L0_mix_Wproj": "L0_mix_WprojT",
              "L1_gnn_in_proj_w": "L1_gnn_in_proj_wT", "L1_gnn_attn_out_w": "L1_gnn_attn_out_wT",
              "L1_gnn_proj_w": "L1_gnn_proj_wT"}
    nc = _bacc.Bacc("TRN2", target_bir_lowering=False, num_devices=1)
    arrays, args = {}, {}
    for name, value in inputs.items():
        a = _np.asarray(value)
        if name in turned:
            name, a = turned[name], a.T
        if a.ndim == 3:
            a = a.transpose(1, 0, 2).reshape(a.shape[1], -1) if name in ("L1_gnn_W",) else a
        if name in ("L0_ffn_b1", "L1_ffn_b1", "L1_gnn_attn_out_b"):
            a = a.reshape(-1, 128).T
        if name in ("L0_ffn_att_src", "L0_ffn_att_dst", "L0_ffn_b2", "L1_gnn_b", "L1_ffn_bd"):
            a = a.reshape(-1)
        a = _np.ascontiguousarray(a)
        arrays[f"in_{name}_dram"] = a
        args[name] = nc.dram_tensor(f"in_{name}_dram", a.shape, _mybir.dt.from_np(a.dtype), kind="ExternalInput").ap()
    out = nc.dram_tensor("out_0_dram", _OUTS[0][0], _mybir.dt.float32, kind="ExternalOutput").ap()
    gps_kernel(nc, args, out)
    r = _run(nc, [arrays], core_ids=[0])
    return r.results[0]["out_0_dram"]
```

```python
import concourse.bass as bass
from concourse import mybir
from contextlib import ExitStack

F32 = mybir.dt.float32
I32 = mybir.dt.int32
BF16 = mybir.dt.bfloat16
ALU = mybir.AluOpType
ACT = mybir.ActivationFunctionType
AX = mybir.AxisListType

N = 3125
D = 256
P = 125
NT = N // P
KC = D // 128
E_GRAPH = 53125
E_GAT = 32768
N_REL = 6
N_EXP0 = 4
HID0 = 512
N_EXP1 = 8
HID1 = 1024
ROUND = 12582912.0
FAR = -3.0e38
EPS = 1e-5


class Chain:

    def __init__(self, eng, sem, base=0):
        self.eng, self.sem, self.base, self.n = eng, sem, base, 0

    def __call__(self, ins):
        self.n += 1
        ins.then_inc(self.sem, 1)
        self.eng.wait_ge(self.sem, self.base + self.n)


class Phase:

    def __init__(self, nc, ctx, name):
        self.nc, self.ctx, self.name, self.sems = nc, ctx, name, []
        ctx.callback(self.give_back)

    def sb(self, name, shape, dt=F32):
        return self.ctx.enter_context(self.nc.sbuf_tensor(f"{self.name}_{name}", shape, dt))

    def ps(self, name, shape, dt=F32):
        return self.ctx.enter_context(self.nc.psum_tensor(f"{self.name}_{name}", shape, dt))

    def sem(self, name):
        self.sems.append(self.nc.alloc_semaphore(f"{self.name}_{name}"))
        return self.sems[-1]

    def give_back(self):
        if self.sems:
            self.nc.clear_and_free_semaphores(self.sems)
            self.nc.all_engine_barrier()


def rows(ap):
    return ap.rearrange("(t p) f -> p t f", p=P)


def make_constants(nc, cn):
    with ExitStack() as ctx:
        ph = Phase(nc, ctx, "cst")
        ramp_i = ph.sb("ramp_i", [128, 576], I32)
        part_i = ph.sb("part_i", [128, 1], I32)
        filled, made = ph.sem("filled"), ph.sem("made")
        with nc.Block() as block:
            @block.gpsimd
            def _(pool):
                nc.gpsimd.memset(cn["ident"][:, :], 0.0).then_inc(filled, 1)
                nc.gpsimd.memset(cn["ones"][:, :], 1.0).then_inc(filled, 1)
                nc.gpsimd.memset(cn["tri"][:, :], 1.0).then_inc(filled, 1)
                nc.gpsimd.memset(cn["blocks"][:, :], 0.0).then_inc(filled, 1)
                nc.gpsimd.memset(cn["zeros"][:, :], 0.0).then_inc(filled, 1)
                nc.gpsimd.memset(cn["one_row"][:, :], 1.0).then_inc(filled, 1)
                nc.gpsimd.iota(ramp_i[:, :], [[1, 576]], base=0, channel_multiplier=0).then_inc(made, 1)
                nc.gpsimd.iota(part_i[:, :], [[1, 1]], base=0, channel_multiplier=1).then_inc(made, 1)
                pool.wait_ge(filled, 6)
                nc.gpsimd.affine_select(out=cn["ident"][:, :], in_=cn["ident"][:, :], compare_op=ALU.not_equal,
                                        fill=1.0, base=0, pattern=[[-1, 128]], channel_multiplier=1).then_inc(made, 1)
                nc.gpsimd.affine_select(out=cn["tri"][:, :], in_=cn["tri"][:, :], compare_op=ALU.is_gt,
                                        fill=0.0, base=0, pattern=[[1, 128]], channel_multiplier=-1).then_inc(made, 1)

            @block.vector
            def _(dve):
                dve.wait_ge(made, 4)
                nc.vector.tensor_copy(cn["ramp"][:, :], ramp_i[:, :])
                nc.vector.tensor_copy(cn["part"][:, :], part_i[:, :])
                for h in range(4):
                    nc.vector.memset(cn["blocks"][32 * h:32 * h + 32, 32 * h:32 * h + 32], 1.0)


def layer_norm_stats(nc, ph, rstd, mean, x, tiles=NT):
    st = ph.sb("st", [P, tiles, 6])
    mv = ph.sb("mv", [P, tiles, 2])
    ve = ph.sb("ve", [P, tiles])
    sd = ph.sb("sd", [P, tiles])
    steps, var_ready, root_ready = ph.sem("ln_steps"), ph.sem("var_ready"), ph.sem("root_ready")
    with nc.Block() as block:
        @block.vector
        def _(dve):
            chain = Chain(dve, steps)
            with dve.Fori(0, tiles) as t:
                nc.vector.bn_stats(st[:, bass.ds(t, 1), :].rearrange("p a f -> p (a f)"),
                                   x[:, bass.ds(t, 1), :].rearrange("p a f -> p (a f)")).then_inc(steps, 1)
            chain.n = tiles
            dve.wait_ge(steps, tiles)
            for t in range(tiles):
                last = nc.vector.bn_aggr(mv[:, t, :], st[:, t, :])
                if t < tiles - 1:
                    last.then_inc(steps, 1)
                    chain.n += 1
            chain(last)
            chain(nc.vector.tensor_copy(mean[:, :], mv[:, :, 0]))
            nc.vector.tensor_scalar(ve[:, :], mv[:, :, 1], EPS, None, ALU.add).then_inc(var_ready, 1)
            dve.wait_ge(root_ready, 1)
            nc.vector.reciprocal(rstd[:, :], sd[:, :])

        @block.scalar
        def _(act):
            act.wait_ge(var_ready, 1)
            nc.scalar.activation(sd[:, :], ve[:, :], ACT.Sqrt).then_inc(root_ready, 1)


class Sorting:

    def __init__(self, nc, keep, work, parts, cols, step, nb, tiles, fields, key_d, other_d, type_d=None, weight_d=None,
                 kept=None):
        self.nc, self.parts, self.cols, self.step, self.nb, self.tiles = nc, parts, cols, step, nb, tiles
        self.key_d, self.other_d, self.type_d, self.weight_d = key_d, other_d, type_d, weight_d
        assert cols % step == 0 and tiles % 16 == 0 and tiles >= parts * cols // 128 + nb
        self.rounds = cols // step
        self.tab, self.tb = kept or (keep.sb("tab", [128, tiles, fields], I32), keep.sb("tb", [1, tiles], I32))
        self.table = nc.dram_tensor(f"table_{keep.name}", [128 * tiles, fields], I32, kind="Internal").ap()
        self.addr, self.rec = work.sb("addr", [parts, cols], I32), work.sb("rec", [parts, cols, fields], I32)
        self.ridx, self.rrec = work.sb("ridx", [parts, step], I32), work.sb("rrec", [parts, step, fields], I32)
        self.recs_ready, self.cleared = work.sem("recs_ready"), work.sem("cleared")
        self.copied, self.scattered, self.gate = work.sem("copied"), work.sem("scattered"), work.sem("gate")

    def load_columns(self, ph):
        shape = [self.parts, self.cols]
        self.key_i, self.other_i, self.one = ph.sb("key_i", shape, I32), ph.sb("other_i", shape, I32), ph.sb("one", shape)
        self.type_i = ph.sb("type_i", shape, I32) if self.type_d is not None else None
        self.loaded, self.empty_ready = ph.sem("loaded"), ph.sem("empty_ready")
        self.n_loads = 2 + (self.type_d is not None) + (self.weight_d is not None)

    def feed(self, sp):
        def cut(d):
            return d.rearrange("(p c) -> p c", p=self.parts)
        sp.dma_start(self.key_i[:, :], cut(self.key_d)).then_inc(self.loaded, 16)
        sp.dma_start(self.other_i[:, :], cut(self.other_d)).then_inc(self.loaded, 16)
        if self.type_d is not None:
            sp.dma_start(self.type_i[:, :], cut(self.type_d)).then_inc(self.loaded, 16)
        if self.weight_d is not None:
            sp.dma_start(self.one[:, :], cut(self.weight_d)).then_inc(self.loaded, 16)

    def clear(self, sp):
        sp.wait_ge(self.empty_ready, 1)
        sp.dma_start(self.table.rearrange("(p t) f -> p t f", p=128), self.tab[:, :, :]).then_inc(self.cleared, 16)
        sp.wait_ge(self.cleared, 16)

    def scatter(self, pool, first, last):
        nc, step = self.nc, self.step
        pool.wait_ge(self.recs_ready, 1)
        pool.wait_ge(self.cleared, 16)
        with pool.Fori(first, last) as c:
            nc.gpsimd.tensor_copy(self.ridx[:, :], self.addr[:, bass.ds(c * step, step)]).then_inc(self.copied, 1)
            nc.gpsimd.tensor_copy(self.rrec[:, :, :], self.rec[:, bass.ds(c * step, step), :]).then_inc(self.copied, 1)
            pool.wait_ge(self.copied, c * 2 + 2)
            pool.sem_inc(self.gate, 1)
            for u in range(step):
                nc.gpsimd.indirect_dma_start(self.table, bass.IndirectOffsetOnAxis(ap=self.ridx[:, u:u + 1], axis=0),
                                             self.rrec[:, u, :], None).then_inc(self.scattered, 16)
            pool.wait_ge(self.scattered, c * (16 * step) + 16 * step)
            pool.sem_inc(self.gate, 1)


def reload_tables(nc, ph, sorts):
    reloaded = ph.sem("reloaded")
    with nc.Block() as block:
        @block.sync
        def _(sp):
            for s in sorts:
                sp.dma_start(s.tab[:, :, :], s.table.rearrange("(p t) f -> p t f", p=128)).then_inc(reloaded, 16)
            sp.wait_ge(reloaded, 16 * len(sorts))


def sort_addresses(nc, ctx, cn, name, sorts, pool_job=None):
    work = []
    pmax, cmax = max(s.parts for s in sorts), max(s.cols for s in sorts)
    ph = Phase(nc, ctx, f"sorts_{name}")
    for s in sorts:
        s.load_columns(Phase(nc, ctx, f"cols_{name}{len(work)}"))
        work.append(s)
    nbmax, tmax = max(s.nb for s in sorts), max(s.tiles for s in sorts)
    key_a, bk_a, loc_a, pos_a, run_a = (ph.sb(n, [pmax, cmax]) for n in ("key", "bk", "loc", "pos", "run"))
    hit_a = ph.sb("hit", [pmax, 2, cmax])
    run2_a, pos2_a = ph.sb("run2", [pmax, cmax]), ph.sb("pos2", [pmax, cmax])
    cnt_a, pre_a = ph.sb("cnt", [pmax, nbmax]), ph.sb("pre", [pmax, nbmax])
    tot_a, lots_a, upto_a, start_a = (ph.sb(n, [128, nbmax]) for n in ("tot", "lots", "upto", "start"))
    begun_a, start_p = ph.sb("begun", [P, tmax]), ph.sb("start_p", [P, 1])
    ps_tot, ps_pre = ph.ps("ps_tot", [128, nbmax]), ph.ps("ps_pre", [128, nbmax])
    ps_start, ps_tb = ph.ps("ps_start", [P, 1]), [ph.ps(f"ps_tb{i}", [1, 512]) for i in range((tmax + 511) // 512)]
    steps, counted, summed = ph.sem("steps"), ph.sem("counted"), ph.sem("summed")
    started, start_moved, begun_ready, begun_used = (
        ph.sem(n) for n in ("started", "start_moved", "begun_ready", "begun_used"))

    gate = ph.sem("gate")
    n_groups = [0]
    for s in sorts:
        n_groups.append(n_groups[-1] + (s.nb + P - 1) // P)

    with nc.Block() as block:
        @block.sync
        def _(sp):
            for s in sorts:
                s.feed(sp)
            for s in sorts:
                s.clear(sp)

        @block.vector
        def _(dve):
            chain = Chain(dve, steps)
            for n, s in enumerate(sorts):
                p, c, nb = s.parts, s.cols, s.nb
                key, bk, loc, pos = key_a[0:p, 0:c], bk_a[0:p, 0:c], loc_a[0:p, 0:c], pos_a[0:p, 0:c]
                hits, runs = (hit_a[0:p, 0, 0:c], hit_a[0:p, 1, 0:c]), (run_a[0:p, 0:c], run2_a[0:p, 0:c])
                hit, run, one = hits[0], runs[0], s.one[:, :]
                places = (pos, pos2_a[0:p, 0:c])
                cnt, pre, lots, upto, start = (cnt_a[0:p, 0:nb], pre_a[0:p, 0:nb], lots_a[:, 0:nb], upto_a[:, 0:nb],
                                               start_a[:, 0:nb])
                recf = s.rec[:, :, :].bitcast(F32)
                chain(nc.vector.memset(s.tab[:, :, :], 0))
                nc.vector.memset(s.tab[:, :, 1].bitcast(F32), -1.0).then_inc(s.empty_ready, 1)
                chain(nc.vector.memset(s.rec[:, :, :], 0))
                for a in places:
                    chain(nc.vector.memset(a, 0.0))
                dve.wait_ge(s.loaded, 16 * s.n_loads)
                if s.weight_d is not None:
                    chain(nc.vector.tensor_copy(recf[:, :, 2], one))
                chain(nc.vector.memset(one, 1.0))
                chain(nc.vector.tensor_copy(key, s.key_i[:, :]))
                chain(nc.vector.tensor_scalar(bk, key, -float(P // 2), 1.0 / P, ALU.add, ALU.mult))
                chain(nc.vector.tensor_scalar(bk, bk, ROUND, None, ALU.add))
                chain(nc.vector.tensor_scalar(bk, bk, -ROUND, None, ALU.add))
                chain(nc.vector.scalar_tensor_tensor(loc, bk, -float(P), key, ALU.mult, ALU.add))
                chain(nc.vector.tensor_copy(recf[:, :, 1], loc))
                if s.type_d is not None:
                    chain(nc.vector.tensor_copy(hit, s.type_i[:, :]))
                    chain(nc.vector.scalar_tensor_tensor(key, bk, float(N_REL), hit, ALU.mult, ALU.add))
                    chain(nc.vector.tensor_copy(run, s.other_i[:, :]))
                    chain(nc.vector.scalar_tensor_tensor(run, hit, float(N), run, ALU.mult, ALU.add))
                    chain(nc.vector.tensor_copy(s.rec[:, :, 0], run))
                else:
                    chain(nc.vector.tensor_copy(key, bk))
                    chain(nc.vector.tensor_copy(s.rec[:, :, 0], s.other_i[:, :]))
                k0 = chain.n
                with dve.Fori(0, nb) as b:
                    nc.vector.tensor_scalar(hit, key, cn["ramp"][0:p, bass.ds(b, 1)], 0.0, ALU.is_equal,
                                            ALU.add, accum_out=cnt_a[0:p, bass.ds(b, 1)]).then_inc(steps, 1)
                    dve.wait_ge(steps, b + (k0 + 1))
                chain.n = k0 + nb
                nc.vector.tensor_copy(pre[:, 0:1], cnt[:, 0:1]).then_inc(counted, 1)
                dve.wait_ge(summed, n + 1)
                chain(nc.vector.tensor_scalar(lots, ps_tot[:, 0:nb], 1.0 / 128, -127.0 / 256, ALU.mult, ALU.add))
                chain(nc.vector.tensor_scalar(lots, lots, ROUND, None, ALU.add))
                chain(nc.vector.tensor_scalar(lots, lots, -ROUND, 1.0, ALU.add, ALU.add))
                chain(nc.vector.tensor_tensor_scan(upto, cn["one_row"][:, 0:nb], lots, 0.0, ALU.mult, ALU.add))
                chain(nc.vector.tensor_tensor(start, upto, lots, ALU.subtract))
                chain(nc.vector.scalar_tensor_tensor(pre, start[0:p, :], 128.0, ps_pre[0:p, 0:nb], ALU.mult, ALU.add))
                dve.sem_inc(started, 1)
                for a in range(0, nb, P):
                    m, g = min(P, nb - a), n_groups[n] + a // P
                    dve.wait_ge(start_moved, g + 1)
                    chain(nc.vector.tensor_copy(start_p[0:m, :], ps_start[0:m, :]))
                    if g:
                        dve.wait_ge(begun_used, g)
                    nc.vector.tensor_scalar(begun_a[0:m, 0:s.tiles], cn["ramp"][0:m, 0:s.tiles], start_p[0:m, :], None,
                                            ALU.is_ge).then_inc(begun_ready, 1)
                dve.wait_ge(begun_used, n_groups[n + 1])
                for a in range(0, s.tiles, 512):
                    m = min(512, s.tiles - a)
                    chain(nc.vector.tensor_scalar(s.tb[0:1, a:a + m], ps_tb[a // 512][0:1, 0:m], -1.0, None, ALU.add))
                def slots(pair, base):
                    done = 0
                    for what in range(3):
                        for i, bs in enumerate(pair):
                            if what == 0:
                                ins = nc.vector.tensor_scalar(hits[i], key, cn["ramp"][0:p, bs], None, ALU.is_equal)
                            elif what == 1:
                                dve.wait_ge(steps, base + (i + 1))
                                ins = nc.vector.tensor_tensor_scan(runs[i], one, hits[i], pre_a[0:p, bs], ALU.mult, ALU.add)
                            else:
                                dve.wait_ge(steps, base + (len(pair) + i + 1))
                                dve.sem_inc(gate, 1)
                                ins = nc.vector.copy_predicated(places[i], hits[i].bitcast(I32), runs[i])
                            ins.then_inc(steps, 1)
                            done += 1
                    dve.wait_ge(steps, base + done)
                    dve.sem_inc(gate, 1)
                k0 = chain.n
                with dve.Fori(0, nb // 2) as b2:
                    slots([bass.ds(b2 * 2 + i, 1) for i in range(2)], b2 * 6 + k0)
                chain.n = k0 + 6 * (nb // 2)
                if nb % 2:
                    slots([slice(nb - 1, nb)], chain.n)
                    chain.n += 3
                chain(nc.vector.tensor_tensor(pos, pos, places[1], ALU.add))
                chain(nc.vector.tensor_scalar(pos, pos, -1.0, None, ALU.add))
                chain(nc.vector.tensor_scalar(bk, pos, 1.0 / 128, -127.0 / 256, ALU.mult, ALU.add))
                chain(nc.vector.tensor_scalar(bk, bk, ROUND, None, ALU.add))
                chain(nc.vector.tensor_scalar(bk, bk, -ROUND, None, ALU.add))
                chain(nc.vector.scalar_tensor_tensor(run, bk, -128.0, pos, ALU.mult, ALU.add))
                chain(nc.vector.scalar_tensor_tensor(run, run, float(s.tiles), bk, ALU.mult, ALU.add))
                chain(nc.vector.tensor_copy(s.addr[:, :], run))
                dve.sem_inc(s.recs_ready, 1)

        @block.tensor
        def _(pe):
            for n, s in enumerate(sorts):
                pe.wait_ge(counted, n + 1)
                nc.tensor.matmul(ps_tot[:, 0:s.nb], cn["ones"][0:s.parts, :], cnt_a[0:s.parts, 0:s.nb], start=True, stop=True)
                nc.tensor.matmul(ps_pre[:, 0:s.nb], cn["tri"][0:s.parts, :], cnt_a[0:s.parts, 0:s.nb],
                                 start=True, stop=True).then_inc(summed, 1)
                pe.wait_ge(started, n + 1)
                for a in range(0, s.nb, P):
                    m, g = min(P, s.nb - a), n_groups[n] + a // P
                    if g:
                        pe.wait_ge(begun_ready, g)
                    nc.tensor.matmul(ps_start[0:m, :], start_a[0:1, a:a + m], cn["ones"][0:1, 0:1], start=True,
                                     stop=True).then_inc(start_moved, 1)
                    pe.wait_ge(begun_ready, g + 1)
                    for c in range(0, s.tiles, 512):
                        w = min(512, s.tiles - c)
                        ins = nc.tensor.matmul(ps_tb[c // 512][0:1, 0:w], cn["ones"][0:m, 0:1], begun_a[0:m, c:c + w],
                                               start=(a == 0), stop=(a + P >= s.nb))
                    ins.then_inc(begun_used, 1)

        @block.gpsimd
        def _(pool):
            if pool_job is not None:
                pool_job(pool)


def tile_numbers(nc, eng, tb, first, count):
    kind = {"vector": mybir.EngineType.DVE, "tensor": mybir.EngineType.PE}[eng]
    return nc.values_load_multi_w_load_instructions(
        tb[0:1, bass.ds(first, count)], engines=(kind,), min_val=0, max_val=None,
        skip_runtime_bounds_check_because="a bucket is a count of starts below the tile")[1]


def aggregate(nc, ph, cn, so, source, acc, weighted, transposed, pool_job=None):
    G, NG = 4, 4
    tiles, tab = so.tiles, so.tab
    gath, hot = ph.sb("gath", [128, NG, G, D]), ph.sb("hot", [128, NG, G, P])
    idx = ph.sb("idx", [128, NG, G], I32)
    out_p = 128 if transposed else P
    prod = [[ph.ps(f"prod{s}{j}", [128, 512]) for j in range(G)] for s in range(2)]
    w = 2 * P if transposed else D
    gathered = [ph.sem(f"gathered{g}") for g in range(NG)]
    hot_ready = [ph.sem(f"hot_ready{g}") for g in range(NG)]
    used = [ph.sem(f"used{g}") for g in range(NG)]
    added = [ph.sem(f"added{s}") for s in range(2)]
    idx_ready, gate, gate_a, steps = ph.sem("idx_ready"), ph.sem("gate"), ph.sem("gate_a"), ph.sem("steps")
    tabf = tab[:, :, :].bitcast(F32)
    step = NG * G
    rounds = tiles // step

    with nc.Block() as block:
        @block.gpsimd
        def _(pool):
            with pool.Fori(0, rounds) as r:
                for g in range(NG):
                    pool.wait_ge(idx_ready, r * NG + (g + 1))
                    pool.sem_inc(gate, 1)
                    for j in range(G):
                        nc.gpsimd.indirect_dma_start(gath[:, g, j, :], None, source,
                                                     bass.IndirectOffsetOnAxis(ap=idx[:, g, j:j + 1], axis=0)
                                                     ).then_inc(gathered[g], 16)

        @block.scalar
        def _(act):
            with act.Fori(0, rounds) as r:
                for g in range(NG):
                    act.wait_ge(used[g], r + 1)
                    act.sem_inc(gate_a, 1)
                    nc.scalar.activation(idx[:, g, :], tab[:, bass.ds(r * step + g * G, G), 0], ACT.Copy).then_inc(idx_ready, 1)

        @block.vector
        def _(dve):
            for s in range(2):
                dve.sem_inc(added[s], 1)
            def one_hot(r, g, j):
                if j == 0:
                    dve.wait_ge(used[g], r + 1)
                t = bass.ds(r * step + g * G + j, 1)
                ins = nc.vector.tensor_scalar(
                    hot[:, g, j, :], cn["ramp"][:, 0:P], tabf[:, t, 1], tabf[:, t, 2] if weighted else 1.0,
                    ALU.is_equal, ALU.mult)
                if j == G - 1:
                    ins.then_inc(hot_ready[g], 1)

            def one_round(r, last):
                for g in range(NG):
                    numbers = tile_numbers(nc, "vector", so.tb, r * step + g * G, G)
                    dve.wait_ge(used[g], r + 2)
                    for j in range(G):
                        a = acc[:, bass.ds(numbers[j], 1), :].rearrange("p a f -> p (a f)")
                        nc.vector.tensor_tensor(a, a, prod[g % 2][j][0:out_p, 0:w], ALU.add).then_inc(steps, 1)
                        if g + 2 < NG:
                            one_hot(r, g + 2, j)
                        elif not last:
                            one_hot(r + 1, g + 2 - NG, j)
                        dve.wait_ge(steps, r * step + (g * G + j + 1))
                    dve.sem_inc(added[g % 2], 1)
            for g in range(2):
                for j in range(G):
                    one_hot(0, g, j)
            with dve.Fori(0, rounds - 1) as r:
                one_round(r, False)
            one_round(rounds - 1, True)

        @block.tensor
        def _(pe):
            for g in range(NG):
                pe.sem_inc(used[g], 1)
            with pe.Fori(0, rounds) as r:
                for g in range(NG):
                    pe.wait_ge(gathered[g], r * (16 * G) + 16 * G)
                    pe.wait_ge(hot_ready[g], r + 1)
                    pe.wait_ge(added[g % 2], r * 2 + (g // 2 + 1))
                    for j in range(G):
                        if transposed:
                            for h in range(2):
                                ins = nc.tensor.matmul(prod[g % 2][j][:, h * P:(h + 1) * P], gath[:, g, j, h * 128:(h + 1) * 128],
                                                       hot[:, g, j, :], start=True, stop=True)
                        else:
                            ins = nc.tensor.matmul(prod[g % 2][j][0:P, 0:D], hot[:, g, j, :], gath[:, g, j, :], start=True, stop=True)
                    ins.then_inc(used[g], 1)


def project(nc, ph, cn, x, mean, rstd, xT, w_sb, width, evac, stores, kv=None, copies=2, pool_job=None):
    xc, xTc = ph.sb("xc", [P, 2, D]), ph.sb("xTc", [128, 2, KC, P])
    nb = (width + 511) // 512
    pt, po = [ph.ps(f"pt{i}", [128, KC, P]) for i in range(2)], [ph.ps(f"po{i}", [P, 512]) for i in range(nb * copies)]
    low, low_e = ph.sb("low", [P, D]), ph.sb("low_e", [P, D])
    normed, turned, xT_ready, pt_free = ph.sem("normed"), ph.sem("turned"), ph.sem("xT_ready"), ph.sem("pt_free")
    made, evacuated = ph.sem("made"), ph.sem("evacuated")
    stored = [ph.sem(f"stored{i}") for i in range(2)]
    gate, lowered, exped, kv_ready, kv_used = (ph.sem(n) for n in ("gate", "lowered", "exped", "kv_ready", "kv_used"))
    n_st = len(stores)
    assert NT % 2 == 1

    def bank(s, i):
        return po[i + (s * nb if copies == 2 else 0)]

    def each_tile(eng, do):
        with eng.Fori(0, NT // 2) as i:
            for s in range(2):
                do(i * 2 + s, s, i)
        do(NT - 1, 0, NT // 2)

    with nc.Block() as block:
        @block.gpsimd
        def _(pool):
            if pool_job is not None:
                pool_job(pool)

        @block.vector
        def _(dve):
            dve.sem_inc(evacuated, copies * nb)
            if kv is not None:
                nc.vector.memset(kv[1][:, 1, :], 0.0)
                nc.vector.memset(kv[2][:, 1, :], 0.0).then_inc(kv_ready, 1)

            def norm(t, s):
                dve.wait_ge(turned, t + 1)
                nc.vector.tensor_scalar(xc[:, s, :], x[:, bass.ds(t, 1), :].rearrange("p a f -> p (a f)"), mean[:, bass.ds(t, 1)],
                                        rstd[:, bass.ds(t, 1)], ALU.subtract, ALU.mult).then_inc(normed, 1)

            def tile(t, s, i):
                if not (isinstance(t, int) and t == NT - 1):
                    norm(t + 1, 1 - s)
                if kv is not None:
                    dve.wait_ge(kv_used, t + 1)
                if n_st:
                    dve.wait_ge(stored[s], i * (16 * n_st) + 16 * n_st)
                for b in range(nb):
                    dve.wait_ge(made, t * nb + (2 * nb + b + 1))
                    mine = [e for e in evac if e[0] // 512 == b]
                    elus = [e for e in mine if e[2] == "elu"]
                    for c, n, kind, to, bias in elus:
                        nc.vector.tensor_scalar(low[:, :], bank(s, b)[:, c % 512:c % 512 + n], 0.0, None,
                                                ALU.min).then_inc(lowered, 1)
                    for c, n, kind, to, bias in [e for e in mine if e[2] != "elu"] + elus:
                        src = bank(s, b)[:, c % 512:c % 512 + n]
                        if kind == "bias":
                            ins = nc.vector.tensor_tensor(to(t, s), src, bias, ALU.add)
                        elif kind == "copy":
                            ins = nc.vector.tensor_scalar(to(t, s), src, 1.0, None, ALU.mult)
                        else:
                            dve.wait_ge(exped, t + 1)
                            ins = nc.vector.scalar_tensor_tensor(to(t, s), src, 0.0, low_e[:, :], ALU.max, ALU.add)
                    ins.then_inc(evacuated, 1)
                    if kv is not None and b == 0:
                        dve.wait_ge(evacuated, t * nb + (copies * nb + 1))
                        dve.sem_inc(kv_ready, 1)
            norm(0, 0)
            each_tile(dve, tile)

        @block.scalar
        def _(act):
            act.sem_inc(pt_free, 2)

            def tile(t, s, i):
                act.wait_ge(turned, t + 3)
                act.wait_ge(made, t * nb + nb)
                nc.scalar.activation(xTc[:, s, :, :], pt[s][:, :, :], ACT.Copy).then_inc(xT_ready, 1)
                act.sem_inc(gate, 1)
                nc.scalar.activation(xT[:, :, bass.ds(t, 1), :].rearrange("p k a f -> p k (a f)"), pt[s][:, :, :],
                                     ACT.Copy).then_inc(pt_free, 1)
                if kv is not None:
                    act.wait_ge(lowered, t + 1)
                    nc.scalar.activation(low_e[:, :], low[:, :], ACT.Exp).then_inc(exped, 1)
            each_tile(act, tile)

        @block.sync
        def _(sp):
            if not n_st:
                return
            for s in range(2):
                sp.sem_inc(stored[s], 16 * n_st)

            def tile(t, s, i):
                for b, to, buf in stores:
                    sp.wait_ge(evacuated, t * nb + (copies * nb + b + 1))
                    sp.dma_start(to(t), buf(s)).then_inc(stored[s], 16)
            each_tile(sp, tile)
            sp.wait_ge(stored[0], (NT // 2 + 2) * 16 * n_st)
            sp.wait_ge(stored[1], (NT // 2 + 1) * 16 * n_st)

        @block.tensor
        def _(pe):
            pe.sem_inc(turned, 2)
            pe.sem_inc(kv_used, 1)
            pe.sem_inc(made, 2 * nb)

            def turn_tile(t, s):
                pe.wait_ge(normed, t + 1)
                pe.wait_ge(pt_free, t + 1)
                for k in range(KC):
                    ins = nc.tensor.matmul(pt[s][:, k, :], xc[:, s, k * 128:(k + 1) * 128], cn["ident"][0:P, 0:P], start=True, stop=True)
                ins.then_inc(turned, 1)

            def add_kv(t, s):
                kvp, k_sb, v_sb = kv
                pe.wait_ge(kv_ready, t + 1)
                for h in range(2):
                    hs = slice(h * 128, (h + 1) * 128)
                    nc.tensor.matmul(kvp[:, hs], v_sb[:, s, hs], k_sb[:, s, hs], start=False, stop=False, skip_group_check=True)
                    ins = nc.tensor.matmul(kvp[:, 256 + h:257 + h], k_sb[:, s, hs], cn["ones"][0:P, 0:1],
                                           start=False, stop=False, skip_group_check=True)
                ins.then_inc(kv_used, 1)

            def tile(t, s, i):
                if not (isinstance(t, int) and t == NT - 1):
                    turn_tile(t + 1, 1 - s)
                pe.wait_ge(xT_ready, t + 1)
                for b in range(nb):
                    n = min(512, width - 512 * b)
                    pe.wait_ge(evacuated, t * nb + (b + 1))
                    for k in range(KC):
                        ins = nc.tensor.matmul(bank(s, b)[:, 0:n], xTc[:, s, k, :], w_sb[:, k, 512 * b:512 * b + n],
                                               start=(k == 0), stop=(k == KC - 1))
                    ins.then_inc(made, 1)
                if kv is not None:
                    add_kv(t, 1 - s)
            if kv is not None:
                nc.tensor.matmul(kv[0][:, :], cn["zeros"][:, 0:128], cn["zeros"][:, 0:258], start=True, stop=False)
            turn_tile(0, 0)
            each_tile(pe, tile)
            if kv is not None:
                add_kv(NT, 0)
                nc.tensor.matmul(kv[0][:, :], cn["zeros"][:, 0:128], cn["zeros"][:, 0:258], start=False, stop=True)


def fold_context(nc, ph, cn, kvp, cb, kb, ks, wT, fold):
    pf = [ph.ps(f"pf{h}", [128, D]) for h in range(2)]
    ready, made, steps = ph.sem("fc_ready"), ph.sem("fc_made"), ph.sem("fc_steps")
    with nc.Block() as block:
        @block.vector
        def _(dve):
            chain = Chain(dve, steps)
            chain(nc.vector.tensor_copy(ks[:, :], kvp[:, 256:258]))
            for h in range(2):
                nc.vector.tensor_scalar(kb[:, h, :], cn["blocks"][:, :], ks[:, h:h + 1], None, ALU.mult)
                chain(nc.vector.tensor_tensor(cb[:, h, :], kvp[:, h * 128:(h + 1) * 128], cn["blocks"][:, :], ALU.mult))
            dve.sem_inc(ready, 1)
            dve.wait_ge(made, 1)
            for h in range(2):
                nc.vector.tensor_copy(fold[:, h, :], pf[h][:, :])

        @block.tensor
        def _(pe):
            pe.wait_ge(ready, 1)
            for h in range(2):
                ins = nc.tensor.matmul(pf[h][:, :], cb[:, h, :], wT[:, h, :], start=True, stop=True)
            ins.then_inc(made, 1)


def linear_attention(nc, ph, cn, xT, wq, kb, fold, guard, finish, pool_job=None):
    pq, pd, po = ph.ps("pq", [128, 2, P]), ph.ps("pd", [128, 2, P]), ph.ps("po", [P, D])
    low, low_e, q1 = ph.sb("low", [128, 2, P]), ph.sb("low_e", [128, 2, P]), ph.sb("q1", [128, 2, P])
    r0, r1, qn = ph.sb("r0", [128, 2, P]), ph.sb("r1", [128, 2, P]), ph.sb("qn", [128, 2, P])
    q_made, lowered, exped, q_ready = ph.sem("q_made"), ph.sem("lowered"), ph.sem("exped"), ph.sem("q_ready")
    d_made, qn_ready, o_made, finished, steps = (ph.sem("d_made"), ph.sem("qn_ready"), ph.sem("o_made"), ph.sem("finished"),
                                                 ph.sem("la_steps"))
    with nc.Block() as block:
        @block.gpsimd
        def _(pool):
            if pool_job is not None:
                pool_job(pool)

        @block.tensor
        def _(pe):
            pe.sem_inc(finished, 1)

            def q_of(t):
                for h in range(2):
                    for k in range(KC):
                        ins = nc.tensor.matmul(pq[:, h, :], wq[:, k, h * 128:(h + 1) * 128],
                                               xT[:, k, bass.ds(t, 1), :].rearrange("p a f -> p (a f)"), start=(k == 0), stop=(k == KC - 1))
                ins.then_inc(q_made, 1)

            def tile(t, last):
                pe.wait_ge(q_ready, t + 1)
                for h in range(2):
                    ins = nc.tensor.matmul(pd[:, h, :], kb[:, h, :], q1[:, h, :], start=True, stop=True)
                ins.then_inc(d_made, 1)
                if not last:
                    q_of(t + 1)
                pe.wait_ge(qn_ready, t + 1)
                pe.wait_ge(finished, t + 1)
                for h in range(2):
                    ins = nc.tensor.matmul(po[:, :], qn[:, h, :], fold[:, h, :], start=(h == 0), stop=(h == 1))
                ins.then_inc(o_made, 1)
            q_of(0)
            with pe.Fori(0, NT - 1) as t:
                tile(t, False)
            tile(NT - 1, True)

        @block.scalar
        def _(act):
            with act.Fori(0, NT) as t:
                act.wait_ge(lowered, t + 1)
                nc.scalar.activation(low_e[:, :, :], low[:, :, :], ACT.Exp).then_inc(exped, 1)

        @block.vector
        def _(dve):
            def q_of(t):
                dve.wait_ge(q_made, t + 1)
                nc.vector.tensor_scalar(low[:, :, :], pq[:, :, :], 0.0, None, ALU.min).then_inc(lowered, 1)
                dve.wait_ge(exped, t + 1)
                nc.vector.scalar_tensor_tensor(q1[:, :, :], pq[:, :, :], 0.0, low_e[:, :, :], ALU.max, ALU.add).then_inc(q_ready, 1)

            def tile(t, last):
                chain = Chain(dve, steps, t * 2)
                dve.wait_ge(d_made, t + 1)
                dve.wait_ge(q_ready, t + 1)
                chain(nc.vector.tensor_scalar(r0[:, :, :], pd[:, :, :], guard[1], None, guard[0]))
                chain(nc.vector.reciprocal(r1[:, :, :], r0[:, :, :]))
                nc.vector.tensor_tensor(qn[:, :, :], q1[:, :, :], r1[:, :, :], ALU.mult).then_inc(qn_ready, 1)
                if not last:
                    q_of(t + 1)
                dve.wait_ge(o_made, t + 1)
                finish(t, po[:, :]).then_inc(finished, 1)
            q_of(0)
            with dve.Fori(0, NT - 1) as t:
                tile(t, False)
            tile(NT - 1, True)


def load(nc, ph, pairs):
    loaded = ph.sem("weights_loaded")
    with nc.Block() as block:
        @block.sync
        def _(sp):
            for to, src in pairs:
                sp.dma_start(to, src).then_inc(loaded, 16)
            sp.wait_ge(loaded, 16 * len(pairs))


def chunks(w):
    return w.rearrange("(k p) m -> p k m", p=128)


def row(v, parts=P):
    return v.rearrange("(a f) -> a f", a=1).to_broadcast([parts, v.shape[0]])


def layer0(nc, cn, A, x, xT, support_d, pool_jobs):
    with ExitStack() as ctx:
        ph = Phase(nc, ctx, "a1")
        w = ph.sb("w", [128, KC, 3 * D])
        wq, wp = ph.sb("wq", [128, KC, D]), ph.sb("wp", [128, KC, D])
        mean, rstd = ph.sb("mean", [P, NT]), ph.sb("rstd", [P, NT])
        sup, k_sb, v_sb = ph.sb("sup", [P, 2, D]), ph.sb("k", [P, 2, D]), ph.sb("v", [P, 2, D])
        cb, kb, ks, fold = ph.sb("cb", [128, 2, 128]), ph.sb("kb", [128, 2, 128]), ph.sb("ks", [128, 2]), ph.sb("fold", [128, 2, D])
        b0, b1, bias = ph.sb("b0", [P, D]), ph.sb("b1", [P, D]), ph.sb("bias", [P, D])
        kvp = ph.ps("kvp", [128, 258])
        load(nc, ph, [(w[:, :, 0:2 * D], chunks(A["L0_mix_WkvT"])), (w[:, :, 2 * D:3 * D], chunks(A["L0_gnn_weight"])),
                      (wq[:, :, :], chunks(A["L0_mix_WqT"])), (wp[:, :, :], chunks(A["L0_mix_WprojT"])),
                      (b0[:, :], row(A["L0_gnn_bias"])), (b1[:, :], row(A["L0_mix_bproj"])),
                      (x[:, :, :], rows(A["x"]))])
        layer_norm_stats(nc, ph, rstd, mean, x)
        with ExitStack() as inner:
            p2 = Phase(nc, inner, "a2")
            project(nc, p2, cn, x, mean, rstd, xT, w, 3 * D,
                    [(0, D, "elu", lambda t, s: k_sb[:, s, :], None), (D, D, "copy", lambda t, s: v_sb[:, s, :], None),
                     (2 * D, D, "copy", lambda t, s: sup[:, s, :], None)],
                    [(1, lambda t: rows(support_d)[:, bass.ds(t, 1), :].rearrange("p a f -> p (a f)"), lambda s: sup[:, s, :])],
                    kv=(kvp, k_sb, v_sb), pool_job=pool_jobs[0])
        with ExitStack() as inner:
            p3 = Phase(nc, inner, "a3")
            fold_context(nc, p3, cn, kvp, cb, kb, ks, wp, fold)
        with ExitStack() as inner:
            p4 = Phase(nc, inner, "a4")
            gate = p4.sem("bias_ready")
            with nc.Block() as block:
                @block.vector
                def _(dve):
                    nc.vector.tensor_tensor(bias[:, :], b0[:, :], b1[:, :], ALU.add).then_inc(gate, 1)
                    dve.wait_ge(gate, 1)
                    for t in range(NT):
                        nc.vector.tensor_tensor(x[:, t, :], x[:, t, :], bias[:, :], ALU.add)

            def finish(t, psum):
                a = x[:, bass.ds(t, 1), :].rearrange("p a f -> p (a f)")
                return nc.vector.tensor_tensor(a, a, psum, ALU.add)
            linear_attention(nc, p4, cn, xT, wq, kb, fold, (ALU.max, 1e-6), finish, pool_jobs[1])


def spread(ap, axis, shape):
    return ap.unsqueeze(axis).to_broadcast(shape)


def gat_max(nc, ph, cn, so, source, ge, top):
    G, NG, H = 4, 4, 4
    tab = so.tab
    V = 3 * H + 1
    gath, idx = ph.sb("gath", [128, NG, G, 32]), ph.sb("idx", [128, NG, G], I32)
    vals, vT = ph.sb("vals", [128, NG, G, V], BF16), ph.sb("vT", [V, 2, G * 128], BF16)
    pick, ident_b = ph.sb("pick", [V, H + 1, P], BF16), ph.sb("ident_b", [128, 128], BF16)
    mask = ph.sb("mask", [V, H + 1])
    pen, cand, best = ph.sb("pen", [P, G * 128]), ph.sb("cand", [P, H, G * 128]), ph.sb("best", [P, 2, H, G])
    vt = [ph.ps(f"vt{i}", [V, G * 128]) for i in range(2)]
    wide = [ph.ps(f"wide{c}", [P, G * 128]) for c in range(H + 1)]
    gathered = [ph.sem(f"gathered{g}") for g in range(NG)]
    read = [ph.sem(f"read{g}") for g in range(NG)]
    made, freed = [ph.sem(f"made{c}") for c in range(H + 1)], [ph.sem(f"freed{c}") for c in range(H + 1)]
    idx_ready, gate_p, gate_a, steps = ph.sem("idx_ready"), ph.sem("gate_p"), ph.sem("gate_a"), ph.sem("steps")
    vals_ready, turned, vT_ready, picked = ph.sem("vals_ready"), ph.sem("turned"), ph.sem("vT_ready"), ph.sem("picked")
    idx_made = ph.sem("idx_made")
    tabf = tab[:, :, :].bitcast(F32)
    step = NG * G
    rounds = so.tiles // step
    with nc.Block() as block:
        @block.gpsimd
        def _(pool):
            nc.gpsimd.tensor_copy(ident_b[:, :], cn["ident"][:, :]).then_inc(picked, 1)
            nc.gpsimd.tensor_copy(mask[:, H:H + 1], cn["ident"][0:V, V - 1:V]).then_inc(idx_made, 1)
            for c in range(H):
                nc.gpsimd.tensor_tensor(mask[:, c:c + 1], cn["ident"][0:V, c:c + 1], cn["ident"][0:V, H + c:H + c + 1],
                                        ALU.add).then_inc(idx_made, 1)
            pool.wait_ge(idx_made, H + 1)
            for c in range(H):
                nc.gpsimd.tensor_tensor(mask[:, c:c + 1], mask[:, c:c + 1], cn["ident"][0:V, 2 * H + c:2 * H + c + 1],
                                        ALU.add).then_inc(idx_made, 1)
            pool.wait_ge(idx_made, 2 * H + 1)
            for c in range(H + 1):
                nc.gpsimd.tensor_copy(pick[:, c, :], mask[:, c:c + 1].to_broadcast([V, P])).then_inc(picked, 1)
            with pool.Fori(0, rounds) as r:
                for g in range(NG):
                    pool.wait_ge(read[g], r + 1)
                    pool.sem_inc(gate_p, 1)
                    nc.gpsimd.tensor_copy(idx[:, g, :], tab[:, bass.ds(r * step + g * G, G), 0]).then_inc(idx_ready, 1)
                    pool.wait_ge(idx_ready, r * NG + (g + 1))
                    pool.sem_inc(gate_p, 1)
                    for j in range(G):
                        nc.gpsimd.indirect_dma_start(gath[:, g, j, :], None, source,
                                                     bass.IndirectOffsetOnAxis(ap=idx[:, g, j:j + 1], axis=0)
                                                     ).then_inc(gathered[g], 16)

        @block.scalar
        def _(act):
            for g in range(NG):
                act.sem_inc(read[g], 1)
            act.sem_inc(vT_ready, 2)
            with act.Fori(0, rounds) as r:
                def fetch(g):
                    t = bass.ds(r * step + g * G, G)
                    act.wait_ge(gathered[g], r * (16 * G) + 16 * G)
                    act.wait_ge(turned, r * NG + g + 1)
                    act.sem_inc(gate_a, 1)
                    nc.scalar.activation(vals[:, g, :, 0:3 * H], gath[:, g, :, 20:32], ACT.Copy).then_inc(vals_ready, 1)
                    nc.scalar.activation(vals[:, g, :, 3 * H], tabf[:, t, 1], ACT.Copy).then_inc(vals_ready, 1)
                    nc.scalar.activation(ge[:, t, :], gath[:, g, :, 0:20], ACT.Copy).then_inc(read[g], 1)
                for g in range(NG):
                    fetch(g)
                    act.wait_ge(turned, r * NG + g + 2)
                    act.wait_ge(made[0], r * NG + g + 1)
                    nc.scalar.activation(vT[:, g % 2, :], vt[g % 2][:, :], ACT.Copy).then_inc(vT_ready, 1)

        @block.tensor
        def _(pe):
            pe.sem_inc(turned, 1)
            pe.sem_inc(made[0], 1)
            pe.wait_ge(picked, H + 2)

            def turn_group(n, g):
                pe.wait_ge(vals_ready, n * 2 + 2)
                pe.wait_ge(vT_ready, n + 1)
                for j in range(G):
                    ins = nc.tensor.matmul(vt[g % 2][:, j * 128:(j + 1) * 128], vals[:, g, j, :], ident_b[:, :],
                                           start=True, stop=True)
                ins.then_inc(turned, 1)

            def one_round(r, last):
                for g in range(NG):
                    n = r * NG + g
                    if g + 1 < NG or not last:
                        turn_group(n + 1, (g + 1) % NG)
                    pe.wait_ge(vT_ready, n + 3)
                    for c in [H] + list(range(H)):
                        pe.wait_ge(freed[c], n + 1)
                        nc.tensor.matmul(wide[c][:, :], pick[:, c, :], vT[:, g % 2, :], start=True, stop=True).then_inc(made[c], 1)
            turn_group(0, 0)
            with pe.Fori(0, rounds - 1) as r:
                one_round(r, False)
            one_round(rounds - 1, True)

        @block.vector
        def _(dve):
            for c in range(H + 1):
                dve.sem_inc(freed[c], 1)
            per = 1 + 2 * H + G
            dve.sem_inc(steps, G)

            def larger(n, s, numbers, j):
                a = top[:, bass.ds(numbers[j], 1), :].rearrange("p a f -> p (a f)")
                nc.vector.tensor_tensor(a, a, best[:, s, :, j], ALU.max).then_inc(steps, 1)

            def reduce_head(s, c):
                nc.vector.tensor_reduce(best[:, s, c, :], cand[:, c, :].rearrange("p (t e) -> p t e", t=G),
                                        AX.X, ALU.max).then_inc(steps, 1)

            def group(r, g, first):
                n, s = r * NG + g, g % 2
                base = n * per
                if not first:
                    numbers = tile_numbers(nc, "vector", so.tb, r * step + (g - 1) * G, G)
                    dve.wait_ge(steps, base - 2)
                dve.wait_ge(made[H], n + 1)
                nc.vector.tensor_scalar(pen[:, :], wide[H][:, :], cn["part"][0:P, 0:1], FAR,
                                        ALU.not_equal, ALU.mult).then_inc(steps, 1)
                if not first:
                    dve.wait_ge(steps, base)
                    larger(n, 1 - s, numbers, 0)
                dve.wait_ge(steps, base + (G + 1 if first else 1))
                dve.sem_inc(freed[H], 1)
                cand_step, larger_step = (G + 2, G + 3, G + 5, 11) if first else (3, 5, 8, 11), (2, 4, 7, 10)
                for c in range(H):
                    dve.wait_ge(made[c], n + (2 if c == 0 else 1))
                    nc.vector.tensor_tensor(cand[:, c, :], wide[c][:, :], pen[:, :], ALU.add).then_inc(steps, 1)
                    if c:
                        dve.wait_ge(steps, base + cand_step[c - 1])
                        dve.sem_inc(freed[c - 1], 1)
                        reduce_head(s, c - 1)
                    if c + 1 < H and not first:
                        dve.wait_ge(steps, base + larger_step[c])
                        larger(n, 1 - s, numbers, c + 1)
                dve.wait_ge(steps, base + cand_step[H - 1])
                dve.sem_inc(freed[H - 1], 1)
                reduce_head(s, H - 1)

            group(0, 0, True)
            for g in range(1, NG):
                group(0, g, False)
            with dve.Fori(1, rounds) as r:
                for g in range(NG):
                    group(r, g, False)
            numbers = tile_numbers(nc, "vector", so.tb, so.tiles - G, G)
            for j in range(G):
                dve.wait_ge(steps, rounds * NG * per + j)
                larger(0, (NG - 1) % 2, numbers, j)


def gat_spread(nc, ph, cn, so, adm, xp, pool_job):
    G, NG = 4, 4
    hot, hotT = ph.sb("hot", [128, NG, G, P]), ph.sb("hotT", [P, NG, G, 128])
    pt = [ph.ps(f"pt{g}", [P, G, 128]) for g in range(NG)]
    px = [ph.ps(f"px{g}", [128, G, 8]) for g in range(NG)]

    def each(name):
        return [ph.sem(f"{name}{g}") for g in range(NG)]
    hot_ready, turned, hotT_ready, spread_out, kept = (
        each(n) for n in ("hot_ready", "turned", "hotT_ready", "spread_out", "kept"))
    tabf = so.tab[:, :, :].bitcast(F32)
    step = NG * G
    rounds = so.tiles // step
    with nc.Block() as block:
        @block.gpsimd
        def _(pool):
            pool_job(pool)

        @block.vector
        def _(dve):
            for g in range(NG):
                dve.sem_inc(kept[g], 1)
            with dve.Fori(0, rounds) as r:
                for g in range(NG):
                    dve.wait_ge(turned[g], r + 1)
                    for j in range(G):
                        t = bass.ds(r * step + g * G + j, 1)
                        ins = nc.vector.tensor_scalar(hot[:, g, j, :], cn["ramp"][:, 0:P], tabf[:, t, 1], None, ALU.is_equal)
                    ins.then_inc(hot_ready[g], 1)
                for g in range(NG):
                    dve.wait_ge(spread_out[g], r + 2)
                    nc.vector.tensor_scalar(xp[:, bass.ds(r * step + g * G, G), :], px[g][:, :, :], 1.0, None,
                                            ALU.mult).then_inc(kept[g], 1)

        @block.scalar
        def _(act):
            with act.Fori(0, rounds) as r:
                for g in range(NG):
                    act.wait_ge(turned[g], r + 2)
                    act.wait_ge(spread_out[g], r + 1)
                    nc.scalar.activation(hotT[:, g, :, :], pt[g][:, :, :], ACT.Copy).then_inc(hotT_ready[g], 1)

        @block.tensor
        def _(pe):
            for g in range(NG):
                pe.sem_inc(turned[g], 1)
                pe.sem_inc(spread_out[g], 1)
                pe.sem_inc(hotT_ready[g], 1)
            with pe.Fori(0, rounds) as r:
                def turn_group(g):
                    pe.wait_ge(hot_ready[g], r + 1)
                    pe.wait_ge(hotT_ready[g], r + 1)
                    for j in range(G):
                        ins = nc.tensor.matmul(pt[g][:, j, :], hot[:, g, j, :], cn["ident"][:, :], start=True, stop=True)
                    ins.then_inc(turned[g], 1)
                turn_group(0)
                for g in range(NG):
                    if g + 1 < NG:
                        turn_group(g + 1)
                    numbers = tile_numbers(nc, "tensor", so.tb, r * step + g * G, G)
                    pe.wait_ge(hotT_ready[g], r + 2)
                    pe.wait_ge(kept[g], r + 1)
                    for j in range(G):
                        ins = nc.tensor.matmul(px[g][:, j, :], hotT[:, g, j, :],
                                               adm[:, bass.ds(numbers[j], 1), :].rearrange("p a f -> p (a f)"), start=True, stop=True)
                    ins.then_inc(spread_out[g], 1)


def gat_weights(nc, ph, so, ge, xp):
    z0, z1 = ph.sb("z0", [128, so.tiles, 4]), ph.sb("z1", [128, so.tiles, 4])
    steps, ready, exped = ph.sem("steps"), ph.sem("ready"), ph.sem("exped")
    with nc.Block() as block:
        @block.vector
        def _(dve):
            chain = Chain(dve, steps)
            chain(nc.vector.tensor_tensor(z0[:, :, :], xp[:, :, 0:4], ge[:, :, 16:20], ALU.add))
            chain(nc.vector.scalar_tensor_tensor(z1[:, :, :], z0[:, :, :], 0.2, z0[:, :, :], ALU.mult, ALU.max))
            chain(nc.vector.tensor_tensor(z0[:, :, :], z1[:, :, :], xp[:, :, 4:8], ALU.subtract))
            nc.vector.tensor_scalar(z1[:, :, :], z0[:, :, :], 0.0, None, ALU.min).then_inc(ready, 1)
            dve.wait_ge(exped, 1)
            for h in range(4):
                nc.vector.tensor_tensor(ge[:, :, 4 * h:4 * h + 4], ge[:, :, 4 * h:4 * h + 4],
                                        ge[:, :, 16 + h:17 + h].to_broadcast([128, so.tiles, 4]), ALU.mult)

        @block.scalar
        def _(act):
            act.wait_ge(ready, 1)
            nc.scalar.activation(ge[:, :, 16:20], z1[:, :, :], ACT.Exp).then_inc(exped, 1)


def gat_sum(nc, ph, cn, so, ge, num, pool_job):
    G, NG = 4, 4
    hot = ph.sb("hot", [128, NG, G, P])
    pa = [ph.ps(f"pa{g}", [P, G, 20]) for g in range(NG)]
    hot_ready, summed, added = ([ph.sem(f"{n}{g}") for g in range(NG)] for n in ("hot_ready", "summed", "added"))
    steps = ph.sem("steps")
    tabf = so.tab[:, :, :].bitcast(F32)
    step = NG * G
    rounds = so.tiles // step
    with nc.Block() as block:
        @block.gpsimd
        def _(pool):
            pool_job(pool)

        @block.vector
        def _(dve):
            with dve.Fori(0, rounds) as r:
                for g in range(NG):
                    dve.wait_ge(summed[g], r + 1)
                    for j in range(G):
                        t = bass.ds(r * step + g * G + j, 1)
                        ins = nc.vector.tensor_scalar(hot[:, g, j, :], cn["ramp"][:, 0:P], tabf[:, t, 1], None, ALU.is_equal)
                    ins.then_inc(hot_ready[g], 1)
                chain = Chain(dve, steps, r * step)
                for g in range(NG):
                    numbers = tile_numbers(nc, "vector", so.tb, r * step + g * G, G)
                    dve.wait_ge(summed[g], r + 2)
                    for j in range(G):
                        a = num[:, bass.ds(numbers[j], 1), :].rearrange("p a f -> p (a f)")
                        chain(nc.vector.tensor_tensor(a, a, pa[g][:, j, :], ALU.add))

        @block.tensor
        def _(pe):
            for g in range(NG):
                pe.sem_inc(summed[g], 1)
            with pe.Fori(0, rounds) as r:
                for g in range(NG):
                    pe.wait_ge(hot_ready[g], r + 1)
                    for j in range(G):
                        ins = nc.tensor.matmul(pa[g][:, j, :], hot[:, g, j, :], 
                                               ge[:, bass.ds(r * step + g * G + j, 1), :].rearrange("p a f -> p (a f)"), start=True, stop=True)
                    ins.then_inc(summed[g], 1)


def gating(nc, cn, A, x, xT, gates, hs_d, so, pool_jobs):
    with ExitStack() as ctx:
        ph = Phase(nc, ctx, "b1")
        w = ph.sb("w", [128, KC, 16])
        mean, rstd = ph.sb("mean", [P, NT]), ph.sb("rstd", [P, NT])
        h = ph.sb("h", [P, NT, 24])
        att_s, att_d, t16 = ph.sb("att_s", [P, 16]), ph.sb("att_d", [P, 16]), ph.sb("t16", [P, NT, 16])
        u16 = ph.sb("u16", [P, NT, 16])
        top, adm, num = ph.sb("top", [P, NT, 4]), ph.sb("adm", [P, NT, 8]), ph.sb("num", [P, NT, 20])
        ge, xp = ph.sb("ge", [128, so.tiles, 20]), ph.sb("xp", [128, so.tiles, 8])
        bg, lg, lb = ph.sb("bg", [P, 16]), ph.sb("lg", [P, 16]), ph.sb("lb", [P, 16])
        load(nc, ph, [(w[:, :, :], chunks(A["L0_ffn_W_gat"])), (att_s[:, :], row(A["L0_ffn_att_src"])),
                      (att_d[:, :], row(A["L0_ffn_att_dst"])), (bg[:, :], row(A["L0_ffn_b_gat"])),
                      (lg[:, :], row(A["L0_ffn_ln_gamma"])), (lb[:, :], row(A["L0_ffn_ln_beta"]))])
        layer_norm_stats(nc, ph, rstd, mean, x)
        with ExitStack() as inner:
            p2 = Phase(nc, inner, "b2")
            project(nc, p2, cn, x, mean, rstd, xT, w, 16,
                    [(0, 16, "copy", lambda t, s: h[:, bass.ds(t, 1), 0:16].rearrange("p a f -> p (a f)"), None)], [])
        with ExitStack() as inner:
            p3 = Phase(nc, inner, "b3")
            steps, ready, stored = p3.sem("steps"), p3.sem("ready"), p3.sem("stored")
            sent, rest, part = p3.sb("sent", [P, NT, 32]), p3.sb("rest", [P, NT, 4]), p3.sb("part", [P, NT, 4], BF16)
            with nc.Block() as block:
                @block.vector
                def _(dve):
                    chain = Chain(dve, steps)
                    for att, c in ((att_s, 16), (att_d, 20)):
                        chain(nc.vector.tensor_tensor(t16[:, :, :], h[:, :, 0:16], spread(att[:, :], 1, [P, NT, 16]), ALU.mult))
                        chain(nc.vector.tensor_reduce(h[:, :, c:c + 4], t16[:, :, :].rearrange("p t (h e) -> p t h e", h=4),
                                                      AX.X, ALU.add))
                    chain(nc.vector.tensor_copy(rest[:, :, :], h[:, :, 16:20]))
                    for i in range(3):
                        chain(nc.vector.tensor_copy(part[:, :, :], rest[:, :, :]))
                        chain(nc.vector.tensor_copy(sent[:, :, 20 + 4 * i:24 + 4 * i], part[:, :, :]))
                        chain(nc.vector.tensor_tensor(rest[:, :, :], rest[:, :, :], sent[:, :, 20 + 4 * i:24 + 4 * i], ALU.subtract))
                    chain(nc.vector.tensor_copy(sent[:, :, 0:20], h[:, :, 0:20]))
                    dve.sem_inc(ready, 1)
                    nc.vector.tensor_copy(top[:, :, :], h[:, :, 16:20])

                @block.sync
                def _(sp):
                    sp.wait_ge(ready, 1)
                    sp.dma_start(rows(hs_d), sent[:, :, :]).then_inc(stored, 16)
                    sp.wait_ge(stored, 16)
        with ExitStack() as inner:
            p5 = Phase(nc, inner, "bm")
            gat_max(nc, p5, cn, so, hs_d, ge, top)
        with ExitStack() as inner:
            p6 = Phase(nc, inner, "b6")
            steps, ready, exped = p6.sem("steps"), p6.sem("ready"), p6.sem("exped")
            e0, e1 = p6.sb("e0", [P, NT, 4]), p6.sb("e1", [P, NT, 4])
            with nc.Block() as block:
                @block.vector
                def _(dve):
                    chain = Chain(dve, steps)
                    chain(nc.vector.tensor_copy(adm[:, :, 0:4], h[:, :, 20:24]))
                    chain(nc.vector.tensor_tensor(e0[:, :, :], top[:, :, :], h[:, :, 20:24], ALU.add))
                    chain(nc.vector.scalar_tensor_tensor(adm[:, :, 4:8], e0[:, :, :], 0.2, e0[:, :, :], ALU.mult, ALU.max))
                    chain(nc.vector.tensor_tensor(e0[:, :, :], h[:, :, 16:20], h[:, :, 20:24], ALU.add))
                    chain(nc.vector.scalar_tensor_tensor(e1[:, :, :], e0[:, :, :], 0.2, e0[:, :, :], ALU.mult, ALU.max))
                    nc.vector.tensor_tensor(e0[:, :, :], e1[:, :, :], adm[:, :, 4:8], ALU.subtract).then_inc(ready, 1)
                    dve.wait_ge(exped, 1)
                    for hd in range(4):
                        nc.vector.tensor_tensor(num[:, :, 4 * hd:4 * hd + 4], h[:, :, 4 * hd:4 * hd + 4],
                                                num[:, :, 16 + hd:17 + hd].to_broadcast([P, NT, 4]), ALU.mult)

                @block.scalar
                def _(act):
                    act.wait_ge(ready, 1)
                    nc.scalar.activation(num[:, :, 16:20], e0[:, :, :], ACT.Exp).then_inc(exped, 1)
        with ExitStack() as inner:
            gat_spread(nc, Phase(nc, inner, "bx"), cn, so, adm, xp, pool_jobs[0])
        with ExitStack() as inner:
            gat_weights(nc, Phase(nc, inner, "bw"), so, ge, xp)
        with ExitStack() as inner:
            gat_sum(nc, Phase(nc, inner, "bs"), cn, so, ge, num, pool_jobs[1])
        with ExitStack() as inner:
            p8 = Phase(nc, inner, "b8")
            steps, ready, rooted, gap, exped = p8.sem("steps"), p8.sem("ready"), p8.sem("rooted"), p8.sem("gap"), p8.sem("exped")
            den, rden, m, v, sd, rs = (p8.sb(n, [P, NT, 4]) for n in ("den", "rden", "m", "v", "sd", "rs"))
            s, s2, eq, far, sel1, sel2 = (p8.sb(n, [P, NT, 4]) for n in ("s", "s2", "eq", "far", "sel1", "sel2"))
            m1, m2, first, dq, q, w1, w2 = (p8.sb(n, [P, NT]) for n in ("m1", "m2", "first", "dq", "q", "w1", "w2"))

            def all4(a):
                return spread(a[:, :], 2, [P, NT, 4])

            def all16(a):
                return spread(a, 2, [P, NT, 16])
            expert = spread(cn["ramp"][0:P, 0:4], 1, [P, NT, 4])
            with nc.Block() as block:
                @block.vector
                def _(dve):
                    chain = Chain(dve, steps)
                    chain(nc.vector.tensor_scalar(den[:, :, :], num[:, :, 16:20], 1e-16, None, ALU.add))
                    chain(nc.vector.reciprocal(rden[:, :, :], den[:, :, :]))
                    for hd in range(4):
                        chain(nc.vector.tensor_tensor(t16[:, :, 4 * hd:4 * hd + 4], num[:, :, 4 * hd:4 * hd + 4],
                                                      rden[:, :, hd:hd + 1].to_broadcast([P, NT, 4]), ALU.mult))
                    chain(nc.vector.tensor_tensor(t16[:, :, :], t16[:, :, :], spread(bg[:, :], 1, [P, NT, 16]), ALU.add))
                    chain(nc.vector.tensor_reduce(m[:, :, 0], t16[:, :, :], AX.X, ALU.add))
                    chain(nc.vector.tensor_scalar(m[:, :, 1], m[:, :, 0], 1.0 / 16, None, ALU.mult))
                    chain(nc.vector.tensor_tensor(t16[:, :, :], t16[:, :, :], all16(m[:, :, 1]), ALU.subtract))
                    chain(nc.vector.tensor_tensor(u16[:, :, :], t16[:, :, :], t16[:, :, :], ALU.mult))
                    chain(nc.vector.tensor_reduce(v[:, :, 0], u16[:, :, :], AX.X, ALU.add))
                    nc.vector.tensor_scalar(v[:, :, 1], v[:, :, 0], 1.0 / 16, EPS, ALU.mult, ALU.add).then_inc(ready, 1)
                    dve.wait_ge(rooted, 1)
                    chain(nc.vector.reciprocal(rs[:, :, 0], sd[:, :, 0]))
                    chain(nc.vector.tensor_tensor(t16[:, :, :], t16[:, :, :], all16(rs[:, :, 0]), ALU.mult))
                    chain(nc.vector.tensor_tensor(t16[:, :, :], t16[:, :, :], spread(lg[:, :], 1, [P, NT, 16]), ALU.mult))
                    chain(nc.vector.tensor_tensor(t16[:, :, :], t16[:, :, :], spread(lb[:, :], 1, [P, NT, 16]), ALU.add))
                    chain(nc.vector.tensor_reduce(s[:, :, :], t16[:, :, :].rearrange("p t (h e) -> p t e h", h=4), AX.X, ALU.add))
                    chain(nc.vector.tensor_scalar(s[:, :, :], s[:, :, :], 0.25, None, ALU.mult))

                    def choose(score, best, sel):
                        chain(nc.vector.tensor_reduce(best[:, :], score[:, :, :], AX.X, ALU.max))
                        chain(nc.vector.tensor_tensor(eq[:, :, :], score[:, :, :], all4(best), ALU.not_equal))
                        chain(nc.vector.scalar_tensor_tensor(far[:, :, :], eq[:, :, :], 100.0, expert, ALU.mult, ALU.add))
                        chain(nc.vector.tensor_reduce(first[:, :], far[:, :, :], AX.X, ALU.min))
                        chain(nc.vector.tensor_tensor(sel[:, :, :], expert, all4(first), ALU.is_equal))
                    choose(s, m1, sel1)
                    chain(nc.vector.scalar_tensor_tensor(s2[:, :, :], sel1[:, :, :], FAR, s[:, :, :], ALU.mult, ALU.add))
                    choose(s2, m2, sel2)
                    nc.vector.tensor_tensor(dq[:, :], m2[:, :], m1[:, :], ALU.subtract).then_inc(gap, 1)
                    dve.wait_ge(exped, 1)
                    chain(nc.vector.tensor_scalar(w2[:, :], q[:, :], 1.0, None, ALU.add))
                    chain(nc.vector.reciprocal(w1[:, :], w2[:, :]))
                    chain(nc.vector.tensor_tensor(w2[:, :], q[:, :], w1[:, :], ALU.mult))
                    chain(nc.vector.tensor_tensor(sel1[:, :, :], sel1[:, :, :], all4(w1), ALU.mult))
                    chain(nc.vector.tensor_tensor(sel2[:, :, :], sel2[:, :, :], all4(w2), ALU.mult))
                    chain(nc.vector.tensor_tensor(gates[:, :, :], sel1[:, :, :], sel2[:, :, :], ALU.add))

                @block.scalar
                def _(act):
                    act.wait_ge(ready, 1)
                    nc.scalar.activation(sd[:, :, 0], v[:, :, 1], ACT.Sqrt).then_inc(rooted, 1)
                    act.wait_ge(gap, 1)
                    nc.scalar.activation(q[:, :], dq[:, :], ACT.Exp).then_inc(exped, 1)


def experts0(nc, cn, A, x, xT, gates, pool_job):
    M = HID0 // 128
    with ExitStack() as ctx:
        ph = Phase(nc, ctx, "e0")
        w1, w2 = ph.sb("w1", [128, N_EXP0, KC, HID0]), ph.sb("w2", [128, N_EXP0, M, D])
        b1, b2 = ph.sb("b1", [128, N_EXP0, M]), ph.sb("b2", [P, N_EXP0, D])
        hT, tmp = ph.sb("hT", [128, 2, M, P]), ph.sb("tmp", [P, D])
        load(nc, ph, [(w1[:, e, :, :], chunks(A["L0_ffn_W1"][e, :, :])) for e in range(N_EXP0)]
             + [(w2[:, e, :, :], chunks(A["L0_ffn_W2"][e, :, :])) for e in range(N_EXP0)]
             + [(b1[:, :, :], A["L0_ffn_b1"].rearrange("p (e m) -> p e m", e=N_EXP0)),
                (b2[:, :, :].rearrange("p e f -> p (e f)"), row(A["L0_ffn_b2"]))])
        hid = [ph.ps(f"hid{i}", [128, M, P]) for i in range(2)]
        y = [ph.ps(f"y{i}", [P, 512]) for i in range(2)]
        h_made, gelued, y_made, added, steps = (ph.sem(n) for n in ("h_made", "gelued", "y_made", "added", "steps"))
        with nc.Block() as block:
            @block.gpsimd
            def _(pool):
                pool_job(pool)

            @block.tensor
            def _(pe):
                pe.sem_inc(y_made, 2)
                with pe.Fori(0, NT) as t:
                    def hidden(e):
                        s = t * N_EXP0 + e
                        pe.wait_ge(gelued, s + 1)
                        for m in range(M):
                            for k in range(KC):
                                ins = nc.tensor.matmul(hid[e % 2][:, m, :], w1[:, e, k, m * 128:(m + 1) * 128],
                                                       xT[:, k, bass.ds(t, 1), :].rearrange("p a f -> p (a f)"),
                                                       start=(k == 0), stop=(k == KC - 1))
                        ins.then_inc(h_made, 1)
                    hidden(0)
                    for e in range(N_EXP0):
                        if e + 1 < N_EXP0:
                            hidden(e + 1)
                        s = t * N_EXP0 + e
                        pe.wait_ge(gelued, s + 3)
                        pe.wait_ge(added, s + 1)
                        for m in range(M):
                            ins = nc.tensor.matmul(y[e % 2][:, 0:D], hT[:, e % 2, m, :], w2[:, e, m, :], start=(m == 0), stop=(m == M - 1))
                        ins.then_inc(y_made, 1)

            @block.scalar
            def _(act):
                act.sem_inc(gelued, 2)
                with act.Fori(0, NT) as t:
                    for e in range(N_EXP0):
                        s = t * N_EXP0 + e
                        act.wait_ge(h_made, s + 1)
                        act.wait_ge(y_made, s + 1)
                        for m in range(M):
                            ins = nc.scalar.activation(hT[:, e % 2, m, :], hid[e % 2][:, m, :], ACT.Gelu, bias=b1[:, e, m:m + 1])
                        ins.then_inc(gelued, 1)

            @block.vector
            def _(dve):
                dve.sem_inc(added, 2)
                with dve.Fori(0, NT) as t:
                    a = x[:, bass.ds(t, 1), :].rearrange("p a f -> p (a f)")
                    chain = Chain(dve, steps, t * (2 * N_EXP0))
                    for e in range(N_EXP0):
                        dve.wait_ge(y_made, t * N_EXP0 + e + 3)
                        chain(nc.vector.tensor_tensor(tmp[:, :], y[e % 2][:, 0:D], b2[:, e, :], ALU.add))
                        dve.sem_inc(added, 1)
                        chain(nc.vector.scalar_tensor_tensor(a, tmp[:, :], gates[:, bass.ds(t, 1), e], a, ALU.mult, ALU.add))


def mix1(nc, cn, A, x, xT, kvp, mean, rstd):
    H1 = 2 * D
    with ExitStack() as ctx:
        ph = Phase(nc, ctx, "m1")
        wq, wm = ph.sb("wq", [128, KC, D]), ph.sb("wm", [128, KC, D])
        w1, w2 = ph.sb("w1", [128, 2 * KC, H1]), ph.sb("w2", [128, 2 * KC, D])
        g1, b1, g2, b2 = (ph.sb(n, [P, D]) for n in ("g1", "b1", "g2", "b2"))
        cb, kb, ks, fold = ph.sb("cb", [128, 2, 128]), ph.sb("kb", [128, 2, 128]), ph.sb("ks", [128, 2]), ph.sb("fold", [128, 2, D])
        msg = ph.sb("msg", [P, NT, D])
        load(nc, ph, [(wq[:, :, :], chunks(A["L1_mix_Wq"])), (wm[:, :, :], chunks(A["L1_mix_Wm"])),
                      (w1[:, :, :], chunks(A["L1_mix_W1"])), (w2[:, :, :], chunks(A["L1_mix_W2"])),
                      (g1[:, :], row(A["L1_mix_g1"])), (b1[:, :], row(A["L1_mix_b1"])),
                      (g2[:, :], row(A["L1_mix_g2"])), (b2[:, :], row(A["L1_mix_b2"]))])

        def tile_of(a, t):
            return a[:, bass.ds(t, 1), :].rearrange("p a f -> p (a f)")
        with ExitStack() as inner:
            p2 = Phase(nc, inner, "m2")
            fold_context(nc, p2, cn, kvp, cb, kb, ks, wm, fold)
        with ExitStack() as inner:
            p3 = Phase(nc, inner, "m3")
            linear_attention(nc, p3, cn, xT, wq, kb, fold, (ALU.add, 1e-6),
                             lambda t, psum: nc.vector.tensor_scalar(tile_of(msg, t), psum, 1.0, None, ALU.mult))
        with ExitStack() as inner:
            p4 = Phase(nc, inner, "m4")
            mm, mr = p4.sb("mm", [P, NT]), p4.sb("mr", [P, NT])
            layer_norm_stats(nc, p4, mr, mm, msg)
            ma, mc, mn = p4.sb("ma", [P, D]), p4.sb("mc", [P, D]), p4.sb("mn", [P, D])
            mT, hr = p4.sb("mT", [128, KC, P]), p4.sb("hr", [128, 4, P])
            pt, hid, po = p4.ps("pt", [128, KC, P]), p4.ps("hid", [128, 4, P]), p4.ps("po", [P, 512])
            mn_ready, turned, mT_ready, h_made, relued, o_made, kept, steps = (
                p4.sem(n) for n in ("mn_ready", "turned", "mT_ready", "h_made", "relued", "o_made", "kept", "steps"))
            with nc.Block() as block:
                @block.vector
                def _(dve):
                    dve.sem_inc(kept, 1)

                    def norm(t):
                        chain = Chain(dve, steps, t * 2)
                        dve.wait_ge(turned, t + 1)
                        chain(nc.vector.tensor_scalar(ma[:, :], tile_of(msg, t), mm[:, bass.ds(t, 1)], mr[:, bass.ds(t, 1)],
                                                      ALU.subtract, ALU.mult))
                        chain(nc.vector.tensor_tensor(mc[:, :], ma[:, :], g1[:, :], ALU.mult))
                        nc.vector.tensor_tensor(mn[:, :], mc[:, :], b1[:, :], ALU.add).then_inc(mn_ready, 1)

                    def keep(t):
                        dve.wait_ge(o_made, t + 1)
                        nc.vector.tensor_scalar(tile_of(msg, t), po[:, 0:D], 1.0, None, ALU.mult).then_inc(kept, 1)
                    norm(0)
                    with dve.Fori(0, NT - 1) as t:
                        norm(t + 1)
                        keep(t)
                    keep(NT - 1)

                @block.scalar
                def _(act):
                    def fetch(t):
                        act.wait_ge(turned, t + 2)
                        nc.scalar.activation(mT[:, :, :], pt[:, :, :], ACT.Copy).then_inc(mT_ready, 1)

                    def relu(t):
                        act.wait_ge(h_made, t + 1)
                        nc.scalar.activation(hr[:, :, :], hid[:, :, :], ACT.Relu).then_inc(relued, 1)
                    fetch(0)
                    with act.Fori(0, NT - 1) as t:
                        relu(t)
                        fetch(t + 1)
                    relu(NT - 1)

                @block.tensor
                def _(pe):
                    pe.sem_inc(turned, 1)

                    def turn_tile(t):
                        pe.wait_ge(mn_ready, t + 1)
                        for k in range(KC):
                            ins = nc.tensor.matmul(pt[:, k, :], mn[:, k * 128:(k + 1) * 128], cn["ident"][0:P, 0:P], start=True, stop=True)
                        ins.then_inc(turned, 1)

                    def tile(t, last):
                        pe.wait_ge(mT_ready, t + 1)
                        for m in range(4):
                            for k in range(2 * KC):
                                src = (xT[:, k, bass.ds(t, 1), :].rearrange("p a f -> p (a f)") if k < KC else mT[:, k - KC, :])
                                ins = nc.tensor.matmul(hid[:, m, :], w1[:, k, m * 128:(m + 1) * 128], src,
                                                       start=(k == 0), stop=(k == 2 * KC - 1))
                        ins.then_inc(h_made, 1)
                        if not last:
                            turn_tile(t + 1)
                        pe.wait_ge(relued, t + 1)
                        pe.wait_ge(kept, t + 1)
                        for m in range(4):
                            ins = nc.tensor.matmul(po[:, 0:D], hr[:, m, :], w2[:, m, :], start=(m == 0), stop=(m == 3))
                        ins.then_inc(o_made, 1)
                    turn_tile(0)
                    with pe.Fori(0, NT - 1) as t:
                        tile(t, False)
                    tile(NT - 1, True)
        with ExitStack() as inner:
            p5 = Phase(nc, inner, "m5")
            mm, mr = p5.sb("mm", [P, NT]), p5.sb("mr", [P, NT])
            layer_norm_stats(nc, p5, mr, mm, msg)
            ma, mc, xn = p5.sb("ma", [P, D]), p5.sb("mc", [P, D]), p5.sb("xn", [P, D])
            steps = p5.sem("steps")
            with nc.Block() as block:
                @block.vector
                def _(dve):
                    per = 7
                    with dve.Fori(0, NT) as t:
                        chain = Chain(dve, steps, t * per)
                        a = tile_of(x, t)
                        chain(nc.vector.tensor_scalar(ma[:, :], tile_of(msg, t), mm[:, bass.ds(t, 1)], mr[:, bass.ds(t, 1)],
                                                      ALU.subtract, ALU.mult))
                        chain(nc.vector.tensor_tensor(mc[:, :], ma[:, :], g2[:, :], ALU.mult))
                        chain(nc.vector.tensor_tensor(ma[:, :], mc[:, :], b2[:, :], ALU.add))
                        chain(nc.vector.tensor_scalar(xn[:, :], a, mean[:, bass.ds(t, 1)], rstd[:, bass.ds(t, 1)],
                                                      ALU.subtract, ALU.mult))
                        chain(nc.vector.tensor_tensor(a, a, xn[:, :], ALU.add))
                        chain(nc.vector.tensor_tensor(a, a, ma[:, :], ALU.add))
                        chain.n += 1
                        dve.sem_inc(steps, 1)


def relation_attention(nc, ph, A, sT, o_d):
    R, H, W3 = N_REL, 4, 3 * D
    HR = R // 2
    w, bias = ph.sb("w", [128, KC, W3]), ph.sb("bias", [P, W3])
    load(nc, ph, [(w[:, :, :], chunks(A["L1_gnn_in_proj_wT"])), (bias[:, :], row(A["L1_gnn_in_proj_b"]))])
    sc_T = ph.sb("sc_T", [128, R, 2, P])
    q, k, v = ph.sb("q", [P, R, D]), ph.sb("k", [P, R, D]), ph.sb("v", [P, R, D])
    prod, prod_p = ph.sb("prod", [P, HR, D]), ph.sb("prod_p", [P, HR, D])
    sc, ex = ph.sb("sc", [P, H, R, R]), ph.sb("ex", [P, H, R, R])
    mx, sm, rs = ph.sb("mx", [P, H * R]), ph.sb("sm", [P, H * R]), ph.sb("rs", [P, H * R])
    pm, o = ph.sb("pm", [P, H, R]), ph.sb("o", [P, 2, D])
    pk, pq, pv = ([ph.ps(f"p{n}{i}", [P, 2, D]) for i in range(c)] for n, c in (("k", 3), ("q", 3), ("v", 2)))
    fetched, k_made, q_made, v_made, k_kept, q_kept, v_kept = (
        ph.sem(n) for n in ("fetched", "k_made", "q_made", "v_made", "k_kept", "q_kept", "v_kept"))
    shifted, exped, o_ready, stored, steps, gate = (
        ph.sem(n) for n in ("shifted", "exped", "o_ready", "stored", "steps", "gate"))
    p_ready, p_read, v_used = ph.sem("p_ready"), ph.sem("p_read"), ph.sem("v_used")
    units = [(r, s) for r in range(R) for s in range(2)]
    own, pools = units[0::2], units[1::2]

    def product(eng, to, u):
        r, s = u
        return eng.tensor_tensor(to[:, :, :], k[:, s * HR:(s + 1) * HR, :], spread(q[:, r, :], 1, [P, HR, D]), ALU.mult)

    def score(src, u):
        r, s = u
        return nc.vector.tensor_reduce(sc[:, :, r, s * HR:(s + 1) * HR].rearrange("p h s -> p s h"),
                                       src[:, :, :].rearrange("p s (h d) -> p s h d", h=H), AX.X, ALU.add)

    with nc.Block() as block:
        @block.gpsimd
        def _(pool):
            with pool.Fori(0, NT) as t:
                pool.wait_ge(q_kept, t + 2)
                for i, u in enumerate(pools):
                    pool.wait_ge(p_read, t * len(pools) + i + 1)
                    product(nc.gpsimd, prod_p, u).then_inc(p_ready, 1)

        @block.tensor
        def _(pe):
            pe.sem_inc(v_made, 1)
            with pe.Fori(0, NT) as t:
                pe.wait_ge(fetched, t + 1)
                for banks, col, made, kept in ((pk, D, k_made, k_kept), (pq, 0, q_made, q_kept)):
                    pe.wait_ge(kept, t + 1)
                    for r in range(R):
                        for c in range(KC):
                            ins = nc.tensor.matmul(banks[r // 2][:, r % 2, :], sc_T[:, r, c, :], w[:, c, col:col + D],
                                                   start=(c == 0), stop=(c == KC - 1))
                    ins.then_inc(made, 1)
                for i in range(3):
                    pe.wait_ge(v_kept, t * 3 + i + 1)
                    for r in (2 * i, 2 * i + 1):
                        for c in range(KC):
                            ins = nc.tensor.matmul(pv[i % 2][:, r % 2, :], sc_T[:, r, c, :], w[:, c, 2 * D:W3],
                                                   start=(c == 0), stop=(c == KC - 1))
                    ins.then_inc(v_made, 1)

        @block.scalar
        def _(act):
            act.sem_inc(v_kept, 2)

            def fetch(t):
                act.wait_ge(v_made, t * 3 + 1)
                act.sem_inc(gate, 1)
                nc.scalar.activation(sc_T[:, :, :, :].rearrange("p r h f -> p r (h f)"), sT[:, bass.ds(t * R, R), :],
                                     ACT.Copy).then_inc(fetched, 1)

            def tile(t, last):
                act.wait_ge(v_used, t + 1)
                for i in range(3):
                    act.wait_ge(v_made, t * 3 + i + 2)
                    nc.scalar.activation(v[:, 2 * i:2 * i + 2, :], pv[i % 2][:, :, :], ACT.Copy).then_inc(v_kept, 1)
                if not last:
                    fetch(t + 1)
                act.wait_ge(shifted, t + 1)
                nc.scalar.activation(ex[:, :, :, :], sc[:, :, :, :], ACT.Exp, scale=float(D // H) ** -0.5).then_inc(exped, 1)
            fetch(0)
            with act.Fori(0, NT - 1) as t:
                tile(t, False)
            tile(NT - 1, True)

        @block.vector
        def _(dve):
            dve.sem_inc(k_kept, 1)
            dve.sem_inc(q_kept, 1)
            dve.sem_inc(v_used, 1)
            dve.sem_inc(p_read, 1)
            per = 2 * len(own) + len(pools) + 13
            with dve.Fori(0, NT) as t:
                chain = Chain(dve, steps, t * per)
                for banks, col, to, made, kept in ((pk, D, k, k_made, k_kept), (pq, 0, q, q_made, q_kept)):
                    dve.wait_ge(made, t + 1)
                    for i in range(3):
                        ins = nc.vector.tensor_tensor(to[:, 2 * i:2 * i + 2, :], banks[i][:, :, :],
                                                      spread(bias[:, col:col + D], 1, [P, 2, D]), ALU.add)
                    chain(ins)
                    dve.sem_inc(kept, 1)
                for i, u in enumerate(own):
                    chain(product(nc.vector, prod, u))
                    chain(score(prod, u))
                    dve.wait_ge(p_ready, t * len(pools) + i + 1)
                    chain(score(prod_p, pools[i]))
                    dve.sem_inc(p_read, 1)
                flat = sc[:, :, :, :].rearrange("p h r s -> p (h r) s")
                eflat = ex[:, :, :, :].rearrange("p h r s -> p (h r) s")
                chain(nc.vector.tensor_reduce(mx[:, :], flat, AX.X, ALU.max))
                nc.vector.tensor_tensor(flat, flat, spread(mx[:, :], 2, [P, H * R, R]), ALU.subtract).then_inc(shifted, 1)
                dve.wait_ge(exped, t + 1)
                chain(nc.vector.tensor_reduce(sm[:, :], eflat, AX.X, ALU.add))
                chain(nc.vector.reciprocal(rs[:, :], sm[:, :]))
                chain(nc.vector.tensor_tensor(eflat, eflat, spread(rs[:, :], 2, [P, H * R, R]), ALU.mult))
                chain(nc.vector.tensor_reduce(pm[:, :, :], ex[:, :, :, :].rearrange("p h r s -> p h s r"), AX.X, ALU.add))
                chain(nc.vector.tensor_scalar(pm[:, :, :], pm[:, :, :], 1.0 / R, None, ALU.mult))
                dve.wait_ge(v_kept, t * 3 + 5)
                dve.wait_ge(stored, t * 16 + 16)
                for s in range(2):
                    src = slice(s * HR, (s + 1) * HR)
                    chain(nc.vector.tensor_tensor(prod[:, :, :].rearrange("p s (h d) -> p s h d", h=H),
                                                  v[:, src, :].rearrange("p s (h d) -> p s h d", h=H),
                                                  spread(pm[:, :, src].rearrange("p h s -> p s h"), 3, [P, HR, H, D // H]), ALU.mult))
                    if s == 1:
                        dve.sem_inc(v_used, 1)
                    chain(nc.vector.tensor_reduce(o[:, s, :], prod[:, :, :].rearrange("p s f -> p f s"), AX.X, ALU.add))
                nc.vector.tensor_tensor(o[:, 0, :], o[:, 0, :], o[:, 1, :], ALU.add).then_inc(steps, 1)
                chain.n += 1
                dve.wait_ge(steps, t * per + chain.n)
                nc.vector.tensor_tensor(o[:, 0, :], o[:, 0, :], bias[:, 2 * D:W3], ALU.add).then_inc(o_ready, 1)
                assert chain.n == per, chain.n

        @block.sync
        def _(sp):
            sp.sem_inc(stored, 16)
            with sp.Fori(0, NT) as t:
                sp.wait_ge(o_ready, t + 1)
                sp.dma_start(rows(o_d)[:, bass.ds(t, 1), :].rearrange("p a f -> p (a f)"), o[:, 0, :]).then_inc(stored, 16)
            sp.wait_ge(stored, 16 * NT + 16)


def relation_output(nc, ph, cn, A, x, xT, o_d):
    wo, wp = ph.sb("wo", [128, KC, D]), ph.sb("wp", [128, KC, D])
    ab, pb = ph.sb("ab", [128, KC]), ph.sb("pb", [P, D])
    load(nc, ph, [(wo[:, :, :], chunks(A["L1_gnn_attn_out_wT"])), (wp[:, :, :], chunks(A["L1_gnn_proj_wT"])),
                  (ab[:, :], A["L1_gnn_attn_out_b"]), (pb[:, :], row(A["L1_gnn_proj_b"]))])
    o_all = ph.sb("o_all", [P, NT, D])
    oc, oT, sT = ph.sb("oc", [P, D]), ph.sb("oT", [128, KC, P]), ph.sb("sT", [128, KC, P])
    pt, pa, po = ph.ps("pt", [128, KC, P]), ph.ps("pa", [128, KC, P]), ph.ps("po", [P, 512])
    cut, turned, oT_ready, a_made, sT_ready, o_made, added, steps, gate = (
        ph.sem(n) for n in ("cut", "turned", "oT_ready", "a_made", "sT_ready", "o_made", "added", "steps", "gate"))
    loaded = ph.sem("loaded")
    with nc.Block() as block:
        @block.sync
        def _(sp):
            sp.dma_start(o_all[:, :, :], rows(o_d)).then_inc(loaded, 16)

        @block.gpsimd
        def _(pool):
            pool.wait_ge(loaded, 16)
            with pool.Fori(0, NT) as t:
                pool.wait_ge(turned, t + 1)
                pool.sem_inc(gate, 1)
                nc.gpsimd.tensor_copy(oc[:, :], o_all[:, bass.ds(t, 1), :].rearrange("p a f -> p (a f)")).then_inc(cut, 1)

        @block.tensor
        def _(pe):
            pe.sem_inc(turned, 1)
            pe.sem_inc(added, 1)

            def turn_tile(t):
                pe.wait_ge(cut, t + 1)
                for k in range(KC):
                    ins = nc.tensor.matmul(pt[:, k, :], oc[:, k * 128:(k + 1) * 128], cn["ident"][0:P, 0:P], start=True, stop=True)
                ins.then_inc(turned, 1)

            def tile(t, last):
                pe.wait_ge(oT_ready, t + 1)
                for h in range(2):
                    for k in range(KC):
                        ins = nc.tensor.matmul(pa[:, h, :], wo[:, k, h * 128:(h + 1) * 128], oT[:, k, :], start=(k == 0), stop=(k == KC - 1))
                ins.then_inc(a_made, 1)
                if not last:
                    turn_tile(t + 1)
                pe.wait_ge(sT_ready, t + 1)
                pe.wait_ge(added, t + 1)
                for k in range(KC):
                    ins = nc.tensor.matmul(po[:, 0:D], sT[:, k, :], wp[:, k, :], start=(k == 0), stop=(k == KC - 1))
                ins.then_inc(o_made, 1)
            turn_tile(0)
            with pe.Fori(0, NT - 1) as t:
                tile(t, False)
            tile(NT - 1, True)

        @block.scalar
        def _(act):
            act.sem_inc(a_made, 1)
            with act.Fori(0, NT) as t:
                act.wait_ge(turned, t + 2)
                act.wait_ge(a_made, t + 1)
                nc.scalar.activation(oT[:, :, :], pt[:, :, :], ACT.Copy).then_inc(oT_ready, 1)

        @block.vector
        def _(dve):
            with dve.Fori(0, NT) as t:
                chain = Chain(dve, steps, t * 1)
                a = x[:, bass.ds(t, 1), :].rearrange("p a f -> p (a f)")
                nc.vector.tensor_tensor(a, a, pb[:, :], ALU.add).then_inc(steps, 1)
                dve.wait_ge(a_made, t + 2)
                for h in range(KC):
                    ins = nc.vector.scalar_tensor_tensor(sT[:, h, :], pa[:, h, :], ab[:, h:h + 1],
                                                         xT[:, h, bass.ds(t, 1), :].rearrange("p a f -> p (a f)"), ALU.add, ALU.add)
                ins.then_inc(sT_ready, 1)
                dve.wait_ge(steps, t + 1)
                dve.wait_ge(o_made, t + 1)
                nc.vector.tensor_tensor(a, a, po[:, 0:D], ALU.add).then_inc(added, 1)


def in_pairs(eng, count, do):
    with eng.Fori(0, count // 2) as i:
        for s in range(2):
            do(i * 2 + s, s, i)
    if count % 2:
        do(count - 1, 0, count // 2)


class Hidden:

    def __init__(self, nc, ph, cn, w1, b1, n, tiles):
        self.nc, self.cn, self.w1, self.b1, self.n, self.tiles = nc, cn, w1, b1, n, tiles
        self.M = HID1 // 128
        self.rows, self.rT = ph.sb("rows", [n, 2, D]), ph.sb("rT", [128, KC, n])
        self.hT = ph.sb("hT", [128, 2, self.M, n])
        self.pt = ph.ps("pt", [128, KC, n])
        self.hid = [[ph.ps(f"hid{s}{i}", [128, self.M // 2, n]) for i in range(2)] for s in range(2)]
        self.turned, self.rT_ready, self.h_made, self.gelued, self.h_used = (
            ph.sem(k) for k in ("turned", "rT_ready", "h_made", "gelued", "h_used"))

    def tensor(self, pe, wait_rows, use):
        nc, n, M = self.nc, self.n, self.M

        def turn(t, s, i):
            wait_rows(t, s, i)
            for k in range(KC):
                ins = nc.tensor.matmul(self.pt[:, k, :], self.rows[:, s, k * 128:(k + 1) * 128], self.cn["ident"][0:n, 0:n],
                                       start=True, stop=True)
            ins.then_inc(self.turned, 1)

        def hidden(t, s):
            pe.wait_ge(self.rT_ready, t + 1)
            for m in range(M):
                for k in range(KC):
                    ins = nc.tensor.matmul(self.hid[s][m // 4][:, m % 4, :], self.w1[:, k, m * 128:(m + 1) * 128],
                                           self.rT[:, k, :], start=(k == 0), stop=(k == KC - 1))
            ins.then_inc(self.h_made, 1)

        def used(t, s, i):
            pe.wait_ge(self.gelued, t + 1)
            use(t, s, i).then_inc(self.h_used, 1)

        def tile(t, s, i):
            hidden(t + 1, 1 - s)
            turn(t + 2, s, i + 1)
            used(t, s, i)
        pe.sem_inc(self.h_used, 2)
        turn(0, 0, 0)
        hidden(0, 0)
        turn(1, 1, 0)
        in_pairs(pe, self.tiles - 2, tile)
        last = self.tiles - 1
        hidden(last, last % 2)
        used(last - 1, (last - 1) % 2, (last - 1) // 2)
        used(last, last % 2, last // 2)

    def scalar(self, act):
        def tile(t, s, i):
            act.wait_ge(self.turned, t + 1)
            self.nc.scalar.activation(self.rT[:, :, :], self.pt[:, :, :], ACT.Copy).then_inc(self.rT_ready, 1)
            act.wait_ge(self.h_made, t + 1)
            act.wait_ge(self.h_used, t + 1)
            for m in range(self.M):
                ins = self.nc.scalar.activation(self.hT[:, s, m, :], self.hid[s][m // 4][:, m % 4, :], ACT.Gelu,
                                                bias=self.b1[:, m:m + 1])
            ins.then_inc(self.gelued, 1)
        in_pairs(act, self.tiles, tile)


def expert_logits(nc, ph, cn, x, mean, rstd, w1, b1, wg, bg, lg):
    hd = Hidden(nc, ph, cn, w1, b1, P, NT)
    plg = [ph.ps(f"plg{s}", [P, N_EXP1]) for s in range(2)]
    normed, kept = ph.sem("normed"), ph.sem("kept")
    with nc.Block() as block:
        @block.tensor
        def _(pe):
            def use(t, s, i):
                pe.wait_ge(kept, t + 1)
                for m in range(hd.M):
                    ins = nc.tensor.matmul(plg[s][:, :], hd.hT[:, s, m, :], wg[:, m, :], start=(m == 0), stop=(m == hd.M - 1))
                return ins
            hd.tensor(pe, lambda t, s, i: pe.wait_ge(normed, t + 1), use)

        @block.scalar
        def _(act):
            hd.scalar(act)

        @block.vector
        def _(dve):
            dve.sem_inc(kept, 2)

            def norm(t, s):
                nc.vector.tensor_scalar(hd.rows[:, s, :], x[:, bass.ds(t, 1), :].rearrange("p a f -> p (a f)"),
                                        mean[:, bass.ds(t, 1)], rstd[:, bass.ds(t, 1)], ALU.subtract, ALU.mult).then_inc(normed, 1)

            def keep(t, s, i):
                dve.wait_ge(hd.h_used, t + 3)
                nc.vector.tensor_tensor(lg[:, bass.ds(t, 1), :].rearrange("p a f -> p (a f)"), plg[s][:, :], bg[:, :],
                                        ALU.add).then_inc(kept, 1)

            def tile(t, s, i):
                dve.wait_ge(hd.turned, t + 1)
                norm(t + 2, s)
                keep(t, s, i)
            norm(0, 0)
            norm(1, 1)
            in_pairs(dve, NT - 2, tile)
            for t in (NT - 2, NT - 1):
                keep(t, t % 2, t // 2)


def expert_places(nc, ph, cn, x, mean, rstd, lg, pm, pos, tb, xn, sorted_d):
    E, ST = N_EXP1, tb.shape[1]
    ex, pr, far, sel, upto, at = (ph.sb(n, [P, NT, E]) for n in ("ex", "pr", "far", "sel", "upto", "at"))
    mx, sm, rs, first, posf = (ph.sb(n, [P, NT]) for n in ("mx", "sm", "rs", "first", "posf"))
    lots, ends, start = (ph.sb(n, [P, E]) for n in ("lots", "ends", "start"))
    tbf = ph.sb("tbf", [1, ST])
    tot, pre = ph.ps("tot", [128, 512]), ph.ps("pre", [128, 512])
    steps, shifted, exped, chosen, counted, placed, normed, scattered = (
        ph.sem(n) for n in ("steps", "shifted", "exped", "chosen", "counted", "placed", "normed", "scattered"))

    def all8(a):
        return spread(a[:, :], 2, [P, NT, E])

    def by_node(a):
        return spread(a[:, :], 1, [P, NT, E])
    with nc.Block() as block:
        @block.vector
        def _(dve):
            chain = Chain(dve, steps)
            expert = spread(cn["ramp"][0:P, 0:E], 1, [P, NT, E])
            chain(nc.vector.tensor_reduce(mx[:, :], lg[:, :, :], AX.X, ALU.max))
            nc.vector.tensor_tensor(lg[:, :, :], lg[:, :, :], all8(mx), ALU.subtract).then_inc(shifted, 1)
            for t in range(NT):
                nc.vector.tensor_scalar(xn[:, t, :], x[:, t, :], mean[:, t:t + 1], rstd[:, t:t + 1],
                                        ALU.subtract, ALU.mult).then_inc(normed, 1)
            dve.wait_ge(exped, 1)
            chain(nc.vector.tensor_reduce(sm[:, :], ex[:, :, :], AX.X, ALU.add))
            chain(nc.vector.reciprocal(rs[:, :], sm[:, :]))
            chain(nc.vector.tensor_tensor(pr[:, :, :], ex[:, :, :], all8(rs), ALU.mult))
            chain(nc.vector.tensor_reduce(pm[:, :], pr[:, :, :], AX.X, ALU.max))
            chain(nc.vector.tensor_tensor(far[:, :, :], pr[:, :, :], all8(pm), ALU.not_equal))
            chain(nc.vector.scalar_tensor_tensor(sel[:, :, :], far[:, :, :], 100.0, expert, ALU.mult, ALU.add))
            chain(nc.vector.tensor_reduce(first[:, :], sel[:, :, :], AX.X, ALU.min))
            nc.vector.tensor_tensor(sel[:, :, :], expert, all8(first), ALU.is_equal).then_inc(chosen, 1)
            dve.wait_ge(counted, 1)
            totv = tot[0:P, 0:NT * E].rearrange("p (t e) -> p t e", e=E)
            prev = pre[0:P, 0:NT * E].rearrange("p (t e) -> p t e", e=E)
            for e in range(E):
                ins = nc.vector.tensor_tensor_scan(upto[:, :, e], cn["one_row"][0:P, 0:NT], totv[:, :, e], 0.0, ALU.mult, ALU.add)
            chain(ins)
            chain(nc.vector.tensor_scalar(lots[:, :], upto[:, NT - 1, :], 1.0 / 128, -127.0 / 256, ALU.mult, ALU.add))
            chain(nc.vector.tensor_scalar(lots[:, :], lots[:, :], ROUND, None, ALU.add))
            chain(nc.vector.tensor_scalar(lots[:, :], lots[:, :], -ROUND, 1.0, ALU.add, ALU.add))
            chain(nc.vector.tensor_tensor_scan(ends[:, :], cn["one_row"][0:P, 0:E], lots[:, :], 0.0, ALU.mult, ALU.add))
            chain(nc.vector.tensor_tensor(start[:, :], ends[:, :], lots[:, :], ALU.subtract))
            chain(nc.vector.tensor_tensor(at[:, :, :], upto[:, :, :], totv, ALU.subtract))
            chain(nc.vector.tensor_tensor(at[:, :, :], at[:, :, :], prev, ALU.add))
            chain(nc.vector.scalar_tensor_tensor(at[:, :, :], by_node(start), 128.0, at[:, :, :], ALU.mult, ALU.add))
            chain(nc.vector.tensor_tensor(at[:, :, :], at[:, :, :], sel[:, :, :], ALU.mult))
            chain(nc.vector.tensor_reduce(posf[:, :], at[:, :, :], AX.X, ALU.add))
            nc.vector.tensor_copy(pos[:, :], posf[:, :]).then_inc(placed, 1)
            chain(nc.vector.memset(tbf[:, :], -1.0))
            for e in range(E):
                chain(nc.vector.scalar_tensor_tensor(tbf[:, :], cn["ramp"][0:1, 0:ST], start[0:1, e:e + 1], tbf[:, :],
                                                     ALU.is_ge, ALU.add))
            nc.vector.tensor_copy(tb[:, :], tbf[:, :])

        @block.scalar
        def _(act):
            act.wait_ge(shifted, 1)
            nc.scalar.activation(ex[:, :, :], lg[:, :, :], ACT.Exp).then_inc(exped, 1)

        @block.tensor
        def _(pe):
            pe.wait_ge(chosen, 1)
            flat = sel[:, :, :].rearrange("p t e -> p (t e)")
            nc.tensor.matmul(tot[:, 0:NT * E], cn["ones"][0:P, :], flat, start=True, stop=True)
            nc.tensor.matmul(pre[:, 0:NT * E], cn["tri"][0:P, :], flat, start=True, stop=True).then_inc(counted, 1)

        @block.gpsimd
        def _(pool):
            pool.wait_ge(normed, NT)
            pool.wait_ge(placed, 1)
            for t in range(NT):
                nc.gpsimd.indirect_dma_start(sorted_d, bass.IndirectOffsetOnAxis(ap=pos[:, t:t + 1], axis=0),
                                             xn[:, t, :], None).then_inc(scattered, 16)
            pool.wait_ge(scattered, NT * 16)


def expert_outputs(nc, ph, cn, w1, b1, wd, bd, tb, sorted_d, y_d):
    ST = tb.shape[1]
    hd = Hidden(nc, ph, cn, w1, b1, 128, ST)
    y, ysb = [ph.ps(f"y{s}", [128, 512]) for s in range(2)], ph.sb("ysb", [128, 2, D])
    loaded, stored = [ph.sem(f"loaded{s}") for s in range(2)], [ph.sem(f"stored{s}") for s in range(2)]
    y_ready = ph.sem("y_ready")
    x_rows, y_rows = (d.rearrange("(t p) f -> p t f", p=128) for d in (sorted_d, y_d))

    def number(name, t):
        return tile_numbers(nc, name, tb, t, 1)[0]
    with nc.Block() as block:
        @block.tensor
        def _(pe):
            def use(t, s, i):
                e = number("tensor", t)
                pe.wait_ge(y_ready, t + 1)
                for m in range(hd.M):
                    ins = nc.tensor.matmul(y[s][:, 0:D], hd.hT[:, s, m, :], wd[:, m, bass.ds(e, 1), :].rearrange("p a f -> p (a f)"),
                                           start=(m == 0), stop=(m == hd.M - 1))
                return ins
            hd.tensor(pe, lambda t, s, i: pe.wait_ge(loaded[s], i * 16 + 16), use)

        @block.scalar
        def _(act):
            hd.scalar(act)

        @block.vector
        def _(dve):
            dve.sem_inc(y_ready, 2)

            def tile(t, s, i):
                e = number("vector", t)
                dve.wait_ge(hd.h_used, t + 3)
                dve.wait_ge(stored[s], i * 16 + 16)
                nc.vector.tensor_tensor(ysb[:, s, :], y[s][:, 0:D], bd[:, bass.ds(e, 1), :].rearrange("p a f -> p (a f)"),
                                        ALU.add).then_inc(y_ready, 1)
            in_pairs(dve, ST, tile)

        @block.sync
        def _(sp):
            for s in range(2):
                sp.sem_inc(stored[s], 16)

            def fetch(t, s):
                sp.dma_start(hd.rows[:, s, :], x_rows[:, bass.ds(t, 1), :].rearrange("p a f -> p (a f)")).then_inc(loaded[s], 16)

            def store(t, s, i):
                sp.wait_ge(y_ready, t + 3)
                sp.dma_start(y_rows[:, bass.ds(t, 1), :].rearrange("p a f -> p (a f)"), ysb[:, s, :]).then_inc(stored[s], 16)

            def tile(t, s, i):
                sp.wait_ge(hd.turned, t + 1)
                fetch(t + 2, s)
                store(t, s, i)
            fetch(0, 0)
            fetch(1, 1)
            in_pairs(sp, ST - 2, tile)
            for t in (ST - 2, ST - 1):
                store(t, t % 2, t // 2)
            for s in range(2):
                sp.wait_ge(stored[s], (ST // 2 + 1) * 16)


def expert_sum(nc, ph, x, pm, pos, ye, y_d, out):
    G = 5
    gathered = [ph.sem(f"gathered{g}") for g in range(NT // G)]
    summed, stored = ph.sem("summed"), ph.sem("stored")
    with nc.Block() as block:
        @block.gpsimd
        def _(pool):
            for t in range(NT):
                nc.gpsimd.indirect_dma_start(ye[:, t, :], None, y_d, bass.IndirectOffsetOnAxis(ap=pos[:, t:t + 1], axis=0)
                                             ).then_inc(gathered[t // G], 16)

        @block.vector
        def _(dve):
            for g in range(NT // G):
                dve.wait_ge(gathered[g], 16 * G)
                for t in range(g * G, g * G + G):
                    ins = nc.vector.scalar_tensor_tensor(x[:, t, :], ye[:, t, :], pm[:, t:t + 1], x[:, t, :], ALU.mult, ALU.add)
                ins.then_inc(summed, 1)

        @block.sync
        def _(sp):
            for g in range(NT // G):
                sp.wait_ge(summed, g + 1)
                sp.dma_start(rows(out)[:, g * G:g * G + G, :], x[:, g * G:g * G + G, :]).then_inc(stored, 16)
            sp.wait_ge(stored, NT // G * 16)


def experts1(nc, cn, A, x, sorted_d, y_d, out):
    M, E = HID1 // 128, N_EXP1
    ST = sorted_d.shape[0] // 128
    with ExitStack() as ctx:
        ph = Phase(nc, ctx, "f1")
        mean, rstd = ph.sb("mean", [P, NT]), ph.sb("rstd", [P, NT])
        w1, wg, wd = ph.sb("w1", [128, KC, HID1]), ph.sb("wg", [128, M, E]), ph.sb("wd", [128, M, E, D])
        b1, bg, bd = ph.sb("b1", [128, M]), ph.sb("bg", [P, E]), ph.sb("bd", [128, E, D])
        lg, pm, pos = ph.sb("lg", [P, NT, E]), ph.sb("pm", [P, NT]), ph.sb("pos", [P, NT], I32)
        tb, nodes = ph.sb("tb", [1, ST], I32), ph.sb("nodes", [P, NT, D])
        with ExitStack() as inner:
            p1 = Phase(nc, inner, "f0")
            zero, zeroed, cleared = p1.sb("zero", [128, ST // 4, D]), p1.sem("zeroed"), p1.sem("cleared")
            with nc.Block() as block:
                @block.vector
                def _(dve):
                    nc.vector.memset(zero[:, :, :], 0.0).then_inc(zeroed, 1)

                @block.sync
                def _(sp):
                    sp.wait_ge(zeroed, 1)
                    for q in range(4):
                        sp.dma_start(sorted_d.rearrange("(q p t) f -> q p t f", q=4, p=128)[q], zero[:, :, :]).then_inc(cleared, 16)
                    sp.wait_ge(cleared, 64)
        load(nc, ph, [(w1[:, :, :], chunks(A["L1_ffn_W1"])), (wg[:, :, :], chunks(A["L1_ffn_Wg"])),
                      (b1[:, :], A["L1_ffn_b1"]), (bg[:, :], row(A["L1_ffn_bg"])),
                      (bd[:, :, :].rearrange("p e f -> p (e f)"), row(A["L1_ffn_bd"], 128))]
             + [(wd[:, :, e, :], chunks(A["L1_ffn_Wd"][e, :, :])) for e in range(E)])
        layer_norm_stats(nc, ph, rstd, mean, x)
        with ExitStack() as inner:
            expert_logits(nc, Phase(nc, inner, "f2"), cn, x, mean, rstd, w1, b1, wg, bg, lg)
        with ExitStack() as inner:
            expert_places(nc, Phase(nc, inner, "f3"), cn, x, mean, rstd, lg, pm, pos, tb, nodes, sorted_d)
        with ExitStack() as inner:
            expert_outputs(nc, Phase(nc, inner, "f4"), cn, w1, b1, wd, bd, tb, sorted_d, y_d)
        with ExitStack() as inner:
            expert_sum(nc, Phase(nc, inner, "f5"), x, pm, pos, nodes, y_d, out)


def move(nc, ctx, name, pairs):
    ph = Phase(nc, ctx, name)
    moved = ph.sem("moved")
    with nc.Block() as block:
        @block.sync
        def _(sp):
            for to, src in pairs:
                sp.dma_start(to, src).then_inc(moved, 16)
            sp.wait_ge(moved, 16 * len(pairs))


def gps_kernel(nc, A, out):
    with ExitStack() as ctx:
        def sb(name, shape, dt=F32):
            return ctx.enter_context(nc.sbuf_tensor(name, shape, dt))

        def dram(name, shape):
            return nc.dram_tensor(name, shape, F32, kind="Internal").ap()
        cn = {"ident": sb("ident", [128, 128]), "ones": sb("ones", [128, 128]), "tri": sb("tri", [128, 128]),
              "blocks": sb("blocks", [128, 128]), "ramp": sb("ramp", [128, 576]), "part": sb("part", [128, 1]),
              "zeros": sb("zeros", [128, 258]), "one_row": sb("one_row", [128, 150])}
        make_constants(nc, cn)
        x_d, xT_d, o_d = dram("x_kept", [N, D]), dram("xT_kept", [128, KC * N]), dram("attended", [N, D])
        support_d, hs_d, trans_d = dram("support", [N, D]), dram("gat_rows", [N, 32]), dram("transformed", [N_REL * N, D])
        kept_c = sb("tab_c", [128, 576, 2], I32), sb("tb_c", [1, 576], I32)
        with ExitStack() as mid:
            x = mid.enter_context(nc.sbuf_tensor("x", [P, NT, D], F32))
            xT = mid.enter_context(nc.sbuf_tensor("xT", [128, KC, NT, P], F32))
            gates = mid.enter_context(nc.sbuf_tensor("gates", [P, NT, 4], F32))
            keep_a, keep_b = Phase(nc, mid, "ka"), Phase(nc, mid, "kb")
            by_src = Sorting(nc, keep_a, keep_a, P, E_GRAPH // P, 25, NT, 448, 4, A["src"], A["dst"], weight_d=A["edge_weight"])
            by_key = Sorting(nc, keep_b, keep_b, 128, E_GAT // 128, 32, NT, 288, 2, A["L0_ffn_edge_index"][1, :],
                             A["L0_ffn_edge_index"][0, :])
            work_c = Phase(nc, mid, "wc")
            by_rel = Sorting(nc, work_c, work_c, P, E_GRAPH // P, 25, NT * N_REL, 576, 2, A["dst"], A["src"],
                             type_d=A["edge_type_6"], kept=kept_c)
            with ExitStack() as inner:
                sort_addresses(nc, inner, cn, "a", [by_src])
            layer0(nc, cn, A, x, xT, support_d, [lambda pool: by_src.scatter(pool, 0, 7),
                                                 lambda pool: by_src.scatter(pool, 7, 11)])

            def rest(pool):
                by_src.scatter(pool, 11, by_src.rounds)
                by_key.scatter(pool, 0, by_key.rounds)
            with ExitStack() as inner:
                sort_addresses(nc, inner, cn, "bc", [by_key, by_rel], rest)
            with ExitStack() as inner:
                reload_tables(nc, Phase(nc, inner, "rl"), [by_src, by_key])
            with ExitStack() as inner:
                aggregate(nc, Phase(nc, inner, "ag"), cn, by_src, support_d, x, True, False)
            gating(nc, cn, A, x, xT, gates, hs_d, by_key,
                   [lambda pool: by_rel.scatter(pool, 0, 6), lambda pool: by_rel.scatter(pool, 6, 9)])
            experts0(nc, cn, A, x, xT, gates, lambda pool: by_rel.scatter(pool, 9, by_rel.rounds))
            with ExitStack() as inner:
                ph = Phase(nc, inner, "c1")
                mean, rstd = ph.sb("mean", [P, NT]), ph.sb("rstd", [P, NT])
                kvp = ph.ps("kvp", [128, 258])
                with ExitStack() as deep:
                    p2 = Phase(nc, deep, "c2")
                    w = p2.sb("w", [128, KC, 2 * D + N_REL * D])
                    bias, tr = p2.sb("bias", [P, N_REL * D]), p2.sb("tr", [P, 2, N_REL, D])
                    k_sb, v_sb = p2.sb("k", [P, 2, D]), p2.sb("v", [P, 2, D])
                    by_tile = trans_d.rearrange("(r t p) f -> p t r f", r=N_REL, p=P)
                    load(nc, p2, [(w[:, :, 0:D], chunks(A["L1_mix_Wk"])), (w[:, :, D:2 * D], chunks(A["L1_mix_Wv"])),
                                  (w[:, :, 2 * D:], chunks(A["L1_gnn_W"])), (bias[:, :], row(A["L1_gnn_b"]))])
                    layer_norm_stats(nc, p2, rstd, mean, x)

                    def part(b):
                        rs = slice(2 * b - 2, 2 * b)
                        return ((512 * b, 512, "bias", lambda t, s: tr[:, s, rs, :].rearrange("p r f -> p (r f)"),
                                 bias[:, 512 * b - 512:512 * b]),
                                (b, lambda t: by_tile[:, bass.ds(t, 1), rs, :].rearrange("p a r f -> p (a r) f"),
                                 lambda s: tr[:, s, rs, :]))
                    parts = [part(b) for b in range(1, 4)]
                    project(nc, p2, cn, x, mean, rstd, xT, w, 2 * D + N_REL * D,
                            [(0, D, "elu", lambda t, s: k_sb[:, s, :], None), (D, D, "copy", lambda t, s: v_sb[:, s, :], None)]
                            + [p[0] for p in parts], [p[1] for p in parts], kv=(kvp, k_sb, v_sb), copies=1)
                mix1(nc, cn, A, x, xT, kvp, mean, rstd)
                move(nc, inner, "keep", [(rows(x_d), x[:, :, :]), (xT_d, xT[:, :, :, :].rearrange("p k t f -> p (k t f)"))])
        with ExitStack() as mid:
            ph = Phase(nc, mid, "r1")
            sT = ph.sb("sT", [128, NT * N_REL, 2 * P])
            with ExitStack() as inner:
                p2 = Phase(nc, inner, "r2")
                with nc.Block() as block:
                    @block.vector
                    def _(dve):
                        nc.vector.memset(sT[:, :, :], 0.0)
                reload_tables(nc, p2, [by_rel])
                aggregate(nc, Phase(nc, inner, "r4"), cn, by_rel, trans_d, sT, False, True)
            with ExitStack() as inner:
                relation_attention(nc, Phase(nc, inner, "r5"), A, sT, o_d)
        with ExitStack() as mid:
            x = mid.enter_context(nc.sbuf_tensor("x_again", [P, NT, D], F32))
            with ExitStack() as inner:
                xT = inner.enter_context(nc.sbuf_tensor("xT_again", [128, KC, NT, P], F32))
                move(nc, inner, "fetch", [(x[:, :, :], rows(x_d)), (xT[:, :, :, :].rearrange("p k t f -> p (k t f)"), xT_d)])
                relation_output(nc, Phase(nc, inner, "r6"), cn, A, x, xT, o_d)
            slots = (N // 128 + N_EXP1) * 128
            experts1(nc, cn, A, x, dram("by_expert", [slots, D]), dram("expert_out", [slots, D]), out)


_OUTS = [((N, D), "float32")]


def kernel(**inputs):
    import numpy as _np
    import concourse.bacc as _bacc
    from concourse import mybir as _mybir
    from concourse.bass_utils import run_bass_kernel_spmd as _run

    turned = {"L0_mix_Wq": "L0_mix_WqT", "L0_mix_Wkv": "L0_mix_WkvT", "L0_mix_Wproj": "L0_mix_WprojT",
              "L1_gnn_in_proj_w": "L1_gnn_in_proj_wT", "L1_gnn_attn_out_w": "L1_gnn_attn_out_wT",
              "L1_gnn_proj_w": "L1_gnn_proj_wT"}
    nc = _bacc.Bacc("TRN2", target_bir_lowering=False, num_devices=1)
    arrays, args = {}, {}
    for name, value in inputs.items():
        a = _np.asarray(value)
        if name in turned:
            name, a = turned[name], a.T
        if a.ndim == 3:
            a = a.transpose(1, 0, 2).reshape(a.shape[1], -1) if name in ("L1_gnn_W",) else a
        if name in ("L0_ffn_b1", "L1_ffn_b1", "L1_gnn_attn_out_b"):
            a = a.reshape(-1, 128).T
        if name in ("L0_ffn_att_src", "L0_ffn_att_dst", "L0_ffn_b2", "L1_gnn_b", "L1_ffn_bd"):
            a = a.reshape(-1)
        a = _np.ascontiguousarray(a)
        arrays[f"in_{name}_dram"] = a
        args[name] = nc.dram_tensor(f"in_{name}_dram", a.shape, _mybir.dt.from_np(a.dtype), kind="ExternalInput").ap()
    out = nc.dram_tensor("out_0_dram", _OUTS[0][0], _mybir.dt.float32, kind="ExternalOutput").ap()
    gps_kernel(nc, args, out)
    r = _run(nc, [arrays], core_ids=[0])
    return r.results[0]["out_0_dram"]
```

```python
import concourse.bass as bass
from concourse import mybir
from contextlib import ExitStack

F32 = mybir.dt.float32
I32 = mybir.dt.int32
BF16 = mybir.dt.bfloat16
ALU = mybir.AluOpType
ACT = mybir.ActivationFunctionType
AX = mybir.AxisListType

N = 3125
D = 256
P = 125
NT = N // P
KC = D // 128
E_GRAPH = 53125
E_GAT = 32768
N_REL = 6
N_EXP0 = 4
HID0 = 512
N_EXP1 = 8
HID1 = 1024
ROUND = 12582912.0
FAR = -3.0e38
EPS = 1e-5


class Chain:

    def __init__(self, eng, sem, base=0):
        self.eng, self.sem, self.base, self.n = eng, sem, base, 0

    def __call__(self, ins):
        self.n += 1
        ins.then_inc(self.sem, 1)
        self.eng.wait_ge(self.sem, self.base + self.n)


class Phase:

    def __init__(self, nc, ctx, name):
        self.nc, self.ctx, self.name, self.sems = nc, ctx, name, []
        ctx.callback(self.give_back)

    def sb(self, name, shape, dt=F32):
        return self.ctx.enter_context(self.nc.sbuf_tensor(f"{self.name}_{name}", shape, dt))

    def ps(self, name, shape, dt=F32):
        return self.ctx.enter_context(self.nc.psum_tensor(f"{self.name}_{name}", shape, dt))

    def sem(self, name):
        self.sems.append(self.nc.alloc_semaphore(f"{self.name}_{name}"))
        return self.sems[-1]

    def give_back(self):
        if self.sems:
            self.nc.clear_and_free_semaphores(self.sems)
            self.nc.all_engine_barrier()


def rows(ap):
    return ap.rearrange("(t p) f -> p t f", p=P)


def make_constants(nc, cn):
    with ExitStack() as ctx:
        ph = Phase(nc, ctx, "cst")
        ramp_i = ph.sb("ramp_i", [128, 576], I32)
        part_i = ph.sb("part_i", [128, 1], I32)
        filled, made = ph.sem("filled"), ph.sem("made")
        with nc.Block() as block:
            @block.gpsimd
            def _(pool):
                nc.gpsimd.memset(cn["ident"][:, :], 0.0).then_inc(filled, 1)
                nc.gpsimd.memset(cn["ones"][:, :], 1.0).then_inc(filled, 1)
                nc.gpsimd.memset(cn["tri"][:, :], 1.0).then_inc(filled, 1)
                nc.gpsimd.memset(cn["blocks"][:, :], 0.0).then_inc(filled, 1)
                nc.gpsimd.memset(cn["zeros"][:, :], 0.0).then_inc(filled, 1)
                nc.gpsimd.memset(cn["one_row"][:, :], 1.0).then_inc(filled, 1)
                nc.gpsimd.iota(ramp_i[:, :], [[1, 576]], base=0, channel_multiplier=0).then_inc(made, 1)
                nc.gpsimd.iota(part_i[:, :], [[1, 1]], base=0, channel_multiplier=1).then_inc(made, 1)
                pool.wait_ge(filled, 6)
                nc.gpsimd.affine_select(out=cn["ident"][:, :], in_=cn["ident"][:, :], compare_op=ALU.not_equal,
                                        fill=1.0, base=0, pattern=[[-1, 128]], channel_multiplier=1).then_inc(made, 1)
                nc.gpsimd.affine_select(out=cn["tri"][:, :], in_=cn["tri"][:, :], compare_op=ALU.is_gt,
                                        fill=0.0, base=0, pattern=[[1, 128]], channel_multiplier=-1).then_inc(made, 1)

            @block.vector
            def _(dve):
                dve.wait_ge(made, 4)
                nc.vector.tensor_copy(cn["ramp"][:, :], ramp_i[:, :])
                nc.vector.tensor_copy(cn["part"][:, :], part_i[:, :])
                for h in range(4):
                    nc.vector.memset(cn["blocks"][32 * h:32 * h + 32, 32 * h:32 * h + 32], 1.0)


def layer_norm_stats(nc, ph, rstd, mean, x, tiles=NT, pool_job=None, loads=(), x_src=None):
    st = ph.sb("st", [P, tiles, 6])
    mv = ph.sb("mv", [P, tiles, 2])
    ve = ph.sb("ve", [P, tiles])
    sd = ph.sb("sd", [P, tiles])
    steps, var_ready, root_ready = ph.sem("ln_steps"), ph.sem("var_ready"), ph.sem("root_ready")
    x_loaded, loaded = ph.sem("x_loaded"), ph.sem("loaded")
    with nc.Block() as block:
        @block.sync
        def _(sp):
            if x_src is not None:
                sp.dma_start(x[:, :, :], x_src).then_inc(x_loaded, 16)
            for to, src in loads:
                sp.dma_start(to, src).then_inc(loaded, 16)
            if loads:
                sp.wait_ge(loaded, 16 * len(loads))

        @block.gpsimd
        def _(pool):
            if pool_job is not None:
                pool_job(pool)

        @block.vector
        def _(dve):
            chain = Chain(dve, steps)
            if x_src is not None:
                dve.wait_ge(x_loaded, 16)
            with dve.Fori(0, tiles) as t:
                nc.vector.bn_stats(st[:, bass.ds(t, 1), :].rearrange("p a f -> p (a f)"),
                                   x[:, bass.ds(t, 1), :].rearrange("p a f -> p (a f)")).then_inc(steps, 1)
            chain.n = tiles
            dve.wait_ge(steps, tiles)
            for t in range(tiles):
                last = nc.vector.bn_aggr(mv[:, t, :], st[:, t, :])
                if t < tiles - 1:
                    last.then_inc(steps, 1)
                    chain.n += 1
            chain(last)
            chain(nc.vector.tensor_copy(mean[:, :], mv[:, :, 0]))
            nc.vector.tensor_scalar(ve[:, :], mv[:, :, 1], EPS, None, ALU.add).then_inc(var_ready, 1)
            dve.wait_ge(root_ready, 1)
            nc.vector.reciprocal(rstd[:, :], sd[:, :])

        @block.scalar
        def _(act):
            act.wait_ge(var_ready, 1)
            nc.scalar.activation(sd[:, :], ve[:, :], ACT.Sqrt).then_inc(root_ready, 1)


class Sorting:

    def __init__(self, nc, keep, work, parts, cols, step, nb, tiles, fields, key_d, other_d, type_d=None, weight_d=None,
                 kept=None):
        self.nc, self.parts, self.cols, self.step, self.nb, self.tiles = nc, parts, cols, step, nb, tiles
        self.key_d, self.other_d, self.type_d, self.weight_d = key_d, other_d, type_d, weight_d
        assert cols % step == 0 and tiles % 16 == 0 and tiles >= parts * cols // 128 + nb
        self.rounds = cols // step
        self.tab, self.tb = kept or (keep.sb("tab", [128, tiles, fields], I32), keep.sb("tb", [1, tiles], I32))
        self.table = nc.dram_tensor(f"table_{keep.name}", [128 * tiles, fields], I32, kind="Internal").ap()
        self.addr, self.rec = work.sb("addr", [parts, cols], I32), work.sb("rec", [parts, cols, fields], I32)
        self.ridx, self.rrec = work.sb("ridx", [parts, step], I32), work.sb("rrec", [parts, step, fields], I32)
        self.recs_ready, self.cleared = work.sem("recs_ready"), work.sem("cleared")
        self.copied, self.scattered, self.gate = work.sem("copied"), work.sem("scattered"), work.sem("gate")

    def load_columns(self, ph):
        shape = [self.parts, self.cols]
        self.key_i, self.other_i, self.one = ph.sb("key_i", shape, I32), ph.sb("other_i", shape, I32), ph.sb("one", shape)
        self.type_i = ph.sb("type_i", shape, I32) if self.type_d is not None else None
        self.loaded, self.empty_ready = ph.sem("loaded"), ph.sem("empty_ready")
        self.n_loads = 2 + (self.type_d is not None) + (self.weight_d is not None)

    def feed(self, sp):
        def cut(d):
            return d.rearrange("(p c) -> p c", p=self.parts)
        sp.dma_start(self.key_i[:, :], cut(self.key_d)).then_inc(self.loaded, 16)
        sp.dma_start(self.other_i[:, :], cut(self.other_d)).then_inc(self.loaded, 16)
        if self.type_d is not None:
            sp.dma_start(self.type_i[:, :], cut(self.type_d)).then_inc(self.loaded, 16)
        if self.weight_d is not None:
            sp.dma_start(self.one[:, :], cut(self.weight_d)).then_inc(self.loaded, 16)

    def clear(self, sp):
        sp.wait_ge(self.empty_ready, 1)
        sp.dma_start(self.table.rearrange("(p t) f -> p t f", p=128), self.tab[:, :, :]).then_inc(self.cleared, 16)
        sp.wait_ge(self.cleared, 16)

    def scatter(self, pool, first, last):
        nc, step = self.nc, self.step
        pool.wait_ge(self.recs_ready, 1)
        pool.wait_ge(self.cleared, 16)
        with pool.Fori(first, last) as c:
            nc.gpsimd.tensor_copy(self.ridx[:, :], self.addr[:, bass.ds(c * step, step)]).then_inc(self.copied, 1)
            nc.gpsimd.tensor_copy(self.rrec[:, :, :], self.rec[:, bass.ds(c * step, step), :]).then_inc(self.copied, 1)
            pool.wait_ge(self.copied, c * 2 + 2)
            pool.sem_inc(self.gate, 1)
            for u in range(step):
                nc.gpsimd.indirect_dma_start(self.table, bass.IndirectOffsetOnAxis(ap=self.ridx[:, u:u + 1], axis=0),
                                             self.rrec[:, u, :], None).then_inc(self.scattered, 16)
            pool.wait_ge(self.scattered, c * (16 * step) + 16 * step)
            pool.sem_inc(self.gate, 1)


def reload_tables(nc, ph, sorts):
    reloaded = ph.sem("reloaded")
    with nc.Block() as block:
        @block.sync
        def _(sp):
            for s in sorts:
                sp.dma_start(s.tab[:, :, :], s.table.rearrange("(p t) f -> p t f", p=128)).then_inc(reloaded, 16)
            sp.wait_ge(reloaded, 16 * len(sorts))


def sort_addresses(nc, ctx, cn, name, sorts, pool_job=None):
    pmax, cmax = max(s.parts for s in sorts), max(s.cols for s in sorts)
    ph = Phase(nc, ctx, f"sorts_{name}")
    for i, s in enumerate(sorts):
        s.load_columns(Phase(nc, ctx, f"cols_{name}{i}"))
    nbmax, tmax = max(s.nb for s in sorts), max(s.tiles for s in sorts)
    key_a, bk_a, loc_a, pos_a, run_a = (ph.sb(n, [pmax, cmax]) for n in ("key", "bk", "loc", "pos", "run"))
    U = 5
    hit_a, runs_a, pos2_a = ph.sb("hit", [pmax, U, cmax]), ph.sb("runs", [pmax, U, cmax]), ph.sb("pos2", [pmax, cmax])
    cnt_a, pre_a = ph.sb("cnt", [pmax, nbmax]), ph.sb("pre", [pmax, nbmax])
    lots_a, upto_a, start_a = (ph.sb(n, [128, nbmax]) for n in ("lots", "upto", "start"))
    begun_a, start_p = ph.sb("begun", [P, tmax]), ph.sb("start_p", [P, 1])
    ps_tot, ps_pre = ph.ps("ps_tot", [128, nbmax]), ph.ps("ps_pre", [128, nbmax])
    ps_start, ps_tb = ph.ps("ps_start", [P, 1]), [ph.ps(f"ps_tb{i}", [1, 512]) for i in range((tmax + 511) // 512)]
    steps, counted, summed = ph.sem("steps"), ph.sem("counted"), ph.sem("summed")
    started, start_moved, begun_ready, begun_used = (
        ph.sem(n) for n in ("started", "start_moved", "begun_ready", "begun_used"))

    gate = ph.sem("gate")
    n_groups = [0]
    for s in sorts:
        n_groups.append(n_groups[-1] + (s.nb + P - 1) // P)

    with nc.Block() as block:
        @block.sync
        def _(sp):
            for s in sorts:
                s.feed(sp)
            for s in sorts:
                s.clear(sp)

        @block.vector
        def _(dve):
            chain = Chain(dve, steps)
            for n, s in enumerate(sorts):
                p, c, nb = s.parts, s.cols, s.nb
                key, bk, loc, pos = key_a[0:p, 0:c], bk_a[0:p, 0:c], loc_a[0:p, 0:c], pos_a[0:p, 0:c]
                hits, runs = [hit_a[0:p, u, 0:c] for u in range(U)], [runs_a[0:p, u, 0:c] for u in range(U)]
                hit, run, one = hits[0], run_a[0:p, 0:c], s.one[:, :]
                places = (pos, pos2_a[0:p, 0:c])
                cnt, pre, lots, upto, start = (cnt_a[0:p, 0:nb], pre_a[0:p, 0:nb], lots_a[:, 0:nb], upto_a[:, 0:nb],
                                               start_a[:, 0:nb])
                recf = s.rec[:, :, :].bitcast(F32)
                chain(nc.vector.memset(s.tab[:, :, :], 0))
                nc.vector.memset(s.tab[:, :, 1].bitcast(F32), -1.0).then_inc(s.empty_ready, 1)
                chain(nc.vector.memset(s.rec[:, :, :], 0))
                for a in places:
                    chain(nc.vector.memset(a, 0.0))
                dve.wait_ge(s.loaded, 16 * s.n_loads)
                if s.weight_d is not None:
                    chain(nc.vector.tensor_copy(recf[:, :, 2], one))
                chain(nc.vector.memset(one, 1.0))
                chain(nc.vector.tensor_copy(key, s.key_i[:, :]))
                chain(nc.vector.tensor_scalar(bk, key, -float(P // 2), 1.0 / P, ALU.add, ALU.mult))
                chain(nc.vector.tensor_scalar(bk, bk, ROUND, None, ALU.add))
                chain(nc.vector.tensor_scalar(bk, bk, -ROUND, None, ALU.add))
                chain(nc.vector.scalar_tensor_tensor(loc, bk, -float(P), key, ALU.mult, ALU.add))
                chain(nc.vector.tensor_copy(recf[:, :, 1], loc))
                if s.type_d is not None:
                    chain(nc.vector.tensor_copy(hit, s.type_i[:, :]))
                    chain(nc.vector.scalar_tensor_tensor(key, bk, float(N_REL), hit, ALU.mult, ALU.add))
                    chain(nc.vector.tensor_copy(run, s.other_i[:, :]))
                    chain(nc.vector.scalar_tensor_tensor(run, hit, float(N), run, ALU.mult, ALU.add))
                    chain(nc.vector.tensor_copy(s.rec[:, :, 0], run))
                else:
                    chain(nc.vector.tensor_copy(key, bk))
                    chain(nc.vector.tensor_copy(s.rec[:, :, 0], s.other_i[:, :]))
                assert nb % U == 0
                k0 = chain.n
                with dve.Fori(0, nb // U) as i:
                    for u in range(U):
                        b = i * U + u
                        dve.wait_ge(steps, b + (k0 - U + 1))
                        nc.vector.tensor_scalar(hits[u], key, cn["ramp"][0:p, bass.ds(b, 1)], 0.0, ALU.is_equal,
                                                ALU.add, accum_out=cnt_a[0:p, bass.ds(b, 1)]).then_inc(steps, 1)
                chain.n = k0 + nb
                dve.wait_ge(steps, chain.n)
                nc.vector.tensor_copy(pre[:, 0:1], cnt[:, 0:1]).then_inc(counted, 1)
                dve.wait_ge(summed, n + 1)
                chain(nc.vector.tensor_scalar(lots, ps_tot[:, 0:nb], 1.0 / 128, -127.0 / 256, ALU.mult, ALU.add))
                chain(nc.vector.tensor_scalar(lots, lots, ROUND, None, ALU.add))
                chain(nc.vector.tensor_scalar(lots, lots, -ROUND, 1.0, ALU.add, ALU.add))
                chain(nc.vector.tensor_tensor_scan(upto, cn["one_row"][:, 0:nb], lots, 0.0, ALU.mult, ALU.add))
                chain(nc.vector.tensor_tensor(start, upto, lots, ALU.subtract))
                chain(nc.vector.scalar_tensor_tensor(pre, start[0:p, :], 128.0, ps_pre[0:p, 0:nb], ALU.mult, ALU.add))
                dve.sem_inc(started, 1)
                for a in range(0, nb, P):
                    m, g = min(P, nb - a), n_groups[n] + a // P
                    dve.wait_ge(start_moved, g + 1)
                    chain(nc.vector.tensor_copy(start_p[0:m, :], ps_start[0:m, :]))
                    if g:
                        dve.wait_ge(begun_used, g)
                    nc.vector.tensor_scalar(begun_a[0:m, 0:s.tiles], cn["ramp"][0:m, 0:s.tiles], start_p[0:m, :], None,
                                            ALU.is_ge).then_inc(begun_ready, 1)
                dve.wait_ge(begun_used, n_groups[n + 1])
                for a in range(0, s.tiles, 512):
                    m = min(512, s.tiles - a)
                    chain(nc.vector.tensor_scalar(s.tb[0:1, a:a + m], ps_tb[a // 512][0:1, 0:m], -1.0, None, ALU.add))
                k0 = chain.n
                with dve.Fori(0, nb // U) as i:
                    base = i * (3 * U) + k0
                    for u in range(U):
                        nc.vector.tensor_scalar(hits[u], key, cn["ramp"][0:p, bass.ds(i * U + u, 1)], None,
                                                ALU.is_equal).then_inc(steps, 1)
                    for u in range(U):
                        dve.wait_ge(steps, base + (u + 1))
                        nc.vector.tensor_tensor_scan(runs[u], one, hits[u], pre_a[0:p, bass.ds(i * U + u, 1)],
                                                     ALU.mult, ALU.add).then_inc(steps, 1)
                    for u in range(U):
                        dve.wait_ge(steps, base + max(U + u + 1, 2 * U + u - 1))
                        dve.sem_inc(gate, 1)
                        nc.vector.copy_predicated(places[u % 2], hits[u].bitcast(I32), runs[u]).then_inc(steps, 1)
                    dve.wait_ge(steps, base + 3 * U)
                    dve.sem_inc(gate, 1)
                chain.n = k0 + 3 * nb
                chain(nc.vector.tensor_tensor(pos, pos, places[1], ALU.add))
                chain(nc.vector.tensor_scalar(pos, pos, -1.0, None, ALU.add))
                chain(nc.vector.tensor_scalar(bk, pos, 1.0 / 128, -127.0 / 256, ALU.mult, ALU.add))
                chain(nc.vector.tensor_scalar(bk, bk, ROUND, None, ALU.add))
                chain(nc.vector.tensor_scalar(bk, bk, -ROUND, None, ALU.add))
                chain(nc.vector.scalar_tensor_tensor(run, bk, -128.0, pos, ALU.mult, ALU.add))
                chain(nc.vector.scalar_tensor_tensor(run, run, float(s.tiles), bk, ALU.mult, ALU.add))
                chain(nc.vector.tensor_copy(s.addr[:, :], run))
                dve.sem_inc(s.recs_ready, 1)

        @block.tensor
        def _(pe):
            for n, s in enumerate(sorts):
                pe.wait_ge(counted, n + 1)
                nc.tensor.matmul(ps_tot[:, 0:s.nb], cn["ones"][0:s.parts, :], cnt_a[0:s.parts, 0:s.nb], start=True, stop=True)
                nc.tensor.matmul(ps_pre[:, 0:s.nb], cn["tri"][0:s.parts, :], cnt_a[0:s.parts, 0:s.nb],
                                 start=True, stop=True).then_inc(summed, 1)
                pe.wait_ge(started, n + 1)
                for a in range(0, s.nb, P):
                    m, g = min(P, s.nb - a), n_groups[n] + a // P
                    if g:
                        pe.wait_ge(begun_ready, g)
                    nc.tensor.matmul(ps_start[0:m, :], start_a[0:1, a:a + m], cn["ones"][0:1, 0:1], start=True,
                                     stop=True).then_inc(start_moved, 1)
                    pe.wait_ge(begun_ready, g + 1)
                    for c in range(0, s.tiles, 512):
                        w = min(512, s.tiles - c)
                        ins = nc.tensor.matmul(ps_tb[c // 512][0:1, 0:w], cn["ones"][0:m, 0:1], begun_a[0:m, c:c + w],
                                               start=(a == 0), stop=(a + P >= s.nb))
                    ins.then_inc(begun_used, 1)

        @block.gpsimd
        def _(pool):
            if pool_job is not None:
                pool_job(pool)


def tile_numbers(nc, eng, tb, first, count):
    kind = {"vector": mybir.EngineType.DVE, "tensor": mybir.EngineType.PE}[eng]
    return nc.values_load_multi_w_load_instructions(
        tb[0:1, bass.ds(first, count)], engines=(kind,), min_val=0, max_val=None,
        skip_runtime_bounds_check_because="a bucket is a count of starts below the tile")[1]


def aggregate(nc, ph, cn, so, source, acc, weighted, transposed):
    G, NG = 4, 4
    tiles, tab = so.tiles, so.tab
    gath, hot = ph.sb("gath", [128, NG, G, D]), ph.sb("hot", [128, NG, G, P])
    idx = ph.sb("idx", [128, NG, G], I32)
    out_p = 128 if transposed else P
    prod = [[ph.ps(f"prod{s}{j}", [128, 512]) for j in range(G)] for s in range(2)]
    w = 2 * P if transposed else D
    gathered = [ph.sem(f"gathered{g}") for g in range(NG)]
    hot_ready = [ph.sem(f"hot_ready{g}") for g in range(NG)]
    used = [ph.sem(f"used{g}") for g in range(NG)]
    added = [ph.sem(f"added{s}") for s in range(2)]
    idx_ready, gate, gate_a, steps = ph.sem("idx_ready"), ph.sem("gate"), ph.sem("gate_a"), ph.sem("steps")
    tabf = tab[:, :, :].bitcast(F32)
    step = NG * G
    rounds = tiles // step

    with nc.Block() as block:
        @block.gpsimd
        def _(pool):
            with pool.Fori(0, rounds) as r:
                for g in range(NG):
                    pool.wait_ge(idx_ready, r * NG + (g + 1))
                    pool.sem_inc(gate, 1)
                    for j in range(G):
                        nc.gpsimd.indirect_dma_start(gath[:, g, j, :], None, source,
                                                     bass.IndirectOffsetOnAxis(ap=idx[:, g, j:j + 1], axis=0)
                                                     ).then_inc(gathered[g], 16)

        @block.scalar
        def _(act):
            with act.Fori(0, rounds) as r:
                for g in range(NG):
                    act.wait_ge(used[g], r + 1)
                    act.sem_inc(gate_a, 1)
                    nc.scalar.activation(idx[:, g, :], tab[:, bass.ds(r * step + g * G, G), 0], ACT.Copy).then_inc(idx_ready, 1)

        @block.vector
        def _(dve):
            for s in range(2):
                dve.sem_inc(added[s], 1)
            def one_hot(r, g, j):
                if j == 0:
                    dve.wait_ge(used[g], r + 1)
                t = bass.ds(r * step + g * G + j, 1)
                ins = nc.vector.tensor_scalar(
                    hot[:, g, j, :], cn["ramp"][:, 0:P], tabf[:, t, 1], tabf[:, t, 2] if weighted else 1.0,
                    ALU.is_equal, ALU.mult)
                if j == G - 1:
                    ins.then_inc(hot_ready[g], 1)

            def one_round(r, last):
                for g in range(NG):
                    numbers = tile_numbers(nc, "vector", so.tb, r * step + g * G, G)
                    dve.wait_ge(used[g], r + 2)
                    for j in range(G):
                        a = acc[:, bass.ds(numbers[j], 1), :].rearrange("p a f -> p (a f)")
                        nc.vector.tensor_tensor(a, a, prod[g % 2][j][0:out_p, 0:w], ALU.add).then_inc(steps, 1)
                        if g + 2 < NG:
                            one_hot(r, g + 2, j)
                        elif not last:
                            one_hot(r + 1, g + 2 - NG, j)
                        dve.wait_ge(steps, r * step + (g * G + j + 1))
                    dve.sem_inc(added[g % 2], 1)
            for g in range(2):
                for j in range(G):
                    one_hot(0, g, j)
            with dve.Fori(0, rounds - 1) as r:
                one_round(r, False)
            one_round(rounds - 1, True)

        @block.tensor
        def _(pe):
            for g in range(NG):
                pe.sem_inc(used[g], 1)
            with pe.Fori(0, rounds) as r:
                for g in range(NG):
                    pe.wait_ge(gathered[g], r * (16 * G) + 16 * G)
                    pe.wait_ge(hot_ready[g], r + 1)
                    pe.wait_ge(added[g % 2], r * 2 + (g // 2 + 1))
                    for j in range(G):
                        if transposed:
                            for h in range(2):
                                ins = nc.tensor.matmul(prod[g % 2][j][:, h * P:(h + 1) * P], gath[:, g, j, h * 128:(h + 1) * 128],
                                                       hot[:, g, j, :], start=True, stop=True)
                        else:
                            ins = nc.tensor.matmul(prod[g % 2][j][0:P, 0:D], hot[:, g, j, :], gath[:, g, j, :], start=True, stop=True)
                    ins.then_inc(used[g], 1)


def project(nc, ph, cn, x, mean, rstd, xT, w_sb, width, evac, stores, kv=None, copies=2, pool_job=None):
    xc, xTc = ph.sb("xc", [P, 2, D]), ph.sb("xTc", [128, 2, KC, P])
    nb = (width + 511) // 512
    pt, po = [ph.ps(f"pt{i}", [128, KC, P]) for i in range(2)], [ph.ps(f"po{i}", [P, 512]) for i in range(nb * copies)]
    low, low_e = ph.sb("low", [P, D]), ph.sb("low_e", [P, D])
    normed, turned, xT_ready, pt_free = ph.sem("normed"), ph.sem("turned"), ph.sem("xT_ready"), ph.sem("pt_free")
    made, evacuated = ph.sem("made"), ph.sem("evacuated")
    stored = [ph.sem(f"stored{i}") for i in range(2)]
    gate, lowered, exped, kv_ready, kv_used = (ph.sem(n) for n in ("gate", "lowered", "exped", "kv_ready", "kv_used"))
    n_st = len(stores)
    assert NT % 2 == 1

    def bank(s, i):
        return po[i + (s * nb if copies == 2 else 0)]

    def each_tile(eng, do):
        with eng.Fori(0, NT // 2) as i:
            for s in range(2):
                do(i * 2 + s, s, i)
        do(NT - 1, 0, NT // 2)

    with nc.Block() as block:
        @block.gpsimd
        def _(pool):
            if pool_job is not None:
                pool_job(pool)

        @block.vector
        def _(dve):
            dve.sem_inc(evacuated, copies * nb)
            if kv is not None:
                nc.vector.memset(kv[1][:, 1, :], 0.0)
                nc.vector.memset(kv[2][:, 1, :], 0.0).then_inc(kv_ready, 1)

            def norm(t, s):
                dve.wait_ge(turned, t + 1)
                nc.vector.tensor_scalar(xc[:, s, :], x[:, bass.ds(t, 1), :].rearrange("p a f -> p (a f)"), mean[:, bass.ds(t, 1)],
                                        rstd[:, bass.ds(t, 1)], ALU.subtract, ALU.mult).then_inc(normed, 1)

            def tile(t, s, i):
                if not (isinstance(t, int) and t == NT - 1):
                    norm(t + 1, 1 - s)
                if kv is not None:
                    dve.wait_ge(kv_used, t + 1)
                if n_st:
                    dve.wait_ge(stored[s], i * (16 * n_st) + 16 * n_st)
                for b in range(nb):
                    dve.wait_ge(made, t * nb + (2 * nb + b + 1))
                    mine = [e for e in evac if e[0] // 512 == b]
                    elus = [e for e in mine if e[2] == "elu"]
                    for c, n, kind, to, bias in elus:
                        nc.vector.tensor_scalar(low[:, :], bank(s, b)[:, c % 512:c % 512 + n], 0.0, None,
                                                ALU.min).then_inc(lowered, 1)
                    for c, n, kind, to, bias in [e for e in mine if e[2] != "elu"] + elus:
                        src = bank(s, b)[:, c % 512:c % 512 + n]
                        if kind == "bias":
                            ins = nc.vector.tensor_tensor(to(t, s), src, bias, ALU.add)
                        elif kind == "copy":
                            ins = nc.vector.tensor_scalar(to(t, s), src, 1.0, None, ALU.mult)
                        else:
                            dve.wait_ge(exped, t + 1)
                            ins = nc.vector.scalar_tensor_tensor(to(t, s), src, 0.0, low_e[:, :], ALU.max, ALU.add)
                    ins.then_inc(evacuated, 1)
                    if kv is not None and b == 0:
                        dve.wait_ge(evacuated, t * nb + (copies * nb + 1))
                        dve.sem_inc(kv_ready, 1)
            norm(0, 0)
            each_tile(dve, tile)

        @block.scalar
        def _(act):
            act.sem_inc(pt_free, 2)

            def tile(t, s, i):
                act.wait_ge(turned, t + 3)
                act.wait_ge(made, t * nb + nb)
                nc.scalar.activation(xTc[:, s, :, :], pt[s][:, :, :], ACT.Copy).then_inc(xT_ready, 1)
                act.sem_inc(gate, 1)
                nc.scalar.activation(xT[:, :, bass.ds(t, 1), :].rearrange("p k a f -> p k (a f)"), pt[s][:, :, :],
                                     ACT.Copy).then_inc(pt_free, 1)
                if kv is not None:
                    act.wait_ge(lowered, t + 1)
                    nc.scalar.activation(low_e[:, :], low[:, :], ACT.Exp).then_inc(exped, 1)
            each_tile(act, tile)

        @block.sync
        def _(sp):
            if not n_st:
                return
            for s in range(2):
                sp.sem_inc(stored[s], 16 * n_st)

            def tile(t, s, i):
                for b, to, buf in stores:
                    sp.wait_ge(evacuated, t * nb + (copies * nb + b + 1))
                    sp.dma_start(to(t), buf(s)).then_inc(stored[s], 16)
            each_tile(sp, tile)
            sp.wait_ge(stored[0], (NT // 2 + 2) * 16 * n_st)
            sp.wait_ge(stored[1], (NT // 2 + 1) * 16 * n_st)

        @block.tensor
        def _(pe):
            pe.sem_inc(turned, 2)
            pe.sem_inc(kv_used, 1)
            pe.sem_inc(made, 2 * nb)

            def turn_tile(t, s):
                pe.wait_ge(normed, t + 1)
                pe.wait_ge(pt_free, t + 1)
                for k in range(KC):
                    ins = nc.tensor.matmul(pt[s][:, k, :], xc[:, s, k * 128:(k + 1) * 128], cn["ident"][0:P, 0:P], start=True, stop=True)
                ins.then_inc(turned, 1)

            def add_kv(t, s):
                kvp, k_sb, v_sb = kv
                pe.wait_ge(kv_ready, t + 1)
                for h in range(2):
                    hs = slice(h * 128, (h + 1) * 128)
                    nc.tensor.matmul(kvp[:, hs], v_sb[:, s, hs], k_sb[:, s, hs], start=False, stop=False, skip_group_check=True)
                    ins = nc.tensor.matmul(kvp[:, 256 + h:257 + h], k_sb[:, s, hs], cn["ones"][0:P, 0:1],
                                           start=False, stop=False, skip_group_check=True)
                ins.then_inc(kv_used, 1)

            def tile(t, s, i):
                if not (isinstance(t, int) and t == NT - 1):
                    turn_tile(t + 1, 1 - s)
                pe.wait_ge(xT_ready, t + 1)
                for b in range(nb):
                    n = min(512, width - 512 * b)
                    pe.wait_ge(evacuated, t * nb + (b + 1))
                    for k in range(KC):
                        ins = nc.tensor.matmul(bank(s, b)[:, 0:n], xTc[:, s, k, :], w_sb[:, k, 512 * b:512 * b + n],
                                               start=(k == 0), stop=(k == KC - 1))
                    ins.then_inc(made, 1)
                if kv is not None:
                    add_kv(t, 1 - s)
            if kv is not None:
                nc.tensor.matmul(kv[0][:, :], cn["zeros"][:, 0:128], cn["zeros"][:, 0:258], start=True, stop=False)
            turn_tile(0, 0)
            each_tile(pe, tile)
            if kv is not None:
                add_kv(NT, 0)
                nc.tensor.matmul(kv[0][:, :], cn["zeros"][:, 0:128], cn["zeros"][:, 0:258], start=False, stop=True)


def fold_context(nc, ph, cn, kvp, cb, kb, ks, wT, fold):
    pf = [ph.ps(f"pf{h}", [128, D]) for h in range(2)]
    ready, made, steps = ph.sem("fc_ready"), ph.sem("fc_made"), ph.sem("fc_steps")
    with nc.Block() as block:
        @block.vector
        def _(dve):
            chain = Chain(dve, steps)
            chain(nc.vector.tensor_copy(ks[:, :], kvp[:, 256:258]))
            for h in range(2):
                nc.vector.tensor_scalar(kb[:, h, :], cn["blocks"][:, :], ks[:, h:h + 1], None, ALU.mult)
                chain(nc.vector.tensor_tensor(cb[:, h, :], kvp[:, h * 128:(h + 1) * 128], cn["blocks"][:, :], ALU.mult))
            dve.sem_inc(ready, 1)
            dve.wait_ge(made, 1)
            for h in range(2):
                nc.vector.tensor_copy(fold[:, h, :], pf[h][:, :])

        @block.tensor
        def _(pe):
            pe.wait_ge(ready, 1)
            for h in range(2):
                ins = nc.tensor.matmul(pf[h][:, :], cb[:, h, :], wT[:, h, :], start=True, stop=True)
            ins.then_inc(made, 1)


def linear_attention(nc, ph, cn, xT, wq, kb, fold, guard, finish, pool_job=None, keep=None):
    pq, pd, po = ph.ps("pq", [128, 2, P]), ph.ps("pd", [128, 2, P]), ph.ps("po", [P, D])
    low, low_e, q1 = ph.sb("low", [128, 2, P]), ph.sb("low_e", [128, 2, P]), ph.sb("q1", [128, 2, P])
    r0, r1, qn = ph.sb("r0", [128, 2, P]), ph.sb("r1", [128, 2, P]), ph.sb("qn", [128, 2, P])
    q_made, lowered, exped, q_ready = ph.sem("q_made"), ph.sem("lowered"), ph.sem("exped"), ph.sem("q_ready")
    d_made, qn_ready, o_made, finished, steps = (ph.sem("d_made"), ph.sem("qn_ready"), ph.sem("o_made"), ph.sem("finished"),
                                                 ph.sem("la_steps"))
    kept = ph.sem("kept")
    with nc.Block() as block:
        @block.sync
        def _(sp):
            if keep is not None:
                sp.dma_start(keep, xT[:, :, :, :].rearrange("p k t f -> p (k t f)")).then_inc(kept, 16)
                sp.wait_ge(kept, 16)

        @block.gpsimd
        def _(pool):
            if pool_job is not None:
                pool_job(pool)

        @block.tensor
        def _(pe):
            pe.sem_inc(finished, 1)

            def q_of(t):
                for h in range(2):
                    for k in range(KC):
                        ins = nc.tensor.matmul(pq[:, h, :], wq[:, k, h * 128:(h + 1) * 128],
                                               xT[:, k, bass.ds(t, 1), :].rearrange("p a f -> p (a f)"), start=(k == 0), stop=(k == KC - 1))
                ins.then_inc(q_made, 1)

            def tile(t, last):
                pe.wait_ge(q_ready, t + 1)
                for h in range(2):
                    ins = nc.tensor.matmul(pd[:, h, :], kb[:, h, :], q1[:, h, :], start=True, stop=True)
                ins.then_inc(d_made, 1)
                if not last:
                    q_of(t + 1)
                pe.wait_ge(qn_ready, t + 1)
                pe.wait_ge(finished, t + 1)
                for h in range(2):
                    ins = nc.tensor.matmul(po[:, :], qn[:, h, :], fold[:, h, :], start=(h == 0), stop=(h == 1))
                ins.then_inc(o_made, 1)
            q_of(0)
            with pe.Fori(0, NT - 1) as t:
                tile(t, False)
            tile(NT - 1, True)

        @block.scalar
        def _(act):
            with act.Fori(0, NT) as t:
                act.wait_ge(lowered, t + 1)
                nc.scalar.activation(low_e[:, :, :], low[:, :, :], ACT.Exp).then_inc(exped, 1)

        @block.vector
        def _(dve):
            def q_of(t):
                dve.wait_ge(q_made, t + 1)
                nc.vector.tensor_scalar(low[:, :, :], pq[:, :, :], 0.0, None, ALU.min).then_inc(lowered, 1)
                dve.wait_ge(exped, t + 1)
                nc.vector.scalar_tensor_tensor(q1[:, :, :], pq[:, :, :], 0.0, low_e[:, :, :], ALU.max, ALU.add).then_inc(q_ready, 1)

            def tile(t, last):
                chain = Chain(dve, steps, t * 2)
                dve.wait_ge(d_made, t + 1)
                dve.wait_ge(q_ready, t + 1)
                chain(nc.vector.tensor_scalar(r0[:, :, :], pd[:, :, :], guard[1], None, guard[0]))
                chain(nc.vector.reciprocal(r1[:, :, :], r0[:, :, :]))
                nc.vector.tensor_tensor(qn[:, :, :], q1[:, :, :], r1[:, :, :], ALU.mult).then_inc(qn_ready, 1)
                if not last:
                    q_of(t + 1)
                dve.wait_ge(o_made, t + 1)
                finish(t, po[:, :]).then_inc(finished, 1)
            q_of(0)
            with dve.Fori(0, NT - 1) as t:
                tile(t, False)
            tile(NT - 1, True)


def load(nc, ph, pairs):
    loaded = ph.sem("weights_loaded")
    with nc.Block() as block:
        @block.sync
        def _(sp):
            for to, src in pairs:
                sp.dma_start(to, src).then_inc(loaded, 16)
            sp.wait_ge(loaded, 16 * len(pairs))


def chunks(w):
    return w.rearrange("(k p) m -> p k m", p=128)


def row(v, parts=P):
    return v.rearrange("(a f) -> a f", a=1).to_broadcast([parts, v.shape[0]])


def layer0(nc, cn, A, x, xT, support_d, pool_jobs):
    with ExitStack() as ctx:
        ph = Phase(nc, ctx, "a1")
        w = ph.sb("w", [128, KC, 3 * D])
        wq, wp = ph.sb("wq", [128, KC, D]), ph.sb("wp", [128, KC, D])
        mean, rstd = ph.sb("mean", [P, NT]), ph.sb("rstd", [P, NT])
        sup, k_sb, v_sb = ph.sb("sup", [P, 2, D]), ph.sb("k", [P, 2, D]), ph.sb("v", [P, 2, D])
        cb, kb, ks, fold = ph.sb("cb", [128, 2, 128]), ph.sb("kb", [128, 2, 128]), ph.sb("ks", [128, 2]), ph.sb("fold", [128, 2, D])
        b0, b1, bias = ph.sb("b0", [P, D]), ph.sb("b1", [P, D]), ph.sb("bias", [P, D])
        kvp = ph.ps("kvp", [128, 258])
        layer_norm_stats(nc, ph, rstd, mean, x, pool_job=pool_jobs[0],
                         loads=[(w[:, :, 0:2 * D], chunks(A["L0_mix_WkvT"])), (w[:, :, 2 * D:3 * D], chunks(A["L0_gnn_weight"])),
                      (wq[:, :, :], chunks(A["L0_mix_WqT"])), (wp[:, :, :], chunks(A["L0_mix_WprojT"])),
                      (b0[:, :], row(A["L0_gnn_bias"])), (b1[:, :], row(A["L0_mix_bproj"]))], x_src=rows(A["x"]))
        with ExitStack() as inner:
            p2 = Phase(nc, inner, "a2")
            project(nc, p2, cn, x, mean, rstd, xT, w, 3 * D,
                    [(0, D, "elu", lambda t, s: k_sb[:, s, :], None), (D, D, "copy", lambda t, s: v_sb[:, s, :], None),
                     (2 * D, D, "copy", lambda t, s: sup[:, s, :], None)],
                    [(1, lambda t: rows(support_d)[:, bass.ds(t, 1), :].rearrange("p a f -> p (a f)"), lambda s: sup[:, s, :])],
                    kv=(kvp, k_sb, v_sb), pool_job=pool_jobs[1])
        with ExitStack() as inner:
            p3 = Phase(nc, inner, "a3")
            fold_context(nc, p3, cn, kvp, cb, kb, ks, wp, fold)
        with ExitStack() as inner:
            p4 = Phase(nc, inner, "a4")
            gate = p4.sem("bias_ready")
            with nc.Block() as block:
                @block.vector
                def _(dve):
                    nc.vector.tensor_tensor(bias[:, :], b0[:, :], b1[:, :], ALU.add).then_inc(gate, 1)
                    dve.wait_ge(gate, 1)
                    for t in range(NT):
                        nc.vector.tensor_tensor(x[:, t, :], x[:, t, :], bias[:, :], ALU.add)

            def finish(t, psum):
                a = x[:, bass.ds(t, 1), :].rearrange("p a f -> p (a f)")
                return nc.vector.tensor_tensor(a, a, psum, ALU.add)
            linear_attention(nc, p4, cn, xT, wq, kb, fold, (ALU.max, 1e-6), finish, pool_jobs[2])


def spread(ap, axis, shape):
    return ap.unsqueeze(axis).to_broadcast(shape)


def gat_max(nc, ph, cn, so, source, ge, top):
    G, NG, H = 4, 4, 4
    tab = so.tab
    V = 3 * H + 1
    gath, idx = ph.sb("gath", [128, NG, G, 32]), ph.sb("idx", [128, NG, G], I32)
    vals, vT = ph.sb("vals", [128, NG, G, V], BF16), ph.sb("vT", [V, 2, G * 128], BF16)
    pick, ident_b = ph.sb("pick", [V, H + 1, P], BF16), ph.sb("ident_b", [128, 128], BF16)
    mask = ph.sb("mask", [V, H + 1])
    pen, best = ph.sb("pen", [P, 2, G * 128], BF16), ph.sb("best", [P, 2, H, G])
    vt = [ph.ps(f"vt{i}", [V, G * 128]) for i in range(2)]
    wide = [ph.ps(f"wide{c}", [P, G * 128]) for c in range(H + 1)]
    gathered = [ph.sem(f"gathered{g}") for g in range(NG)]
    read = [ph.sem(f"read{g}") for g in range(NG)]
    made, freed = [ph.sem(f"made{c}") for c in range(H + 1)], [ph.sem(f"freed{c}") for c in range(H)]
    idx_ready, gate_p, gate_a, steps = ph.sem("idx_ready"), ph.sem("gate_p"), ph.sem("gate_a"), ph.sem("steps")
    vals_ready, turned, vT_ready, picked = ph.sem("vals_ready"), ph.sem("turned"), ph.sem("vT_ready"), ph.sem("picked")
    idx_made, pen_ready = ph.sem("idx_made"), ph.sem("pen_ready")
    tabf = tab[:, :, :].bitcast(F32)
    step = NG * G
    rounds = so.tiles // step
    with nc.Block() as block:
        @block.gpsimd
        def _(pool):
            nc.gpsimd.tensor_copy(ident_b[:, :], cn["ident"][:, :]).then_inc(picked, 1)
            nc.gpsimd.tensor_copy(mask[:, H:H + 1], cn["ident"][0:V, V - 1:V]).then_inc(idx_made, 1)
            for c in range(H):
                nc.gpsimd.tensor_tensor(mask[:, c:c + 1], cn["ident"][0:V, c:c + 1], cn["ident"][0:V, H + c:H + c + 1],
                                        ALU.add).then_inc(idx_made, 1)
            pool.wait_ge(idx_made, H + 1)
            for c in range(H):
                nc.gpsimd.tensor_tensor(mask[:, c:c + 1], mask[:, c:c + 1], cn["ident"][0:V, 2 * H + c:2 * H + c + 1],
                                        ALU.add).then_inc(idx_made, 1)
            pool.wait_ge(idx_made, 2 * H + 1)
            for c in range(H + 1):
                nc.gpsimd.tensor_copy(pick[:, c, :], mask[:, c:c + 1].to_broadcast([V, P])).then_inc(picked, 1)
            with pool.Fori(0, rounds) as r:
                for g in range(NG):
                    pool.wait_ge(read[g], r + 1)
                    pool.sem_inc(gate_p, 1)
                    nc.gpsimd.tensor_copy(idx[:, g, :], tab[:, bass.ds(r * step + g * G, G), 0]).then_inc(idx_ready, 1)
                    pool.wait_ge(idx_ready, r * NG + (g + 1))
                    pool.sem_inc(gate_p, 1)
                    for j in range(G):
                        nc.gpsimd.indirect_dma_start(gath[:, g, j, :], None, source,
                                                     bass.IndirectOffsetOnAxis(ap=idx[:, g, j:j + 1], axis=0)
                                                     ).then_inc(gathered[g], 16)

        @block.scalar
        def _(act):
            for g in range(NG):
                act.sem_inc(read[g], 1)
            act.sem_inc(vT_ready, 2)
            with act.Fori(0, rounds) as r:
                def fetch(g):
                    t = bass.ds(r * step + g * G, G)
                    act.wait_ge(gathered[g], r * (16 * G) + 16 * G)
                    act.wait_ge(turned, r * NG + g + 1)
                    act.sem_inc(gate_a, 1)
                    nc.scalar.activation(vals[:, g, :, 0:3 * H], gath[:, g, :, 20:32], ACT.Copy).then_inc(vals_ready, 1)
                    nc.scalar.activation(vals[:, g, :, 3 * H], tabf[:, t, 1], ACT.Copy).then_inc(vals_ready, 1)
                    nc.scalar.activation(ge[:, t, :], gath[:, g, :, 0:20], ACT.Copy).then_inc(read[g], 1)
                for g in range(NG):
                    fetch(g)
                    act.wait_ge(turned, r * NG + g + 2)
                    act.wait_ge(made[H - 1], r * NG + g + 1)
                    nc.scalar.activation(vT[:, g % 2, :], vt[g % 2][:, :], ACT.Copy).then_inc(vT_ready, 1)

        @block.tensor
        def _(pe):
            pe.sem_inc(turned, 1)
            pe.sem_inc(made[H - 1], 2)
            pe.wait_ge(picked, H + 2)

            def turn_group(n, g):
                pe.wait_ge(vals_ready, n * 2 + 2)
                pe.wait_ge(vT_ready, n + 1)
                for j in range(G):
                    ins = nc.tensor.matmul(vt[g % 2][:, j * 128:(j + 1) * 128], vals[:, g, j, :], ident_b[:, :],
                                           start=True, stop=True)
                ins.then_inc(turned, 1)

            def key_row(n, s):
                pe.wait_ge(vT_ready, n + 3)
                nc.tensor.matmul(wide[H][:, :], pick[:, H, :], vT[:, s, :], start=True, stop=True).then_inc(made[H], 1)

            def head(n, s, c):
                pe.wait_ge(freed[c], n + 1)
                nc.tensor.matmul(wide[c][:, :], pick[:, c, :], vT[:, s, :], start=True, stop=False)
                nc.tensor.matmul(wide[c][:, :], ident_b[0:P, 0:P], pen[:, s, :], start=False, stop=True).then_inc(made[c], 1)

            def one_round(r, last):
                for g in range(NG):
                    n, s = r * NG + g, g % 2
                    more = g + 1 < NG or not last
                    if more:
                        turn_group(n + 1, (g + 1) % NG)
                    pe.wait_ge(pen_ready, n + 1)
                    head(n, s, 0)
                    head(n, s, 1)
                    if more:
                        key_row(n + 1, 1 - s)
                    head(n, s, 2)
                    head(n, s, 3)
            turn_group(0, 0)
            key_row(0, 0)
            with pe.Fori(0, rounds - 1) as r:
                one_round(r, False)
            one_round(rounds - 1, True)

        @block.vector
        def _(dve):
            for c in range(H):
                dve.sem_inc(freed[c], 1)
            dve.sem_inc(steps, G)

            def penalty(n, s):
                dve.wait_ge(made[H], n + 1)
                nc.vector.tensor_scalar(pen[:, s, :], wide[H][:, :], cn["part"][0:P, 0:1], FAR,
                                        ALU.not_equal, ALU.mult).then_inc(pen_ready, 1)

            def larger(n, s, numbers, j):
                dve.wait_ge(steps, n * G + j)
                a = top[:, bass.ds(numbers[j], 1), :].rearrange("p a f -> p (a f)")
                nc.vector.tensor_tensor(a, a, best[:, s, :, j], ALU.max).then_inc(steps, 1)

            def group(r, g, first=False, last=False):
                n, s = r * NG + g, g % 2
                if not first:
                    numbers = tile_numbers(nc, "vector", so.tb, r * step + (g - 1) * G, G)
                    dve.wait_ge(steps, n * G)
                    dve.wait_ge(freed[H - 1], n + 1)
                for c in range(H):
                    dve.wait_ge(made[c], n + (3 if c == H - 1 else 1))
                    nc.vector.tensor_reduce(best[:, s, c, :], wide[c][:, :].rearrange("p (t e) -> p t e", t=G),
                                            AX.X, ALU.max).then_inc(freed[c], 1)
                    if not first:
                        larger(n, 1 - s, numbers, c)
                    if c == 1 and not last:
                        penalty(n + 1, 1 - s)

            penalty(0, 0)
            group(0, 0, first=True)
            for g in range(1, NG):
                group(0, g)
            with dve.Fori(1, rounds - 1) as r:
                for g in range(NG):
                    group(r, g)
            for g in range(NG):
                group(rounds - 1, g, last=(g == NG - 1))
            numbers = tile_numbers(nc, "vector", so.tb, so.tiles - G, G)
            dve.wait_ge(freed[H - 1], rounds * NG + 1)
            for j in range(G):
                larger(rounds * NG, (NG - 1) % 2, numbers, j)


def gat_spread(nc, ph, cn, so, adm, xp, pool_job):
    G, NG = 4, 4
    hot, ident_b, hotT = ph.sb("hot", [128, NG, G, P], BF16), ph.sb("ident_b", [128, 128], BF16), ph.sb("hotT", [P, NG, G, 128])
    pt = [ph.ps(f"pt{g}", [P, G, 128]) for g in range(NG)]
    px = [ph.ps(f"px{g}", [128, G, 8]) for g in range(NG)]

    def each(name):
        return [ph.sem(f"{name}{g}") for g in range(NG)]
    hot_ready, turned, hotT_ready, spread_out, kept = (
        each(n) for n in ("hot_ready", "turned", "hotT_ready", "spread_out", "kept"))
    tabf = so.tab[:, :, :].bitcast(F32)
    step = NG * G
    rounds = so.tiles // step
    with nc.Block() as block:
        @block.gpsimd
        def _(pool):
            pool_job(pool)

        @block.vector
        def _(dve):
            nc.vector.tensor_copy(ident_b[:, :], cn["ident"][:, :])
            for g in range(NG):
                dve.sem_inc(kept[g], 1)

            def one_hot(r, g):
                dve.wait_ge(turned[g], r + 1)
                for j in range(G):
                    t = bass.ds(r * step + g * G + j, 1)
                    ins = nc.vector.tensor_scalar(hot[:, g, j, :], cn["ramp"][:, 0:P], tabf[:, t, 1], None, ALU.is_equal)
                ins.then_inc(hot_ready[g], 1)

            def one_round(r, last):
                for g in range(NG):
                    if not last:
                        one_hot(r + 1, g)
                    dve.wait_ge(spread_out[g], r + 2)
                    nc.vector.tensor_scalar(xp[:, bass.ds(r * step + g * G, G), :], px[g][:, :, :], 1.0, None,
                                            ALU.mult).then_inc(kept[g], 1)
            for g in range(NG):
                one_hot(0, g)
            with dve.Fori(0, rounds - 1) as r:
                one_round(r, False)
            one_round(rounds - 1, True)

        @block.scalar
        def _(act):
            with act.Fori(0, rounds) as r:
                for g in range(NG):
                    act.wait_ge(turned[g], r + 2)
                    act.wait_ge(spread_out[g], r + 1)
                    nc.scalar.activation(hotT[:, g, :, :], pt[g][:, :, :], ACT.Copy).then_inc(hotT_ready[g], 1)

        @block.tensor
        def _(pe):
            for g in range(NG):
                pe.sem_inc(turned[g], 1)
                pe.sem_inc(spread_out[g], 1)
                pe.sem_inc(hotT_ready[g], 1)
            def turn_group(r, g):
                pe.wait_ge(hot_ready[g], r + 1)
                pe.wait_ge(hotT_ready[g], r + 1)
                for j in range(G):
                    ins = nc.tensor.matmul(pt[g][:, j, :], hot[:, g, j, :], ident_b[:, :], start=True, stop=True)
                ins.then_inc(turned[g], 1)

            def one_round(r, last):
                for g in range(NG):
                    if g + 1 < NG:
                        turn_group(r, g + 1)
                    elif not last:
                        turn_group(r + 1, 0)
                    numbers = tile_numbers(nc, "tensor", so.tb, r * step + g * G, G)
                    pe.wait_ge(hotT_ready[g], r + 2)
                    pe.wait_ge(kept[g], r + 1)
                    for j in range(G):
                        ins = nc.tensor.matmul(px[g][:, j, :], hotT[:, g, j, :],
                                               adm[:, bass.ds(numbers[j], 1), :].rearrange("p a f -> p (a f)"), start=True, stop=True)
                    ins.then_inc(spread_out[g], 1)
            turn_group(0, 0)
            with pe.Fori(0, rounds - 1) as r:
                one_round(r, False)
            one_round(rounds - 1, True)


def gat_weights(nc, ph, so, ge, xp):
    z0, z1 = ph.sb("z0", [128, so.tiles, 4]), ph.sb("z1", [128, so.tiles, 4])
    steps, ready, exped = ph.sem("steps"), ph.sem("ready"), ph.sem("exped")
    with nc.Block() as block:
        @block.vector
        def _(dve):
            chain = Chain(dve, steps)
            chain(nc.vector.tensor_tensor(z0[:, :, :], xp[:, :, 0:4], ge[:, :, 16:20], ALU.add))
            chain(nc.vector.scalar_tensor_tensor(z1[:, :, :], z0[:, :, :], 0.2, z0[:, :, :], ALU.mult, ALU.max))
            chain(nc.vector.tensor_tensor(z0[:, :, :], z1[:, :, :], xp[:, :, 4:8], ALU.subtract))
            nc.vector.tensor_scalar(z1[:, :, :], z0[:, :, :], 0.0, None, ALU.min).then_inc(ready, 1)
            dve.wait_ge(exped, 1)
            for h in range(4):
                nc.vector.tensor_tensor(ge[:, :, 4 * h:4 * h + 4], ge[:, :, 4 * h:4 * h + 4],
                                        ge[:, :, 16 + h:17 + h].to_broadcast([128, so.tiles, 4]), ALU.mult)

        @block.scalar
        def _(act):
            act.wait_ge(ready, 1)
            nc.scalar.activation(ge[:, :, 16:20], z1[:, :, :], ACT.Exp).then_inc(exped, 1)


def gat_sum(nc, ph, cn, so, ge, num, pool_job):
    G, NG = 4, 4
    hot = ph.sb("hot", [128, NG, G, P])
    part = ph.sb("part", [P, G, NT, 20])
    pa = [ph.ps(f"pa{g}", [P, G, 20]) for g in range(NG)]
    hot_ready, summed, added = ([ph.sem(f"{n}{g}") for g in range(NG)] for n in ("hot_ready", "summed", "added"))
    steps = ph.sem("steps")
    tabf = so.tab[:, :, :].bitcast(F32)
    step = NG * G
    rounds = so.tiles // step
    with nc.Block() as block:
        @block.gpsimd
        def _(pool):
            pool_job(pool)

        @block.vector
        def _(dve):
            nc.vector.memset(part[:, :, :, :], 0.0).then_inc(steps, 1)
            def one_hot(r, g):
                dve.wait_ge(summed[g], r + 1)
                for j in range(G):
                    t = bass.ds(r * step + g * G + j, 1)
                    ins = nc.vector.tensor_scalar(hot[:, g, j, :], cn["ramp"][:, 0:P], tabf[:, t, 1], None, ALU.is_equal)
                ins.then_inc(hot_ready[g], 1)

            def one_round(r, last):
                for g in range(NG):
                    if not last:
                        one_hot(r + 1, g)
                    numbers = tile_numbers(nc, "vector", so.tb, r * step + g * G, G)
                    dve.wait_ge(summed[g], r + 2)
                    for j in range(G):
                        a = part[:, j, bass.ds(numbers[j], 1), :].rearrange("p a f -> p (a f)")
                        ins = nc.vector.tensor_tensor(a, a, pa[g][:, j, :], ALU.add)
                        ins.then_inc(steps, 1)
                    dve.wait_ge(steps, r * step + (g * G + G + 1))
                    dve.sem_inc(added[g], 1)
            for g in range(NG):
                one_hot(0, g)
            with dve.Fori(0, rounds - 1) as r:
                one_round(r, False)
            one_round(rounds - 1, True)
            chain = Chain(dve, steps, so.tiles + 1)
            dve.wait_ge(steps, so.tiles + 1)
            for j in range(G):
                chain(nc.vector.tensor_tensor(num[:, :, :], num[:, :, :], part[:, j, :, :], ALU.add))

        @block.tensor
        def _(pe):
            for g in range(NG):
                pe.sem_inc(summed[g], 1)
                pe.sem_inc(added[g], 1)
            with pe.Fori(0, rounds) as r:
                for g in range(NG):
                    pe.wait_ge(hot_ready[g], r + 1)
                    pe.wait_ge(added[g], r + 1)
                    for j in range(G):
                        ins = nc.tensor.matmul(pa[g][:, j, :], hot[:, g, j, :], 
                                               ge[:, bass.ds(r * step + g * G + j, 1), :].rearrange("p a f -> p (a f)"), start=True, stop=True)
                    ins.then_inc(summed[g], 1)


def gating(nc, cn, A, x, xT, gates, hs_d, so, pool_jobs):
    with ExitStack() as ctx:
        ph = Phase(nc, ctx, "b1")
        w = ph.sb("w", [128, KC, 16])
        mean, rstd = ph.sb("mean", [P, NT]), ph.sb("rstd", [P, NT])
        h = ph.sb("h", [P, NT, 24])
        att_s, att_d, t16 = ph.sb("att_s", [P, 16]), ph.sb("att_d", [P, 16]), ph.sb("t16", [P, NT, 16])
        u16 = ph.sb("u16", [P, NT, 16])
        top, adm, num = ph.sb("top", [P, NT, 4]), ph.sb("adm", [P, NT, 8]), ph.sb("num", [P, NT, 20])
        ge, xp = ph.sb("ge", [128, so.tiles, 20]), ph.sb("xp", [128, so.tiles, 8])
        bg, lg, lb = ph.sb("bg", [P, 16]), ph.sb("lg", [P, 16]), ph.sb("lb", [P, 16])
        layer_norm_stats(nc, ph, rstd, mean, x,
                         loads=[(w[:, :, :], chunks(A["L0_ffn_W_gat"])), (att_s[:, :], row(A["L0_ffn_att_src"])),
                      (att_d[:, :], row(A["L0_ffn_att_dst"])), (bg[:, :], row(A["L0_ffn_b_gat"])),
                      (lg[:, :], row(A["L0_ffn_ln_gamma"])), (lb[:, :], row(A["L0_ffn_ln_beta"]))])
        with ExitStack() as inner:
            p2 = Phase(nc, inner, "b2")
            project(nc, p2, cn, x, mean, rstd, xT, w, 16,
                    [(0, 16, "copy", lambda t, s: h[:, bass.ds(t, 1), 0:16].rearrange("p a f -> p (a f)"), None)], [],
                    pool_job=pool_jobs[0])
        with ExitStack() as inner:
            p3 = Phase(nc, inner, "b3")
            steps, ready, stored = p3.sem("steps"), p3.sem("ready"), p3.sem("stored")
            sent, rest, part = p3.sb("sent", [P, NT, 32]), p3.sb("rest", [P, NT, 4]), p3.sb("part", [P, NT, 4], BF16)
            with nc.Block() as block:
                @block.vector
                def _(dve):
                    chain = Chain(dve, steps)
                    for att, c in ((att_s, 16), (att_d, 20)):
                        chain(nc.vector.tensor_tensor(t16[:, :, :], h[:, :, 0:16], spread(att[:, :], 1, [P, NT, 16]), ALU.mult))
                        chain(nc.vector.tensor_reduce(h[:, :, c:c + 4], t16[:, :, :].rearrange("p t (h e) -> p t h e", h=4),
                                                      AX.X, ALU.add))
                    chain(nc.vector.tensor_copy(rest[:, :, :], h[:, :, 16:20]))
                    for i in range(3):
                        chain(nc.vector.tensor_copy(part[:, :, :], rest[:, :, :]))
                        chain(nc.vector.tensor_copy(sent[:, :, 20 + 4 * i:24 + 4 * i], part[:, :, :]))
                        chain(nc.vector.tensor_tensor(rest[:, :, :], rest[:, :, :], sent[:, :, 20 + 4 * i:24 + 4 * i], ALU.subtract))
                    chain(nc.vector.tensor_copy(sent[:, :, 0:20], h[:, :, 0:20]))
                    dve.sem_inc(ready, 1)
                    nc.vector.tensor_copy(top[:, :, :], h[:, :, 16:20])

                @block.sync
                def _(sp):
                    sp.dma_start(so.tab[:, :, :], so.table.rearrange("(p t) f -> p t f", p=128)).then_inc(stored, 16)
                    sp.wait_ge(ready, 1)
                    sp.dma_start(rows(hs_d), sent[:, :, :]).then_inc(stored, 16)
                    sp.wait_ge(stored, 32)
        with ExitStack() as inner:
            p5 = Phase(nc, inner, "bm")
            gat_max(nc, p5, cn, so, hs_d, ge, top)
        with ExitStack() as inner:
            p6 = Phase(nc, inner, "b6")
            steps, ready, exped = p6.sem("steps"), p6.sem("ready"), p6.sem("exped")
            e0, e1 = p6.sb("e0", [P, NT, 4]), p6.sb("e1", [P, NT, 4])
            with nc.Block() as block:
                @block.vector
                def _(dve):
                    chain = Chain(dve, steps)
                    chain(nc.vector.tensor_copy(adm[:, :, 0:4], h[:, :, 20:24]))
                    chain(nc.vector.tensor_tensor(e0[:, :, :], top[:, :, :], h[:, :, 20:24], ALU.add))
                    chain(nc.vector.scalar_tensor_tensor(adm[:, :, 4:8], e0[:, :, :], 0.2, e0[:, :, :], ALU.mult, ALU.max))
                    chain(nc.vector.tensor_tensor(e0[:, :, :], h[:, :, 16:20], h[:, :, 20:24], ALU.add))
                    chain(nc.vector.scalar_tensor_tensor(e1[:, :, :], e0[:, :, :], 0.2, e0[:, :, :], ALU.mult, ALU.max))
                    nc.vector.tensor_tensor(e0[:, :, :], e1[:, :, :], adm[:, :, 4:8], ALU.subtract).then_inc(ready, 1)
                    dve.wait_ge(exped, 1)
                    for hd in range(4):
                        nc.vector.tensor_tensor(num[:, :, 4 * hd:4 * hd + 4], h[:, :, 4 * hd:4 * hd + 4],
                                                num[:, :, 16 + hd:17 + hd].to_broadcast([P, NT, 4]), ALU.mult)

                @block.scalar
                def _(act):
                    act.wait_ge(ready, 1)
                    nc.scalar.activation(num[:, :, 16:20], e0[:, :, :], ACT.Exp).then_inc(exped, 1)
        with ExitStack() as inner:
            gat_spread(nc, Phase(nc, inner, "bx"), cn, so, adm, xp, pool_jobs[1])
        with ExitStack() as inner:
            gat_weights(nc, Phase(nc, inner, "bw"), so, ge, xp)
        with ExitStack() as inner:
            gat_sum(nc, Phase(nc, inner, "bs"), cn, so, ge, num, pool_jobs[2])
        with ExitStack() as inner:
            p8 = Phase(nc, inner, "b8")
            steps, ready, rooted, gap, exped = p8.sem("steps"), p8.sem("ready"), p8.sem("rooted"), p8.sem("gap"), p8.sem("exped")
            den, rden, m, v, sd, rs = (p8.sb(n, [P, NT, 4]) for n in ("den", "rden", "m", "v", "sd", "rs"))
            s, s2, eq, far, sel1, sel2 = (p8.sb(n, [P, NT, 4]) for n in ("s", "s2", "eq", "far", "sel1", "sel2"))
            m1, m2, first, dq, q, w1, w2 = (p8.sb(n, [P, NT]) for n in ("m1", "m2", "first", "dq", "q", "w1", "w2"))

            def all4(a):
                return spread(a[:, :], 2, [P, NT, 4])

            def all16(a):
                return spread(a, 2, [P, NT, 16])
            expert = spread(cn["ramp"][0:P, 0:4], 1, [P, NT, 4])
            with nc.Block() as block:
                @block.vector
                def _(dve):
                    chain = Chain(dve, steps)
                    chain(nc.vector.tensor_scalar(den[:, :, :], num[:, :, 16:20], 1e-16, None, ALU.add))
                    chain(nc.vector.reciprocal(rden[:, :, :], den[:, :, :]))
                    for hd in range(4):
                        chain(nc.vector.tensor_tensor(t16[:, :, 4 * hd:4 * hd + 4], num[:, :, 4 * hd:4 * hd + 4],
                                                      rden[:, :, hd:hd + 1].to_broadcast([P, NT, 4]), ALU.mult))
                    chain(nc.vector.tensor_tensor(t16[:, :, :], t16[:, :, :], spread(bg[:, :], 1, [P, NT, 16]), ALU.add))
                    chain(nc.vector.tensor_reduce(m[:, :, 0], t16[:, :, :], AX.X, ALU.add))
                    chain(nc.vector.tensor_scalar(m[:, :, 1], m[:, :, 0], 1.0 / 16, None, ALU.mult))
                    chain(nc.vector.tensor_tensor(t16[:, :, :], t16[:, :, :], all16(m[:, :, 1]), ALU.subtract))
                    chain(nc.vector.tensor_tensor(u16[:, :, :], t16[:, :, :], t16[:, :, :], ALU.mult))
                    chain(nc.vector.tensor_reduce(v[:, :, 0], u16[:, :, :], AX.X, ALU.add))
                    nc.vector.tensor_scalar(v[:, :, 1], v[:, :, 0], 1.0 / 16, EPS, ALU.mult, ALU.add).then_inc(ready, 1)
                    dve.wait_ge(rooted, 1)
                    chain(nc.vector.reciprocal(rs[:, :, 0], sd[:, :, 0]))
                    chain(nc.vector.tensor_tensor(t16[:, :, :], t16[:, :, :], all16(rs[:, :, 0]), ALU.mult))
                    chain(nc.vector.tensor_tensor(t16[:, :, :], t16[:, :, :], spread(lg[:, :], 1, [P, NT, 16]), ALU.mult))
                    chain(nc.vector.tensor_tensor(t16[:, :, :], t16[:, :, :], spread(lb[:, :], 1, [P, NT, 16]), ALU.add))
                    chain(nc.vector.tensor_reduce(s[:, :, :], t16[:, :, :].rearrange("p t (h e) -> p t e h", h=4), AX.X, ALU.add))
                    chain(nc.vector.tensor_scalar(s[:, :, :], s[:, :, :], 0.25, None, ALU.mult))

                    def choose(score, best, sel):
                        chain(nc.vector.tensor_reduce(best[:, :], score[:, :, :], AX.X, ALU.max))
                        chain(nc.vector.tensor_tensor(eq[:, :, :], score[:, :, :], all4(best), ALU.not_equal))
                        chain(nc.vector.scalar_tensor_tensor(far[:, :, :], eq[:, :, :], 100.0, expert, ALU.mult, ALU.add))
                        chain(nc.vector.tensor_reduce(first[:, :], far[:, :, :], AX.X, ALU.min))
                        chain(nc.vector.tensor_tensor(sel[:, :, :], expert, all4(first), ALU.is_equal))
                    choose(s, m1, sel1)
                    chain(nc.vector.scalar_tensor_tensor(s2[:, :, :], sel1[:, :, :], FAR, s[:, :, :], ALU.mult, ALU.add))
                    choose(s2, m2, sel2)
                    nc.vector.tensor_tensor(dq[:, :], m2[:, :], m1[:, :], ALU.subtract).then_inc(gap, 1)
                    dve.wait_ge(exped, 1)
                    chain(nc.vector.tensor_scalar(w2[:, :], q[:, :], 1.0, None, ALU.add))
                    chain(nc.vector.reciprocal(w1[:, :], w2[:, :]))
                    chain(nc.vector.tensor_tensor(w2[:, :], q[:, :], w1[:, :], ALU.mult))
                    chain(nc.vector.tensor_tensor(sel1[:, :, :], sel1[:, :, :], all4(w1), ALU.mult))
                    chain(nc.vector.tensor_tensor(sel2[:, :, :], sel2[:, :, :], all4(w2), ALU.mult))
                    chain(nc.vector.tensor_tensor(gates[:, :, :], sel1[:, :, :], sel2[:, :, :], ALU.add))

                @block.scalar
                def _(act):
                    act.wait_ge(ready, 1)
                    nc.scalar.activation(sd[:, :, 0], v[:, :, 1], ACT.Sqrt).then_inc(rooted, 1)
                    act.wait_ge(gap, 1)
                    nc.scalar.activation(q[:, :], dq[:, :], ACT.Exp).then_inc(exped, 1)


def experts0(nc, cn, A, x, xT, gates, pool_job):
    M = HID0 // 128
    with ExitStack() as ctx:
        ph = Phase(nc, ctx, "e0")
        w1, w2 = ph.sb("w1", [128, N_EXP0, KC, HID0]), ph.sb("w2", [128, N_EXP0, M, D])
        b1, b2 = ph.sb("b1", [128, N_EXP0, M]), ph.sb("b2", [P, N_EXP0, D])
        hT, tmp = ph.sb("hT", [128, 2, M, P]), ph.sb("tmp", [P, D])
        load(nc, ph, [(w1[:, e, :, :], chunks(A["L0_ffn_W1"][e, :, :])) for e in range(N_EXP0)]
             + [(w2[:, e, :, :], chunks(A["L0_ffn_W2"][e, :, :])) for e in range(N_EXP0)]
             + [(b1[:, :, :], A["L0_ffn_b1"].rearrange("p (e m) -> p e m", e=N_EXP0)),
                (b2[:, :, :].rearrange("p e f -> p (e f)"), row(A["L0_ffn_b2"]))])
        hid = [ph.ps(f"hid{i}", [128, M, P]) for i in range(2)]
        y = [ph.ps(f"y{i}", [P, 512]) for i in range(2)]
        h_made, gelued, y_made, added, steps = (ph.sem(n) for n in ("h_made", "gelued", "y_made", "added", "steps"))
        with nc.Block() as block:
            @block.gpsimd
            def _(pool):
                pool_job(pool)

            @block.tensor
            def _(pe):
                pe.sem_inc(y_made, 2)
                with pe.Fori(0, NT) as t:
                    def hidden(e):
                        s = t * N_EXP0 + e
                        pe.wait_ge(gelued, s + 1)
                        for m in range(M):
                            for k in range(KC):
                                ins = nc.tensor.matmul(hid[e % 2][:, m, :], w1[:, e, k, m * 128:(m + 1) * 128],
                                                       xT[:, k, bass.ds(t, 1), :].rearrange("p a f -> p (a f)"),
                                                       start=(k == 0), stop=(k == KC - 1))
                        ins.then_inc(h_made, 1)
                    hidden(0)
                    for e in range(N_EXP0):
                        if e + 1 < N_EXP0:
                            hidden(e + 1)
                        s = t * N_EXP0 + e
                        pe.wait_ge(gelued, s + 3)
                        pe.wait_ge(added, s + 1)
                        for m in range(M):
                            ins = nc.tensor.matmul(y[e % 2][:, 0:D], hT[:, e % 2, m, :], w2[:, e, m, :], start=(m == 0), stop=(m == M - 1))
                        ins.then_inc(y_made, 1)

            @block.scalar
            def _(act):
                act.sem_inc(gelued, 2)
                with act.Fori(0, NT) as t:
                    for e in range(N_EXP0):
                        s = t * N_EXP0 + e
                        act.wait_ge(h_made, s + 1)
                        act.wait_ge(y_made, s + 1)
                        for m in range(M):
                            ins = nc.scalar.activation(hT[:, e % 2, m, :], hid[e % 2][:, m, :], ACT.Gelu, bias=b1[:, e, m:m + 1])
                        ins.then_inc(gelued, 1)

            @block.vector
            def _(dve):
                dve.sem_inc(added, 2)
                with dve.Fori(0, NT) as t:
                    a = x[:, bass.ds(t, 1), :].rearrange("p a f -> p (a f)")
                    chain = Chain(dve, steps, t * (2 * N_EXP0))
                    for e in range(N_EXP0):
                        dve.wait_ge(y_made, t * N_EXP0 + e + 3)
                        chain(nc.vector.tensor_tensor(tmp[:, :], y[e % 2][:, 0:D], b2[:, e, :], ALU.add))
                        dve.sem_inc(added, 1)
                        chain(nc.vector.scalar_tensor_tensor(a, tmp[:, :], gates[:, bass.ds(t, 1), e], a, ALU.mult, ALU.add))


def mix1(nc, cn, A, x, xT, xT_d, kvp, mean, rstd):
    H1 = 2 * D
    with ExitStack() as ctx:
        ph = Phase(nc, ctx, "m1")
        wq, wm = ph.sb("wq", [128, KC, D]), ph.sb("wm", [128, KC, D])
        w1, w2 = ph.sb("w1", [128, 2 * KC, H1]), ph.sb("w2", [128, 2 * KC, D])
        g1, b1, g2, b2 = (ph.sb(n, [P, D]) for n in ("g1", "b1", "g2", "b2"))
        cb, kb, ks, fold = ph.sb("cb", [128, 2, 128]), ph.sb("kb", [128, 2, 128]), ph.sb("ks", [128, 2]), ph.sb("fold", [128, 2, D])
        msg = ph.sb("msg", [P, NT, D])
        load(nc, ph, [(wq[:, :, :], chunks(A["L1_mix_Wq"])), (wm[:, :, :], chunks(A["L1_mix_Wm"])),
                      (w1[:, :, :], chunks(A["L1_mix_W1"])), (w2[:, :, :], chunks(A["L1_mix_W2"])),
                      (g1[:, :], row(A["L1_mix_g1"])), (b1[:, :], row(A["L1_mix_b1"])),
                      (g2[:, :], row(A["L1_mix_g2"])), (b2[:, :], row(A["L1_mix_b2"]))])

        def tile_of(a, t):
            return a[:, bass.ds(t, 1), :].rearrange("p a f -> p (a f)")
        with ExitStack() as inner:
            p2 = Phase(nc, inner, "m2")
            fold_context(nc, p2, cn, kvp, cb, kb, ks, wm, fold)
        with ExitStack() as inner:
            p3 = Phase(nc, inner, "m3")
            linear_attention(nc, p3, cn, xT, wq, kb, fold, (ALU.add, 1e-6),
                             lambda t, psum: nc.vector.tensor_scalar(tile_of(msg, t), psum, 1.0, None, ALU.mult), keep=xT_d)
        with ExitStack() as inner:
            p4 = Phase(nc, inner, "m4")
            mm, mr = p4.sb("mm", [P, NT]), p4.sb("mr", [P, NT])
            layer_norm_stats(nc, p4, mr, mm, msg)
            ma, mc, mn = p4.sb("ma", [P, D]), p4.sb("mc", [P, D]), p4.sb("mn", [P, D])
            mT, hr = p4.sb("mT", [128, KC, P]), p4.sb("hr", [128, 4, P])
            pt, hid, po = p4.ps("pt", [128, KC, P]), p4.ps("hid", [128, 4, P]), p4.ps("po", [P, 512])
            mn_ready, turned, mT_ready, h_made, relued, o_made, kept, steps = (
                p4.sem(n) for n in ("mn_ready", "turned", "mT_ready", "h_made", "relued", "o_made", "kept", "steps"))
            with nc.Block() as block:
                @block.vector
                def _(dve):
                    dve.sem_inc(kept, 1)

                    def norm(t):
                        chain = Chain(dve, steps, t * 2)
                        dve.wait_ge(turned, t + 1)
                        chain(nc.vector.tensor_scalar(ma[:, :], tile_of(msg, t), mm[:, bass.ds(t, 1)], mr[:, bass.ds(t, 1)],
                                                      ALU.subtract, ALU.mult))
                        chain(nc.vector.tensor_tensor(mc[:, :], ma[:, :], g1[:, :], ALU.mult))
                        nc.vector.tensor_tensor(mn[:, :], mc[:, :], b1[:, :], ALU.add).then_inc(mn_ready, 1)

                    def keep(t):
                        dve.wait_ge(o_made, t + 1)
                        nc.vector.tensor_scalar(tile_of(msg, t), po[:, 0:D], 1.0, None, ALU.mult).then_inc(kept, 1)
                    norm(0)
                    with dve.Fori(0, NT - 1) as t:
                        norm(t + 1)
                        keep(t)
                    keep(NT - 1)

                @block.scalar
                def _(act):
                    def fetch(t):
                        act.wait_ge(turned, t + 2)
                        nc.scalar.activation(mT[:, :, :], pt[:, :, :], ACT.Copy).then_inc(mT_ready, 1)

                    def relu(t):
                        act.wait_ge(h_made, t + 1)
                        nc.scalar.activation(hr[:, :, :], hid[:, :, :], ACT.Relu).then_inc(relued, 1)
                    fetch(0)
                    with act.Fori(0, NT - 1) as t:
                        relu(t)
                        fetch(t + 1)
                    relu(NT - 1)

                @block.tensor
                def _(pe):
                    pe.sem_inc(turned, 1)

                    def turn_tile(t):
                        pe.wait_ge(mn_ready, t + 1)
                        for k in range(KC):
                            ins = nc.tensor.matmul(pt[:, k, :], mn[:, k * 128:(k + 1) * 128], cn["ident"][0:P, 0:P], start=True, stop=True)
                        ins.then_inc(turned, 1)

                    def tile(t, last):
                        pe.wait_ge(mT_ready, t + 1)
                        for m in range(4):
                            for k in range(2 * KC):
                                src = (xT[:, k, bass.ds(t, 1), :].rearrange("p a f -> p (a f)") if k < KC else mT[:, k - KC, :])
                                ins = nc.tensor.matmul(hid[:, m, :], w1[:, k, m * 128:(m + 1) * 128], src,
                                                       start=(k == 0), stop=(k == 2 * KC - 1))
                        ins.then_inc(h_made, 1)
                        if not last:
                            turn_tile(t + 1)
                        pe.wait_ge(relued, t + 1)
                        pe.wait_ge(kept, t + 1)
                        for m in range(4):
                            ins = nc.tensor.matmul(po[:, 0:D], hr[:, m, :], w2[:, m, :], start=(m == 0), stop=(m == 3))
                        ins.then_inc(o_made, 1)
                    turn_tile(0)
                    with pe.Fori(0, NT - 1) as t:
                        tile(t, False)
                    tile(NT - 1, True)
        with ExitStack() as inner:
            p5 = Phase(nc, inner, "m5")
            mm, mr = p5.sb("mm", [P, NT]), p5.sb("mr", [P, NT])
            layer_norm_stats(nc, p5, mr, mm, msg)
            xn = p5.sb("xn", [P, NT, D])
            mine = 4 * NT // 5
            scaled, xn_ready = p5.sem("scaled"), p5.sem("xn_ready")

            def all_tiles(a):
                return spread(a[:, :], 1, [P, NT, D])

            with nc.Block() as block:
                @block.vector
                def _(dve):
                    chain = Chain(dve, scaled, NT)
                    with dve.Fori(0, NT) as t:
                        nc.vector.tensor_scalar(tile_of(msg, t), tile_of(msg, t), mm[:, bass.ds(t, 1)], mr[:, bass.ds(t, 1)],
                                                ALU.subtract, ALU.mult).then_inc(scaled, 1)
                    for t in range(mine, NT):
                        nc.vector.tensor_scalar(xn[:, t, :], x[:, t, :], mean[:, t:t + 1], rstd[:, t:t + 1],
                                                ALU.subtract, ALU.mult)
                    dve.wait_ge(scaled, NT)
                    chain(nc.vector.tensor_tensor(msg[:, :, :], msg[:, :, :], all_tiles(g2), ALU.mult))
                    chain(nc.vector.tensor_tensor(msg[:, :, :], msg[:, :, :], all_tiles(b2), ALU.add))
                    dve.wait_ge(xn_ready, mine)
                    chain(nc.vector.tensor_tensor(x[:, :, :], x[:, :, :], msg[:, :, :], ALU.add))
                    chain(nc.vector.tensor_tensor(x[:, :, :], x[:, :, :], xn[:, :, :], ALU.add))

                @block.gpsimd
                def _(pool):
                    for t in range(mine):
                        nc.gpsimd.tensor_scalar(xn[:, t, :], x[:, t, :], mean[:, t:t + 1], rstd[:, t:t + 1],
                                                ALU.subtract, ALU.mult).then_inc(xn_ready, 1)


def relation_attention(nc, ph, cn, A, sT, o_d):
    R, H, W3 = N_REL, 4, 3 * D
    HR = R // 2
    w, bias = ph.sb("w", [128, KC, W3]), ph.sb("bias", [P, D])
    part, ones_b = ph.sb("part", [3, 2, 2, D], BF16), ph.sb("ones_b", [3, P], BF16)
    with ExitStack() as inner:
        p0 = Phase(nc, inner, "rb")
        wide, rest, one = p0.sb("wide", [3, 2, D]), p0.sb("rest", [3, 2, D]), p0.sb("one", [3, 2, D], BF16)
        sel, loaded, steps = p0.sb("sel", [3, 2, D]), p0.sem("loaded"), p0.sem("steps")
        with nc.Block() as block:
            @block.sync
            def _(sp):
                sp.dma_start(w[:, :, :], chunks(A["L1_gnn_in_proj_wT"])).then_inc(loaded, 16)
                sp.dma_start(bias[:, :], row(A["L1_gnn_in_proj_b"][2 * D:W3])).then_inc(loaded, 16)
                sp.dma_start(rest[:, :, :].rearrange("p a f -> p (a f)"), row(A["L1_gnn_in_proj_b"][0:2 * D], 3)).then_inc(loaded, 16)

            @block.vector
            def _(dve):
                chain = Chain(dve, steps)
                nc.vector.memset(ones_b[:, :], 1.0)
                dve.wait_ge(loaded, 48)
                for i in range(3):
                    chain(nc.vector.tensor_copy(one[:, :, :], rest[:, :, :]))
                    chain(nc.vector.tensor_copy(wide[:, :, :], one[:, :, :]))
                    chain(nc.vector.tensor_tensor(rest[:, :, :], rest[:, :, :], wide[:, :, :], ALU.subtract))
                    if i == 0:
                        chain(nc.vector.tensor_scalar(sel[:, :, :], wide[:, :, :], cn["ident"][0:3, i:i + 1], None, ALU.mult))
                    else:
                        chain(nc.vector.scalar_tensor_tensor(sel[:, :, :], wide[:, :, :], cn["ident"][0:3, i:i + 1], sel[:, :, :],
                                                             ALU.mult, ALU.add))
                for qk in range(2):
                    for i in range(2):
                        nc.vector.tensor_copy(part[:, qk, i, :], sel[:, qk, :])
    sc_T = ph.sb("sc_T", [128, R, 2, P])
    q, k, v = ph.sb("q", [P, R, D]), ph.sb("k", [P, R, D]), ph.sb("v", [P, R, D])
    prod, prod_p = ph.sb("prod", [P, HR, D]), ph.sb("prod_p", [P, 2, HR, D])
    sc, ex = ph.sb("sc", [P, H, R, R]), ph.sb("ex", [P, H, R, R])
    mx, sm, rs = ph.sb("mx", [P, H * R]), ph.sb("sm", [P, H * R]), ph.sb("rs", [P, H * R])
    pm, o = ph.sb("pm", [P, H, R]), ph.sb("o", [P, 2, D])
    pk, pq, pv = ([ph.ps(f"p{n}{i}", [P, 2, D]) for i in range(c)] for n, c in (("k", 3), ("q", 3), ("v", 2)))
    fetched, k_made, q_made, v_made, k_kept, q_kept, v_kept = (
        ph.sem(n) for n in ("fetched", "k_made", "q_made", "v_made", "k_kept", "q_kept", "v_kept"))
    shifted, exped, o_ready, stored, steps, gate = (
        ph.sem(n) for n in ("shifted", "exped", "o_ready", "stored", "steps", "gate"))
    p_made, p_ready, p_read, v_used, qk_used = (ph.sem(n) for n in ("p_made", "p_ready", "p_read", "v_used", "qk_used"))
    units = [(r, s) for r in range(R) for s in range(2)]
    own, pools = units[0::2], units[1::2]

    def product(eng, to, u):
        r, s = u
        return eng.tensor_tensor(to, k[:, s * HR:(s + 1) * HR, :], spread(q[:, r, :], 1, [P, HR, D]), ALU.mult)

    def score(src, u, n=D // H):
        r, s = u
        return nc.vector.tensor_reduce(sc[:, :, r, s * HR:(s + 1) * HR].rearrange("p h s -> p s h"),
                                       src.rearrange("p s (h d) -> p s h d", h=H)[:, :, :, 0:n], AX.X, ALU.add)

    with nc.Block() as block:
        @block.gpsimd
        def _(pool):
            with pool.Fori(0, NT) as t:
                pool.wait_ge(k_kept, t * 3 + 6)
                pool.wait_ge(q_kept, t * 3 + 6)
                for i, u in enumerate(pools):
                    pool.wait_ge(p_read, t * len(pools) + i + 1)
                    buf = prod_p[:, i % 2, :, :]
                    product(nc.gpsimd, buf, u).then_inc(p_made, 1)
                    pool.wait_ge(p_made, t * len(pools) + i + 1)
                    hd = buf.rearrange("p s (h d) -> p s h d", h=H)
                    nc.gpsimd.tensor_tensor(hd[:, :, :, 0:D // H // 2], hd[:, :, :, 0:D // H // 2], hd[:, :, :, D // H // 2:],
                                            ALU.add).then_inc(p_ready, 1)

        @block.tensor
        def _(pe):
            pe.sem_inc(v_made, 1)
            with pe.Fori(0, NT) as t:
                pe.wait_ge(fetched, t + 1)
                for banks, col, made, kept in ((pk, D, k_made, k_kept), (pq, 0, q_made, q_kept)):
                    for i in range(3):
                        pe.wait_ge(kept, t * 3 + i + 1)
                        nc.tensor.matmul(banks[i][:, :, :].rearrange("p r f -> p (r f)"), ones_b[:, :],
                                         part[:, col // D, :, :].rearrange("p r f -> p (r f)"), start=True, stop=False,
                                         skip_group_check=True)
                        for r in (2 * i, 2 * i + 1):
                            for c in range(KC):
                                ins = nc.tensor.matmul(banks[i][:, r % 2, :], sc_T[:, r, c, :], w[:, c, col:col + D],
                                                       start=False, stop=(r % 2 == 1 and c == KC - 1), skip_group_check=True)
                        ins.then_inc(made, 1)
                for i in range(3):
                    pe.wait_ge(v_kept, t * 3 + i + 1)
                    for r in (2 * i, 2 * i + 1):
                        for c in range(KC):
                            ins = nc.tensor.matmul(pv[i % 2][:, r % 2, :], sc_T[:, r, c, :], w[:, c, 2 * D:W3],
                                                   start=(c == 0), stop=(c == KC - 1))
                    ins.then_inc(v_made, 1)

        @block.scalar
        def _(act):
            act.sem_inc(v_kept, 2)
            act.sem_inc(k_kept, 3)
            act.sem_inc(q_kept, 3)

            def keep(t):
                act.wait_ge(qk_used, t + 1)
                for banks, to, made, kept in ((pk, k, k_made, k_kept), (pq, q, q_made, q_kept)):
                    for i in range(3):
                        act.wait_ge(made, t * 3 + i + 1)
                        nc.scalar.activation(to[:, 2 * i:2 * i + 2, :], banks[i][:, :, :], ACT.Copy).then_inc(kept, 1)

            def fetch(t):
                act.wait_ge(v_made, t * 3 + 1)
                act.sem_inc(gate, 1)
                nc.scalar.activation(sc_T[:, :, :, :].rearrange("p r h f -> p r (h f)"), sT[:, bass.ds(t * R, R), :],
                                     ACT.Copy).then_inc(fetched, 1)

            def tile(t, last):
                act.wait_ge(v_used, t + 1)
                for i in range(3):
                    act.wait_ge(v_made, t * 3 + i + 2)
                    nc.scalar.activation(v[:, 2 * i:2 * i + 2, :], pv[i % 2][:, :, :], ACT.Copy).then_inc(v_kept, 1)
                if not last:
                    fetch(t + 1)
                act.wait_ge(shifted, t + 1)
                nc.scalar.activation(ex[:, :, :, :], sc[:, :, :, :], ACT.Exp, scale=float(D // H) ** -0.5).then_inc(exped, 1)
                if not last:
                    keep(t + 1)
            fetch(0)
            keep(0)
            with act.Fori(0, NT - 1) as t:
                tile(t, False)
            tile(NT - 1, True)

        @block.vector
        def _(dve):
            dve.sem_inc(qk_used, 1)
            dve.sem_inc(v_used, 1)
            dve.sem_inc(p_read, 2)
            per = 2 * len(own) + 11
            with dve.Fori(0, NT) as t:
                chain = Chain(dve, steps, t * per)
                dve.wait_ge(k_kept, t * 3 + 6)
                dve.wait_ge(q_kept, t * 3 + 6)
                for i, u in enumerate(own):
                    product(nc.vector, prod[:, :, :], u).then_inc(steps, 1)
                    chain.n += 1
                    dve.wait_ge(p_ready, t * len(pools) + i + 1)
                    score(prod_p[:, i % 2, :, :], pools[i], D // H // 2).then_inc(p_read, 1)
                    dve.wait_ge(steps, t * per + chain.n)
                    chain(score(prod[:, :, :], u))
                dve.wait_ge(p_read, (t + 1) * len(pools) + 2)
                dve.sem_inc(qk_used, 1)
                flat = sc[:, :, :, :].rearrange("p h r s -> p (h r) s")
                eflat = ex[:, :, :, :].rearrange("p h r s -> p (h r) s")
                chain(nc.vector.tensor_reduce(mx[:, :], flat, AX.X, ALU.max))
                nc.vector.tensor_tensor(flat, flat, spread(mx[:, :], 2, [P, H * R, R]), ALU.subtract).then_inc(shifted, 1)
                dve.wait_ge(exped, t + 1)
                chain(nc.vector.tensor_reduce(sm[:, :], eflat, AX.X, ALU.add))
                chain(nc.vector.reciprocal(rs[:, :], sm[:, :]))
                chain(nc.vector.tensor_tensor(eflat, eflat, spread(rs[:, :], 2, [P, H * R, R]), ALU.mult))
                chain(nc.vector.tensor_reduce(pm[:, :, :], ex[:, :, :, :].rearrange("p h r s -> p h s r"), AX.X, ALU.add))
                chain(nc.vector.tensor_scalar(pm[:, :, :], pm[:, :, :], 1.0 / R, None, ALU.mult))
                dve.wait_ge(v_kept, t * 3 + 5)
                dve.wait_ge(stored, t * 16 + 16)
                for s in range(2):
                    src = slice(s * HR, (s + 1) * HR)
                    chain(nc.vector.tensor_tensor(prod[:, :, :].rearrange("p s (h d) -> p s h d", h=H),
                                                  v[:, src, :].rearrange("p s (h d) -> p s h d", h=H),
                                                  spread(pm[:, :, src].rearrange("p h s -> p s h"), 3, [P, HR, H, D // H]), ALU.mult))
                    if s == 1:
                        dve.sem_inc(v_used, 1)
                    chain(nc.vector.tensor_reduce(o[:, s, :], prod[:, :, :].rearrange("p s f -> p f s"), AX.X, ALU.add))
                nc.vector.tensor_tensor(o[:, 0, :], o[:, 0, :], o[:, 1, :], ALU.add).then_inc(steps, 1)
                chain.n += 1
                dve.wait_ge(steps, t * per + chain.n)
                nc.vector.tensor_tensor(o[:, 0, :], o[:, 0, :], bias[:, :], ALU.add).then_inc(o_ready, 1)
                assert chain.n == per, chain.n

        @block.sync
        def _(sp):
            sp.sem_inc(stored, 16)
            with sp.Fori(0, NT) as t:
                sp.wait_ge(o_ready, t + 1)
                sp.dma_start(rows(o_d)[:, bass.ds(t, 1), :].rearrange("p a f -> p (a f)"), o[:, 0, :]).then_inc(stored, 16)
            sp.wait_ge(stored, 16 * NT + 16)


def relation_output(nc, ph, cn, A, x, xT, x_d, xT_d, o_d):
    wo, wp = ph.sb("wo", [128, KC, D]), ph.sb("wp", [128, KC, D])
    ab, pb = ph.sb("ab", [128, KC]), ph.sb("pb", [P, D])
    load(nc, ph, [(x[:, :, :], rows(x_d)), (xT[:, :, :, :].rearrange("p k t f -> p (k t f)"), xT_d),
                  (wo[:, :, :], chunks(A["L1_gnn_attn_out_wT"])), (wp[:, :, :], chunks(A["L1_gnn_proj_wT"])),
                  (ab[:, :], A["L1_gnn_attn_out_b"]), (pb[:, :], row(A["L1_gnn_proj_b"]))])
    o_all = ph.sb("o_all", [P, NT, D])
    oc, oT, sT = ph.sb("oc", [P, D]), ph.sb("oT", [128, KC, P]), ph.sb("sT", [128, KC, P])
    pt, pa, po = ph.ps("pt", [128, KC, P]), ph.ps("pa", [128, KC, P]), ph.ps("po", [P, 512])
    cut, turned, oT_ready, a_made, sT_ready, o_made, added, steps, gate = (
        ph.sem(n) for n in ("cut", "turned", "oT_ready", "a_made", "sT_ready", "o_made", "added", "steps", "gate"))
    loaded = ph.sem("loaded")
    with nc.Block() as block:
        @block.sync
        def _(sp):
            sp.dma_start(o_all[:, :, :], rows(o_d)).then_inc(loaded, 16)

        @block.gpsimd
        def _(pool):
            pool.wait_ge(loaded, 16)
            with pool.Fori(0, NT) as t:
                pool.wait_ge(turned, t + 1)
                pool.sem_inc(gate, 1)
                nc.gpsimd.tensor_copy(oc[:, :], o_all[:, bass.ds(t, 1), :].rearrange("p a f -> p (a f)")).then_inc(cut, 1)

        @block.tensor
        def _(pe):
            pe.sem_inc(turned, 1)
            pe.sem_inc(added, 1)

            def turn_tile(t):
                pe.wait_ge(cut, t + 1)
                for k in range(KC):
                    ins = nc.tensor.matmul(pt[:, k, :], oc[:, k * 128:(k + 1) * 128], cn["ident"][0:P, 0:P], start=True, stop=True)
                ins.then_inc(turned, 1)

            def tile(t, last):
                pe.wait_ge(oT_ready, t + 1)
                for h in range(2):
                    for k in range(KC):
                        ins = nc.tensor.matmul(pa[:, h, :], wo[:, k, h * 128:(h + 1) * 128], oT[:, k, :], start=(k == 0), stop=(k == KC - 1))
                ins.then_inc(a_made, 1)
                if not last:
                    turn_tile(t + 1)
                pe.wait_ge(sT_ready, t + 1)
                pe.wait_ge(added, t + 1)
                for k in range(KC):
                    ins = nc.tensor.matmul(po[:, 0:D], sT[:, k, :], wp[:, k, :], start=(k == 0), stop=(k == KC - 1))
                ins.then_inc(o_made, 1)
            turn_tile(0)
            with pe.Fori(0, NT - 1) as t:
                tile(t, False)
            tile(NT - 1, True)

        @block.scalar
        def _(act):
            act.sem_inc(a_made, 1)
            with act.Fori(0, NT) as t:
                act.wait_ge(turned, t + 2)
                act.wait_ge(a_made, t + 1)
                nc.scalar.activation(oT[:, :, :], pt[:, :, :], ACT.Copy).then_inc(oT_ready, 1)

        @block.vector
        def _(dve):
            with dve.Fori(0, NT) as t:
                a = x[:, bass.ds(t, 1), :].rearrange("p a f -> p (a f)")
                nc.vector.tensor_tensor(a, a, pb[:, :], ALU.add).then_inc(steps, 1)
                dve.wait_ge(a_made, t + 2)
                for h in range(KC):
                    ins = nc.vector.scalar_tensor_tensor(sT[:, h, :], pa[:, h, :], ab[:, h:h + 1],
                                                         xT[:, h, bass.ds(t, 1), :].rearrange("p a f -> p (a f)"), ALU.add, ALU.add)
                ins.then_inc(sT_ready, 1)
                dve.wait_ge(steps, t + 1)
                dve.wait_ge(o_made, t + 1)
                nc.vector.tensor_tensor(a, a, po[:, 0:D], ALU.add).then_inc(added, 1)


def in_pairs(eng, count, do):
    with eng.Fori(0, count // 2) as i:
        for s in range(2):
            do(i * 2 + s, s, i)
    if count % 2:
        do(count - 1, 0, count // 2)


class Hidden:

    def __init__(self, nc, ph, cn, w1, b1, n, tiles):
        self.nc, self.cn, self.w1, self.b1, self.n, self.tiles = nc, cn, w1, b1, n, tiles
        self.M = HID1 // 128
        self.rows, self.rT = ph.sb("rows", [n, 2, D]), ph.sb("rT", [128, KC, n])
        self.hT = ph.sb("hT", [128, 2, self.M, n])
        self.pt = ph.ps("pt", [128, KC, n])
        self.hid = [[ph.ps(f"hid{s}{i}", [128, self.M // 2, n]) for i in range(2)] for s in range(2)]
        self.turned, self.rT_ready, self.h_made, self.gelued, self.h_used = (
            ph.sem(k) for k in ("turned", "rT_ready", "h_made", "gelued", "h_used"))

    def tensor(self, pe, wait_rows, use):
        nc, n, M = self.nc, self.n, self.M

        def turn(t, s, i):
            wait_rows(t, s, i)
            for k in range(KC):
                ins = nc.tensor.matmul(self.pt[:, k, :], self.rows[:, s, k * 128:(k + 1) * 128], self.cn["ident"][0:n, 0:n],
                                       start=True, stop=True)
            ins.then_inc(self.turned, 1)

        def hidden(t, s):
            pe.wait_ge(self.rT_ready, t + 1)
            for m in range(M):
                for k in range(KC):
                    ins = nc.tensor.matmul(self.hid[s][m // 4][:, m % 4, :], self.w1[:, k, m * 128:(m + 1) * 128],
                                           self.rT[:, k, :], start=(k == 0), stop=(k == KC - 1))
            ins.then_inc(self.h_made, 1)

        def used(t, s, i):
            pe.wait_ge(self.gelued, t + 1)
            use(t, s, i).then_inc(self.h_used, 1)

        def tile(t, s, i):
            hidden(t + 1, 1 - s)
            turn(t + 2, s, i + 1)
            used(t, s, i)
        pe.sem_inc(self.h_used, 2)
        turn(0, 0, 0)
        hidden(0, 0)
        turn(1, 1, 0)
        in_pairs(pe, self.tiles - 2, tile)
        last = self.tiles - 1
        hidden(last, last % 2)
        used(last - 1, (last - 1) % 2, (last - 1) // 2)
        used(last, last % 2, last // 2)

    def scalar(self, act):
        def fetch(t):
            act.wait_ge(self.turned, t + 1)
            self.nc.scalar.activation(self.rT[:, :, :], self.pt[:, :, :], ACT.Copy).then_inc(self.rT_ready, 1)

        def gelu(t, s):
            act.wait_ge(self.h_made, t + 1)
            act.wait_ge(self.h_used, t + 1)
            for m in range(self.M):
                ins = self.nc.scalar.activation(self.hT[:, s, m, :], self.hid[s][m // 4][:, m % 4, :], ACT.Gelu,
                                                bias=self.b1[:, m:m + 1])
            ins.then_inc(self.gelued, 1)

        def tile(t, s, i):
            fetch(t + 1)
            gelu(t, s)
        fetch(0)
        in_pairs(act, self.tiles - 1, tile)
        gelu(self.tiles - 1, (self.tiles - 1) % 2)


def expert_logits(nc, ph, cn, x, mean, rstd, w1, b1, wg, bg, lg):
    hd = Hidden(nc, ph, cn, w1, b1, P, NT)
    plg = [ph.ps(f"plg{s}", [P, N_EXP1]) for s in range(2)]
    normed, kept = ph.sem("normed"), ph.sem("kept")
    with nc.Block() as block:
        @block.tensor
        def _(pe):
            def use(t, s, i):
                pe.wait_ge(kept, t + 1)
                for m in range(hd.M):
                    ins = nc.tensor.matmul(plg[s][:, :], hd.hT[:, s, m, :], wg[:, m, :], start=(m == 0), stop=(m == hd.M - 1))
                return ins
            hd.tensor(pe, lambda t, s, i: pe.wait_ge(normed, t + 1), use)

        @block.scalar
        def _(act):
            hd.scalar(act)

        @block.vector
        def _(dve):
            dve.sem_inc(kept, 2)

            def norm(t, s):
                nc.vector.tensor_scalar(hd.rows[:, s, :], x[:, bass.ds(t, 1), :].rearrange("p a f -> p (a f)"),
                                        mean[:, bass.ds(t, 1)], rstd[:, bass.ds(t, 1)], ALU.subtract, ALU.mult).then_inc(normed, 1)

            def keep(t, s, i):
                dve.wait_ge(hd.h_used, t + 3)
                nc.vector.tensor_tensor(lg[:, bass.ds(t, 1), :].rearrange("p a f -> p (a f)"), plg[s][:, :], bg[:, :],
                                        ALU.add).then_inc(kept, 1)

            def tile(t, s, i):
                dve.wait_ge(hd.turned, t + 1)
                norm(t + 2, s)
                keep(t, s, i)
            norm(0, 0)
            norm(1, 1)
            in_pairs(dve, NT - 2, tile)
            for t in (NT - 2, NT - 1):
                keep(t, t % 2, t // 2)


def expert_places(nc, ph, cn, x, mean, rstd, lg, pm, pos, tb, xn, sorted_d):
    E, ST = N_EXP1, tb.shape[1]
    ex, pr, far, sel, upto, at = (ph.sb(n, [P, NT, E]) for n in ("ex", "pr", "far", "sel", "upto", "at"))
    mx, sm, rs, first, posf = (ph.sb(n, [P, NT]) for n in ("mx", "sm", "rs", "first", "posf"))
    lots, ends, start = (ph.sb(n, [P, E]) for n in ("lots", "ends", "start"))
    tbf = ph.sb("tbf", [1, ST])
    tot, pre = ph.ps("tot", [128, 512]), ph.ps("pre", [128, 512])
    steps, shifted, exped, chosen, counted, placed, normed, scattered = (
        ph.sem(n) for n in ("steps", "shifted", "exped", "chosen", "counted", "placed", "normed", "scattered"))

    def all8(a):
        return spread(a[:, :], 2, [P, NT, E])

    def by_node(a):
        return spread(a[:, :], 1, [P, NT, E])
    with nc.Block() as block:
        @block.vector
        def _(dve):
            chain = Chain(dve, steps)
            expert = spread(cn["ramp"][0:P, 0:E], 1, [P, NT, E])
            chain(nc.vector.tensor_reduce(mx[:, :], lg[:, :, :], AX.X, ALU.max))
            nc.vector.tensor_tensor(lg[:, :, :], lg[:, :, :], all8(mx), ALU.subtract).then_inc(shifted, 1)
            for t in range(NT):
                nc.vector.tensor_scalar(xn[:, t, :], x[:, t, :], mean[:, t:t + 1], rstd[:, t:t + 1],
                                        ALU.subtract, ALU.mult).then_inc(normed, 1)
            dve.wait_ge(exped, 1)
            chain(nc.vector.tensor_reduce(sm[:, :], ex[:, :, :], AX.X, ALU.add))
            chain(nc.vector.reciprocal(rs[:, :], sm[:, :]))
            chain(nc.vector.tensor_tensor(pr[:, :, :], ex[:, :, :], all8(rs), ALU.mult))
            chain(nc.vector.tensor_reduce(pm[:, :], pr[:, :, :], AX.X, ALU.max))
            chain(nc.vector.tensor_tensor(far[:, :, :], pr[:, :, :], all8(pm), ALU.not_equal))
            chain(nc.vector.scalar_tensor_tensor(sel[:, :, :], far[:, :, :], 100.0, expert, ALU.mult, ALU.add))
            chain(nc.vector.tensor_reduce(first[:, :], sel[:, :, :], AX.X, ALU.min))
            nc.vector.tensor_tensor(sel[:, :, :], expert, all8(first), ALU.is_equal).then_inc(chosen, 1)
            dve.wait_ge(counted, 1)
            totv = tot[0:P, 0:NT * E].rearrange("p (t e) -> p t e", e=E)
            prev = pre[0:P, 0:NT * E].rearrange("p (t e) -> p t e", e=E)
            for e in range(E):
                ins = nc.vector.tensor_tensor_scan(upto[:, :, e], cn["one_row"][0:P, 0:NT], totv[:, :, e], 0.0, ALU.mult, ALU.add)
            chain(ins)
            chain(nc.vector.tensor_scalar(lots[:, :], upto[:, NT - 1, :], 1.0 / 128, -127.0 / 256, ALU.mult, ALU.add))
            chain(nc.vector.tensor_scalar(lots[:, :], lots[:, :], ROUND, None, ALU.add))
            chain(nc.vector.tensor_scalar(lots[:, :], lots[:, :], -ROUND, 1.0, ALU.add, ALU.add))
            chain(nc.vector.tensor_tensor_scan(ends[:, :], cn["one_row"][0:P, 0:E], lots[:, :], 0.0, ALU.mult, ALU.add))
            chain(nc.vector.tensor_tensor(start[:, :], ends[:, :], lots[:, :], ALU.subtract))
            chain(nc.vector.tensor_tensor(at[:, :, :], upto[:, :, :], totv, ALU.subtract))
            chain(nc.vector.tensor_tensor(at[:, :, :], at[:, :, :], prev, ALU.add))
            chain(nc.vector.scalar_tensor_tensor(at[:, :, :], by_node(start), 128.0, at[:, :, :], ALU.mult, ALU.add))
            chain(nc.vector.tensor_tensor(at[:, :, :], at[:, :, :], sel[:, :, :], ALU.mult))
            chain(nc.vector.tensor_reduce(posf[:, :], at[:, :, :], AX.X, ALU.add))
            nc.vector.tensor_copy(pos[:, :], posf[:, :]).then_inc(placed, 1)
            chain(nc.vector.memset(tbf[:, :], -1.0))
            for e in range(E):
                chain(nc.vector.scalar_tensor_tensor(tbf[:, :], cn["ramp"][0:1, 0:ST], start[0:1, e:e + 1], tbf[:, :],
                                                     ALU.is_ge, ALU.add))
            nc.vector.tensor_copy(tb[:, :], tbf[:, :])

        @block.scalar
        def _(act):
            act.wait_ge(shifted, 1)
            nc.scalar.activation(ex[:, :, :], lg[:, :, :], ACT.Exp).then_inc(exped, 1)

        @block.tensor
        def _(pe):
            pe.wait_ge(chosen, 1)
            flat = sel[:, :, :].rearrange("p t e -> p (t e)")
            nc.tensor.matmul(tot[:, 0:NT * E], cn["ones"][0:P, :], flat, start=True, stop=True)
            nc.tensor.matmul(pre[:, 0:NT * E], cn["tri"][0:P, :], flat, start=True, stop=True).then_inc(counted, 1)

        @block.gpsimd
        def _(pool):
            pool.wait_ge(normed, NT)
            pool.wait_ge(placed, 1)
            for t in range(NT):
                nc.gpsimd.indirect_dma_start(sorted_d, bass.IndirectOffsetOnAxis(ap=pos[:, t:t + 1], axis=0),
                                             xn[:, t, :], None).then_inc(scattered, 16)
            pool.wait_ge(scattered, NT * 16)


def expert_outputs(nc, ph, cn, w1, b1, wd, bd, tb, sorted_d, y_d):
    ST = tb.shape[1]
    hd = Hidden(nc, ph, cn, w1, b1, 128, ST)
    y, ysb = [ph.ps(f"y{s}", [128, 512]) for s in range(2)], ph.sb("ysb", [128, 2, D])
    loaded, stored = [ph.sem(f"loaded{s}") for s in range(2)], [ph.sem(f"stored{s}") for s in range(2)]
    y_ready = ph.sem("y_ready")
    x_rows, y_rows = (d.rearrange("(t p) f -> p t f", p=128) for d in (sorted_d, y_d))

    def number(name, t):
        return tile_numbers(nc, name, tb, t, 1)[0]
    with nc.Block() as block:
        @block.tensor
        def _(pe):
            def use(t, s, i):
                e = number("tensor", t)
                pe.wait_ge(y_ready, t + 1)
                for m in range(hd.M):
                    ins = nc.tensor.matmul(y[s][:, 0:D], hd.hT[:, s, m, :], wd[:, m, bass.ds(e, 1), :].rearrange("p a f -> p (a f)"),
                                           start=(m == 0), stop=(m == hd.M - 1))
                return ins
            hd.tensor(pe, lambda t, s, i: pe.wait_ge(loaded[s], i * 16 + 16), use)

        @block.scalar
        def _(act):
            hd.scalar(act)

        @block.vector
        def _(dve):
            dve.sem_inc(y_ready, 2)

            def tile(t, s, i):
                e = number("vector", t)
                dve.wait_ge(hd.h_used, t + 3)
                dve.wait_ge(stored[s], i * 16 + 16)
                nc.vector.tensor_tensor(ysb[:, s, :], y[s][:, 0:D], bd[:, bass.ds(e, 1), :].rearrange("p a f -> p (a f)"),
                                        ALU.add).then_inc(y_ready, 1)
            in_pairs(dve, ST, tile)

        @block.sync
        def _(sp):
            for s in range(2):
                sp.sem_inc(stored[s], 16)

            def fetch(t, s):
                sp.dma_start(hd.rows[:, s, :], x_rows[:, bass.ds(t, 1), :].rearrange("p a f -> p (a f)")).then_inc(loaded[s], 16)

            def store(t, s, i):
                sp.wait_ge(y_ready, t + 3)
                sp.dma_start(y_rows[:, bass.ds(t, 1), :].rearrange("p a f -> p (a f)"), ysb[:, s, :]).then_inc(stored[s], 16)

            def tile(t, s, i):
                sp.wait_ge(hd.turned, t + 1)
                fetch(t + 2, s)
                store(t, s, i)
            fetch(0, 0)
            fetch(1, 1)
            in_pairs(sp, ST - 2, tile)
            for t in (ST - 2, ST - 1):
                store(t, t % 2, t // 2)
            for s in range(2):
                sp.wait_ge(stored[s], (ST // 2 + 1) * 16)


def expert_sum(nc, ph, x, pm, pos, ye, y_d, out):
    G = 5
    gathered = [ph.sem(f"gathered{g}") for g in range(NT // G)]
    summed, stored = ph.sem("summed"), ph.sem("stored")
    with nc.Block() as block:
        @block.gpsimd
        def _(pool):
            for t in range(NT):
                nc.gpsimd.indirect_dma_start(ye[:, t, :], None, y_d, bass.IndirectOffsetOnAxis(ap=pos[:, t:t + 1], axis=0)
                                             ).then_inc(gathered[t // G], 16)

        @block.vector
        def _(dve):
            for g in range(NT // G):
                dve.wait_ge(gathered[g], 16 * G)
                for t in range(g * G, g * G + G):
                    ins = nc.vector.scalar_tensor_tensor(x[:, t, :], ye[:, t, :], pm[:, t:t + 1], x[:, t, :], ALU.mult, ALU.add)
                ins.then_inc(summed, 1)

        @block.sync
        def _(sp):
            for g in range(NT // G):
                sp.wait_ge(summed, g + 1)
                sp.dma_start(rows(out)[:, g * G:g * G + G, :], x[:, g * G:g * G + G, :]).then_inc(stored, 16)
            sp.wait_ge(stored, NT // G * 16)


def experts1(nc, cn, A, x, sorted_d, y_d, out):
    M, E = HID1 // 128, N_EXP1
    ST = sorted_d.shape[0] // 128
    with ExitStack() as ctx:
        ph = Phase(nc, ctx, "f1")
        mean, rstd = ph.sb("mean", [P, NT]), ph.sb("rstd", [P, NT])
        w1, wg, wd = ph.sb("w1", [128, KC, HID1]), ph.sb("wg", [128, M, E]), ph.sb("wd", [128, M, E, D])
        b1, bg, bd = ph.sb("b1", [128, M]), ph.sb("bg", [P, E]), ph.sb("bd", [128, E, D])
        lg, pm, pos = ph.sb("lg", [P, NT, E]), ph.sb("pm", [P, NT]), ph.sb("pos", [P, NT], I32)
        tb, nodes = ph.sb("tb", [1, ST], I32), ph.sb("nodes", [P, NT, D])
        with ExitStack() as inner:
            p1 = Phase(nc, inner, "f0")
            zero, zeroed, cleared = p1.sb("zero", [128, ST // 4, D]), p1.sem("zeroed"), p1.sem("cleared")
            with nc.Block() as block:
                @block.vector
                def _(dve):
                    nc.vector.memset(zero[:, :, :], 0.0).then_inc(zeroed, 1)

                @block.sync
                def _(sp):
                    sp.wait_ge(zeroed, 1)
                    for q in range(4):
                        sp.dma_start(sorted_d.rearrange("(q p t) f -> q p t f", q=4, p=128)[q], zero[:, :, :]).then_inc(cleared, 16)
                    sp.wait_ge(cleared, 64)
        layer_norm_stats(nc, ph, rstd, mean, x,
                         loads=[(w1[:, :, :], chunks(A["L1_ffn_W1"])), (wg[:, :, :], chunks(A["L1_ffn_Wg"])),
                      (b1[:, :], A["L1_ffn_b1"]), (bg[:, :], row(A["L1_ffn_bg"])),
                      (bd[:, :, :].rearrange("p e f -> p (e f)"), row(A["L1_ffn_bd"], 128))]
             + [(wd[:, :, e, :], chunks(A["L1_ffn_Wd"][e, :, :])) for e in range(E)])
        with ExitStack() as inner:
            expert_logits(nc, Phase(nc, inner, "f2"), cn, x, mean, rstd, w1, b1, wg, bg, lg)
        with ExitStack() as inner:
            expert_places(nc, Phase(nc, inner, "f3"), cn, x, mean, rstd, lg, pm, pos, tb, nodes, sorted_d)
        with ExitStack() as inner:
            expert_outputs(nc, Phase(nc, inner, "f4"), cn, w1, b1, wd, bd, tb, sorted_d, y_d)
        with ExitStack() as inner:
            expert_sum(nc, Phase(nc, inner, "f5"), x, pm, pos, nodes, y_d, out)


def move(nc, ctx, name, pairs):
    ph = Phase(nc, ctx, name)
    moved = ph.sem("moved")
    with nc.Block() as block:
        @block.sync
        def _(sp):
            for to, src in pairs:
                sp.dma_start(to, src).then_inc(moved, 16)
            sp.wait_ge(moved, 16 * len(pairs))


def gps_kernel(nc, A, out):
    with ExitStack() as ctx:
        def sb(name, shape, dt=F32):
            return ctx.enter_context(nc.sbuf_tensor(name, shape, dt))

        def dram(name, shape):
            return nc.dram_tensor(name, shape, F32, kind="Internal").ap()
        cn = {"ident": sb("ident", [128, 128]), "ones": sb("ones", [128, 128]), "tri": sb("tri", [128, 128]),
              "blocks": sb("blocks", [128, 128]), "ramp": sb("ramp", [128, 576]), "part": sb("part", [128, 1]),
              "zeros": sb("zeros", [128, 258]), "one_row": sb("one_row", [128, 150])}
        make_constants(nc, cn)
        x_d, xT_d, o_d = dram("x_kept", [N, D]), dram("xT_kept", [128, KC * N]), dram("attended", [N, D])
        support_d, hs_d, trans_d = dram("support", [N, D]), dram("gat_rows", [N, 32]), dram("transformed", [N_REL * N, D])
        kept_c = sb("tab_c", [128, 576, 2], I32), sb("tb_c", [1, 576], I32)
        with ExitStack() as mid:
            x = mid.enter_context(nc.sbuf_tensor("x", [P, NT, D], F32))
            xT = mid.enter_context(nc.sbuf_tensor("xT", [128, KC, NT, P], F32))
            gates = mid.enter_context(nc.sbuf_tensor("gates", [P, NT, 4], F32))
            keep_a, keep_b = Phase(nc, mid, "ka"), Phase(nc, mid, "kb")
            by_src = Sorting(nc, keep_a, keep_a, P, E_GRAPH // P, 25, NT, 448, 4, A["src"], A["dst"], weight_d=A["edge_weight"])
            by_key = Sorting(nc, keep_b, keep_b, 128, E_GAT // 128, 32, NT, 288, 2, A["L0_ffn_edge_index"][1, :],
                             A["L0_ffn_edge_index"][0, :])
            work_c = Phase(nc, mid, "wc")
            by_rel = Sorting(nc, work_c, work_c, P, E_GRAPH // P, 25, NT * N_REL, 576, 2, A["dst"], A["src"],
                             type_d=A["edge_type_6"], kept=kept_c)
            with ExitStack() as inner:
                sort_addresses(nc, inner, cn, "a", [by_src])
            def rounds_of(first, last):
                return lambda pool: by_src.scatter(pool, first, last)
            layer0(nc, cn, A, x, xT, support_d, [rounds_of(0, 1), rounds_of(1, 6), rounds_of(6, 10)])

            def rest(pool):
                by_src.scatter(pool, 10, by_src.rounds)
                by_key.scatter(pool, 0, by_key.rounds - 2)
            with ExitStack() as inner:
                sort_addresses(nc, inner, cn, "bc", [by_key, by_rel], rest)
            with ExitStack() as inner:
                reload_tables(nc, Phase(nc, inner, "rl"), [by_src])
            with ExitStack() as inner:
                aggregate(nc, Phase(nc, inner, "ag"), cn, by_src, support_d, x, True, False)
            gating(nc, cn, A, x, xT, gates, hs_d, by_key,
                   [lambda pool: by_key.scatter(pool, by_key.rounds - 2, by_key.rounds), lambda pool: by_rel.scatter(pool, 0, 4), lambda pool: by_rel.scatter(pool, 4, 10)])
            experts0(nc, cn, A, x, xT, gates, lambda pool: by_rel.scatter(pool, 10, by_rel.rounds))
            with ExitStack() as inner:
                ph = Phase(nc, inner, "c1")
                mean, rstd = ph.sb("mean", [P, NT]), ph.sb("rstd", [P, NT])
                kvp = ph.ps("kvp", [128, 258])
                with ExitStack() as deep:
                    p2 = Phase(nc, deep, "c2")
                    w = p2.sb("w", [128, KC, 2 * D + N_REL * D])
                    bias, tr = p2.sb("bias", [P, N_REL * D]), p2.sb("tr", [P, 2, N_REL, D])
                    k_sb, v_sb = p2.sb("k", [P, 2, D]), p2.sb("v", [P, 2, D])
                    by_tile = trans_d.rearrange("(r t p) f -> p t r f", r=N_REL, p=P)
                    layer_norm_stats(nc, p2, rstd, mean, x,
                                     loads=[(w[:, :, 0:D], chunks(A["L1_mix_Wk"])), (w[:, :, D:2 * D], chunks(A["L1_mix_Wv"])),
                                  (w[:, :, 2 * D:], chunks(A["L1_gnn_W"])), (bias[:, :], row(A["L1_gnn_b"]))])

                    def part(b):
                        rs = slice(2 * b - 2, 2 * b)
                        return ((512 * b, 512, "bias", lambda t, s: tr[:, s, rs, :].rearrange("p r f -> p (r f)"),
                                 bias[:, 512 * b - 512:512 * b]),
                                (b, lambda t: by_tile[:, bass.ds(t, 1), rs, :].rearrange("p a r f -> p (a r) f"),
                                 lambda s: tr[:, s, rs, :]))
                    parts = [part(b) for b in range(1, 4)]
                    project(nc, p2, cn, x, mean, rstd, xT, w, 2 * D + N_REL * D,
                            [(0, D, "elu", lambda t, s: k_sb[:, s, :], None), (D, D, "copy", lambda t, s: v_sb[:, s, :], None)]
                            + [p[0] for p in parts], [p[1] for p in parts], kv=(kvp, k_sb, v_sb), copies=1)
                mix1(nc, cn, A, x, xT, xT_d, kvp, mean, rstd)
                move(nc, inner, "keep", [(rows(x_d), x[:, :, :])])
        with ExitStack() as mid:
            ph = Phase(nc, mid, "r1")
            sT = ph.sb("sT", [128, NT * N_REL, 2 * P])
            with ExitStack() as inner:
                p2 = Phase(nc, inner, "r2")
                half = NT * N_REL * 9 // 16
                reloaded = p2.sem("reloaded")
                with nc.Block() as block:
                    @block.sync
                    def _(sp):
                        sp.dma_start(by_rel.tab[:, :, :], by_rel.table.rearrange("(p t) f -> p t f", p=128)).then_inc(reloaded, 16)
                        sp.wait_ge(reloaded, 16)

                    @block.vector
                    def _(dve):
                        nc.vector.memset(sT[:, 0:half, :], 0.0)

                    @block.gpsimd
                    def _(pool):
                        nc.gpsimd.memset(sT[:, half:, :], 0.0)
                aggregate(nc, Phase(nc, inner, "r4"), cn, by_rel, trans_d, sT, False, True)
            with ExitStack() as inner:
                relation_attention(nc, Phase(nc, inner, "r5"), cn, A, sT, o_d)
        with ExitStack() as mid:
            x = mid.enter_context(nc.sbuf_tensor("x_again", [P, NT, D], F32))
            with ExitStack() as inner:
                xT = inner.enter_context(nc.sbuf_tensor("xT_again", [128, KC, NT, P], F32))
                relation_output(nc, Phase(nc, inner, "r6"), cn, A, x, xT, x_d, xT_d, o_d)
            slots = (N // 128 + N_EXP1) * 128
            experts1(nc, cn, A, x, dram("by_expert", [slots, D]), dram("expert_out", [slots, D]), out)


_OUTS = [((N, D), "float32")]


def kernel(**inputs):
    import numpy as _np
    import concourse.bacc as _bacc
    from concourse import mybir as _mybir
    from concourse.bass_utils import run_bass_kernel_spmd as _run

    turned = {"L0_mix_Wq": "L0_mix_WqT", "L0_mix_Wkv": "L0_mix_WkvT", "L0_mix_Wproj": "L0_mix_WprojT",
              "L1_gnn_in_proj_w": "L1_gnn_in_proj_wT", "L1_gnn_attn_out_w": "L1_gnn_attn_out_wT",
              "L1_gnn_proj_w": "L1_gnn_proj_wT"}
    nc = _bacc.Bacc("TRN2", target_bir_lowering=False, num_devices=1)
    arrays, args = {}, {}
    for name, value in inputs.items():
        a = _np.asarray(value)
        if name in turned:
            name, a = turned[name], a.T
        if a.ndim == 3:
            a = a.transpose(1, 0, 2).reshape(a.shape[1], -1) if name in ("L1_gnn_W",) else a
        if name in ("L0_ffn_b1", "L1_ffn_b1", "L1_gnn_attn_out_b"):
            a = a.reshape(-1, 128).T
        if name in ("L0_ffn_att_src", "L0_ffn_att_dst", "L0_ffn_b2", "L1_gnn_b", "L1_ffn_bd"):
            a = a.reshape(-1)
        a = _np.ascontiguousarray(a)
        arrays[f"in_{name}_dram"] = a
        args[name] = nc.dram_tensor(f"in_{name}_dram", a.shape, _mybir.dt.from_np(a.dtype), kind="ExternalInput").ap()
    out = nc.dram_tensor("out_0_dram", _OUTS[0][0], _mybir.dt.float32, kind="ExternalOutput").ap()
    gps_kernel(nc, args, out)
    r = _run(nc, [arrays], core_ids=[0])
    return r.results[0]["out_0_dram"]
```
